# Optimizing a Trainium2 kernel written in Bass

```python
import numpy as np
import jax
import jax.numpy as jnp

def _softmax(x, axis=-1):
    return jax.nn.softmax(x, axis=axis)

def _gelu(x):
    return jax.nn.gelu(x, approximate=True)

def _silu(x):
    return jax.nn.silu(x)

def _sigmoid(x):
    return jax.nn.sigmoid(x)

def _layernorm(x, axis=-1, eps=1e-05):
    m = jnp.mean(x, axis=axis, keepdims=True)
    v = jnp.var(x, axis=axis, keepdims=True)
    return (x - m) / jnp.sqrt(v + eps)

def _scatter_add(tgt, idx, src, axis=0):
    return tgt.at[idx].add(src)

def _segment_sum(src, seg, n):
    return jax.ops.segment_sum(src, seg, n)
kernel_name = 'mk_decoder_postln_d4_seqx_r8_f589de'

def setup_inputs(seed: int=0):
    np.random.seed(seed)
    _w = jnp.asarray

    def _rec_inputs():
        import jax
        import jax.numpy as jnp
        _rk = jax.random.key(seed)
        x = -0.0003929 + 0.9999 * jax.random.normal(jax.random.fold_in(_rk, 1), (4, 256, 128), jnp.float32)
        _lenS = 256 - jax.random.randint(jax.random.fold_in(_rk, 7), (4,), 0, max(1, 256 // 4) + 1, jnp.int32)
        _lenS2 = 1601 - jax.random.randint(jax.random.fold_in(_rk, 8), (4,), 0, max(1, 1601 // 4) + 1, jnp.int32)
        _ctx_1024P = jax.random.normal(jax.random.fold_in(_rk, 11), (4, 16, 128), jnp.float32)
        _ctx_1024c = jax.random.dirichlet(jax.random.fold_in(_rk, 511), 0.3 * jnp.ones((16,), jnp.float32), (4, 1601))
        _ctx_1024t = jnp.einsum('bsk,bkd->bsd', _ctx_1024c, _ctx_1024P)
        _ctx_1024t = _ctx_1024t * jax.lax.rsqrt(jnp.mean(jnp.square(_ctx_1024t)) + 1e-12) * 0.953939
        ctx_1024 = -1.39393e-06 + 0.999914 * (_ctx_1024t + 0.3 * jax.random.normal(jax.random.fold_in(_rk, 611), (4, 1601, 128), jnp.float32))
        return (x, ctx_1024)
    x, ctx_1024 = _rec_inputs()

    def _L0_attn_setup():
        import jax, jax.numpy as jnp
        import numpy as np
        from jax.scipy.linalg import solve_triangular
        B, L, D, H = (1, 256, 128, 4)
        DK = DV = D // H
        CONV = 4
        FIR_S, FIR_M, FIR_L = (3, 15, 63)
        CHUNK = 32

        def _l2norm(x):
            return x * jax.lax.rsqrt(jnp.sum(x * x, -1, keepdims=True) + 1e-06)

        def _short_conv(x, w):
            K = w.shape[-1]
            l = x.shape[1]
            xp = jnp.pad(x, ((0, 0), (K - 1, 0), (0, 0)))
            y = sum((xp[:, j:j + l, :] * w[:, j] for j in range(K)))
            return jax.nn.silu(y)

        def _fir(x, filt):
            b, l, h, d = x.shape
            K = filt.shape[-1]
            xf = jnp.transpose(x.reshape(b, l, h * d), (0, 2, 1))
            y = jax.lax.conv_general_dilated(xf, filt.reshape(h * d, 1, K), (1,), [(K - 1, 0)], feature_group_count=h * d)
            return jnp.transpose(y, (0, 2, 1)).reshape(b, l, h, d)

        def _delta_rule_chunkwise(q, k, v, beta):
            b, h, Lq, dk = q.shape
            c = CHUNK
            n = Lq // c
            q = _l2norm(q)
            k = _l2norm(k)
            v = v * beta[..., None]
            kb = k * beta[..., None]
            rs = lambda t: t.reshape(b, h, n, c, t.shape[-1])
            qc, kc, vc, kbc = (rs(q), rs(k), rs(v), rs(kb))
            tri_strict = jnp.tril(jnp.ones((c, c), bool), -1)
            A = jnp.where(tri_strict, -(kbc @ jnp.swapaxes(kc, -1, -2)), 0.0)
            eye = jnp.eye(c, dtype=q.dtype)
            M = eye - A
            T = solve_triangular(M, jnp.broadcast_to(eye, M.shape), lower=True)
            u = T @ vc
            w = T @ kbc
            causal = jnp.tril(jnp.ones((c, c), bool))

            def step(S, inp):
                q_i, k_i, u_i, w_i = inp
                attn = jnp.where(causal, q_i @ jnp.swapaxes(k_i, -1, -2), 0.0)
                u_adj = u_i - w_i @ S
                o_i = q_i @ S + attn @ u_adj
                return (S + jnp.swapaxes(k_i, -1, -2) @ u_adj, o_i)
            S0 = jnp.zeros((b, h, dk, v.shape[-1]), q.dtype)
            mv = lambda t: jnp.moveaxis(t, 2, 0)
            _, o = jax.lax.scan(step, S0, (mv(qc), mv(kc), mv(u), mv(w)))
            return jnp.moveaxis(o, 0, 2).reshape(b, h, Lq, -1)

        def _rmsnorm(x, w, eps=1e-05):
            return x * jax.lax.rsqrt(jnp.mean(x * x, -1, keepdims=True) + eps) * w
        key = jax.random.key(seed)
        ks = jax.random.split(key, 16)
        wn = lambda k, shape, s: jax.random.normal(k, shape, jnp.float32) * s

        def fir_init(k, K):
            f = jnp.zeros((H, DV, K), jnp.float32).at[..., -1].set(1.0)
            return f + wn(k, (H, DV, K), 0.01)
        return {'hidden_states': jax.random.normal(ks[0], (B, L, D), jnp.float32), 'Wq': wn(ks[1], (D, D), 0.02), 'Wk': wn(ks[2], (D, D), 0.02), 'Wv': wn(ks[3], (D, D), 0.02), 'Wb': wn(ks[4], (H, D), 0.02), 'conv_q': wn(ks[5], (D, CONV), 0.1), 'conv_k': wn(ks[6], (D, CONV), 0.1), 'conv_v': wn(ks[7], (D, CONV), 0.1), 'fir_s': fir_init(ks[8], FIR_S), 'fir_m': fir_init(ks[9], FIR_M), 'fir_l': fir_init(ks[10], FIR_L), 'gate_w': wn(ks[11], (H, 5, D), 1.0 / np.sqrt(D)), 'gate_b': jnp.zeros((H, 5), jnp.float32), 'log_temp': jnp.zeros((H, 1), jnp.float32), 'eps_param': jnp.full((H, 1), 0.02, jnp.float32), 'norm_w': jnp.ones((DV,), jnp.float32), 'Wo': wn(ks[12], (D, D), 0.02)}
    _L0_attn_all = _L0_attn_setup()
    _L0_attn_in = {k: v for k, v in _L0_attn_all.items() if k in ('Wq', 'Wk', 'Wv', 'Wb', 'conv_q', 'conv_k', 'conv_v', 'fir_s', 'fir_m', 'fir_l', 'gate_w', 'gate_b', 'log_temp', 'eps_param', 'norm_w', 'Wo')}
    del _L0_attn_all

    def _L0_xattn_setup():
        import jax, jax.numpy as jnp
        import numpy as np
        B, C_LEN, Q_LEN, D = (8, 256, 64, 128)
        key = jax.random.key(seed)
        ks = jax.random.split(key, 10)
        scale = 1.0 / np.sqrt(D)
        return {'c': jax.random.normal(ks[0], (B, C_LEN, D), dtype=jnp.float32), 'q': jax.random.normal(ks[1], (B, Q_LEN, D), dtype=jnp.float32), 'w_cq': jax.random.normal(ks[2], (D,), dtype=jnp.float32) * scale, 'b_cq': jax.random.normal(ks[3], (), dtype=jnp.float32) * scale, 'w_c': jax.random.normal(ks[4], (D,), dtype=jnp.float32) * scale, 'b_c': jax.random.normal(ks[5], (), dtype=jnp.float32) * scale, 'w_q': jax.random.normal(ks[6], (D,), dtype=jnp.float32) * scale, 'b_q': jax.random.normal(ks[7], (), dtype=jnp.float32) * scale, 'W_l': jax.random.normal(ks[8], (D, 4 * D), dtype=jnp.float32) * (1.0 / np.sqrt(4 * D)), 'b_l': jax.random.normal(ks[9], (D,), dtype=jnp.float32) * (1.0 / np.sqrt(4 * D))}
    _L0_xattn_all = _L0_xattn_setup()
    _L0_xattn_in = {k: v for k, v in _L0_xattn_all.items() if k in ('w_cq', 'b_cq', 'w_c', 'b_c', 'w_q', 'b_q', 'W_l', 'b_l')}
    del _L0_xattn_all

    def _L0_ffn_setup():
        import jax, jax.numpy as jnp
        import numpy as np
        D = 128
        E = 8
        K = 2
        DF = 512
        B, S = (2, 256)
        EPS_LN = 1e-05
        EPS_TOPK = 1e-08

        def _xavier(key, shape, fan_in, fan_out, dtype=jnp.float32):
            bound = float(np.sqrt(6.0 / (fan_in + fan_out)))
            return jax.random.uniform(key, shape, dtype, -bound, bound)
        key = jax.random.key(seed)
        kx, kg, k1, k2 = jax.random.split(key, 4)
        return {'x': jax.random.normal(kx, (B, S, D), jnp.float32), 'gamma': jnp.ones((D,), jnp.float32), 'beta': jnp.zeros((D,), jnp.float32), 'Wg': _xavier(kg, (E, D), D, E), 'bg': jnp.zeros((E,), jnp.float32), 'W1': _xavier(k1, (E, DF, D), D, DF), 'b1': jnp.zeros((E, DF), jnp.float32), 'W2': _xavier(k2, (E, D, DF), DF, D), 'b2': jnp.zeros((E, D), jnp.float32)}
    _L0_ffn_all = _L0_ffn_setup()
    _L0_ffn_in = {k: v for k, v in _L0_ffn_all.items() if k in ('gamma', 'beta', 'Wg', 'bg', 'W1', 'b1', 'W2', 'b2')}
    del _L0_ffn_all

    def _L1_attn_setup():
        import jax, jax.numpy as jnp
        import numpy as np
        NUM_HEADS = 16
        STRIDE = 32
        WINDOW = 64

        def _sparse_mask(n: int) -> jnp.ndarray:
            i = jnp.arange(n)[:, None]
            j = jnp.arange(n)[None, :]
            return (j % STRIDE == 0) | (jnp.abs(i - j) <= WINDOW)
        key = jax.random.key(seed)
        k0, k1, k2 = jax.random.split(key, 3)
        d = 128
        return {'x': jax.random.normal(k0, (1, 256, d), dtype=jnp.float32), 'w_qkv': jax.random.normal(k1, (d, 3 * d), dtype=jnp.float32) / np.sqrt(d), 'b_qkv': jnp.zeros((3 * d,), dtype=jnp.float32), 'w_out': jax.random.normal(k2, (d, d), dtype=jnp.float32) / np.sqrt(d), 'b_out': jnp.zeros((d,), dtype=jnp.float32)}
    _L1_attn_all = _L1_attn_setup()
    _L1_attn_in = {k: v for k, v in _L1_attn_all.items() if k in ('w_qkv', 'b_qkv', 'w_out', 'b_out')}
    del _L1_attn_all

    def _L1_xattn_setup():
        import jax, jax.numpy as jnp
        import numpy as np
        B, N, M = (4, 256, 256)
        DIM = 128
        HEADS = 16
        DIM_HEAD = 64
        INNER = HEADS * DIM_HEAD
        SCALE = 8.0

        def layer_norm(x, g, eps=1e-05):
            mean = jnp.mean(x, axis=-1, keepdims=True)
            var = jnp.mean((x - mean) ** 2, axis=-1, keepdims=True)
            return (x - mean) * jax.lax.rsqrt(var + eps) * g

        def l2norm(t, eps=1e-12):
            n = jnp.maximum(jnp.linalg.norm(t, axis=-1, keepdims=True), eps)
            return t / n
        key = jax.random.key(seed)
        ks = jax.random.split(key, 8)
        x = jax.random.normal(ks[0], (B, N, DIM), dtype=jnp.float32)
        context = jax.random.normal(ks[1], (B, M, DIM), dtype=jnp.float32)
        g_norm = jnp.ones((DIM,), dtype=jnp.float32)
        null_kv = jax.random.normal(ks[2], (2, DIM_HEAD), dtype=jnp.float32)
        Wq = jax.random.normal(ks[3], (DIM, INNER), dtype=jnp.float32) / np.sqrt(DIM)
        Wkv = jax.random.normal(ks[4], (DIM, 2 * INNER), dtype=jnp.float32) / np.sqrt(DIM)
        q_scale = jnp.ones((DIM_HEAD,), dtype=jnp.float32)
        k_scale = jnp.ones((DIM_HEAD,), dtype=jnp.float32)
        Wout = jax.random.normal(ks[5], (INNER, DIM), dtype=jnp.float32) / np.sqrt(INNER)
        g_out = jnp.ones((DIM,), dtype=jnp.float32)
        return {'x': x, 'context': context, 'g_norm': g_norm, 'null_kv': null_kv, 'Wq': Wq, 'Wkv': Wkv, 'q_scale': q_scale, 'k_scale': k_scale, 'Wout': Wout, 'g_out': g_out}
    _L1_xattn_all = _L1_xattn_setup()
    _L1_xattn_in = {k: v for k, v in _L1_xattn_all.items() if k in ('g_norm', 'null_kv', 'Wq', 'Wkv', 'q_scale', 'k_scale', 'Wout', 'g_out')}
    del _L1_xattn_all

    def _L1_ffn_setup():
        import jax, jax.numpy as jnp
        import numpy as np
        from jax import lax
        D_MODEL = 128
        D_FF = 512
        NUM_EXPERTS = 24
        TOP_K = 2
        key = jax.random.key(seed)
        ks = jax.random.split(key, 7)
        s1 = 1.0 / np.sqrt(D_MODEL)
        s2 = 1.0 / np.sqrt(D_FF)
        x = jax.random.normal(ks[0], (2, 128, D_MODEL), dtype=jnp.float32)
        gate_w = jax.random.uniform(ks[1], (D_MODEL, NUM_EXPERTS), jnp.float32, -s1, s1)
        gate_b = jax.random.uniform(ks[2], (NUM_EXPERTS,), jnp.float32, -s1, s1)
        w1 = jax.random.uniform(ks[3], (NUM_EXPERTS, D_MODEL, D_FF), jnp.float32, -s1, s1)
        b1 = jax.random.uniform(ks[4], (NUM_EXPERTS, D_FF), jnp.float32, -s1, s1)
        w2 = jax.random.uniform(ks[5], (NUM_EXPERTS, D_FF, D_MODEL), jnp.float32, -s2, s2)
        b2 = jax.random.uniform(ks[6], (NUM_EXPERTS, D_MODEL), jnp.float32, -s2, s2)
        return {'x': x, 'gate_w': gate_w, 'gate_b': gate_b, 'w1': w1, 'b1': b1, 'w2': w2, 'b2': b2}
    _L1_ffn_all = _L1_ffn_setup()
    _L1_ffn_in = {k: v for k, v in _L1_ffn_all.items() if k in ('gate_w', 'gate_b', 'w1', 'b1', 'w2', 'b2')}
    del _L1_ffn_all

    def _L2_attn_setup():
        import jax, jax.numpy as jnp
        import numpy as np
        N_EMBD = 128
        N_HEAD = 16
        HORIZON = 64
        HS = N_EMBD // N_HEAD
        BD = max(HS // 4, 16)

        def _windows(t, delta):
            B, nh, T, D = t.shape
            padded = jnp.pad(t, ((0, 0), (0, 0), (delta - 1, 0), (0, 0)))
            idx = jnp.arange(T)[:, None] + jnp.arange(delta)[None, :]
            return padded[:, :, idx]
        key = jax.random.key(seed)
        ks = jax.random.split(key, 12)
        s = 0.02
        B, T = (2, 128)
        return {'x': jax.random.normal(ks[0], (B, T, N_EMBD), jnp.float32), 'W_disp': jax.random.normal(ks[1], (N_EMBD, N_HEAD * BD), jnp.float32) * s, 'W_val': jax.random.normal(ks[2], (N_EMBD, N_EMBD), jnp.float32) * s, 'rel_pos_emb': jax.random.normal(ks[3], (HORIZON, BD), jnp.float32) * s, 'W_strain': jax.random.normal(ks[4], (BD, BD), jnp.float32) * s, 'W_pos': jax.random.normal(ks[5], (BD, BD), jnp.float32) * s, 'W_bond': jax.random.normal(ks[6], (BD, 1), jnp.float32) * s, 'W_dmg': jax.random.normal(ks[7], (BD, BD), jnp.float32) * s, 'b_dmg': jnp.zeros((BD,), jnp.float32), 'W_dmg_out': jax.random.normal(ks[8], (BD, 1), jnp.float32) * s, 'b_dmg_out': jnp.full((1,), -3.0, jnp.float32), 'W_cproj': jax.random.normal(ks[9], (N_EMBD, N_EMBD), jnp.float32) * s}
    _L2_attn_all = _L2_attn_setup()
    _L2_attn_in = {k: v for k, v in _L2_attn_all.items() if k in ('W_disp', 'W_val', 'rel_pos_emb', 'W_strain', 'W_pos', 'W_bond', 'W_dmg', 'b_dmg', 'W_dmg_out', 'b_dmg_out', 'W_cproj')}
    del _L2_attn_all

    def _L2_xattn_setup():
        import jax, jax.numpy as jnp
        import numpy as np
        B, T, S, D = (4, 256, 512, 128)
        TOP_K = 32

        def _read(query, mem_state, top_k, Wq, bq, Wk, bk, Wv, bv, Wo, bo):
            b, t, d = query.shape
            s = mem_state.shape[1]
            scale = 1.0 / np.sqrt(d)
            q = query @ Wq.T + bq
            k = mem_state @ Wk.T + bk
            v = mem_state @ Wv.T + bv
            scores = jnp.einsum('btd,bsd->bts', q, k) * scale
            if top_k < s:
                vals, idx = jax.lax.top_k(scores, top_k)
                b_ix = jnp.arange(b)[:, None, None]
                t_ix = jnp.arange(t)[None, :, None]
                masked = jnp.full_like(scores, -jnp.inf)
                scores = masked.at[b_ix, t_ix, idx].set(vals)
            attn = jax.nn.softmax(scores, axis=-1)
            ctx = jnp.einsum('bts,bsd->btd', attn, v)
            return ctx @ Wo.T + bo
        key = jax.random.key(seed)
        ks = jax.random.split(key, 12)
        std = 0.02
        inp = {'query': jax.random.normal(ks[0], (B, T, D), dtype=jnp.float32), 'mem_state': jax.random.normal(ks[1], (B, S, D), dtype=jnp.float32), 'top_k': TOP_K, 'Wq': jax.random.normal(ks[2], (D, D), dtype=jnp.float32) * std, 'bq': jnp.zeros((D,), dtype=jnp.float32), 'Wk': jax.random.normal(ks[3], (D, D), dtype=jnp.float32) * std, 'bk': jnp.zeros((D,), dtype=jnp.float32), 'Wv': jax.random.normal(ks[4], (D, D), dtype=jnp.float32) * std, 'bv': jnp.zeros((D,), dtype=jnp.float32), 'Wo': jax.random.normal(ks[5], (D, D), dtype=jnp.float32) * std, 'bo': jnp.zeros((D,), dtype=jnp.float32)}
        return inp
    _L2_xattn_all = _L2_xattn_setup()
    _L2_xattn_in = {k: v for k, v in _L2_xattn_all.items() if k in ('Wq', 'bq', 'Wk', 'bk', 'Wv', 'bv', 'Wo', 'bo')}
    del _L2_xattn_all

    def _L2_ffn_setup():
        import jax, jax.numpy as jnp
        import numpy as np
        DIM = 128
        DEPTH = 6
        HEADS = 16
        DIM_HEAD = 64
        WINDOW = 32
        INNER = HEADS * DIM_HEAD
        DIM_INNER = int(DIM * 4 * 2 / 3)
        QK_SCALE = 8.0

        def shift_tokens(t):
            a, s = jnp.split(t, 2, -1)
            s = jnp.pad(s, ((0, 0), (1, 0), (0, 0)))[:, :-1]
            return jnp.concatenate([a, s], -1)

        def l2norm(t):
            return t / jnp.maximum(jnp.linalg.norm(t, axis=-1, keepdims=True), 1e-12)

        def rotate_half(x):
            x1, x2 = jnp.split(x, 2, -1)
            return jnp.concatenate([-x2, x1], -1)

        def rotary_tables(n):
            half = jnp.arange(0, DIM_HEAD, 2, dtype=jnp.float32)
            inv_freq = 1.0 / 10000.0 ** (half / DIM_HEAD)
            t = jnp.arange(n, dtype=jnp.float32)
            freqs = t[:, None] * inv_freq[None, :]
            freqs = jnp.concatenate([freqs, freqs], -1)
            base_scale = (half + 0.4 * DIM_HEAD) / (1.4 * DIM_HEAD)
            power = (t - n // 2) / (WINDOW // 2)
            scale = base_scale[None, :] ** power[:, None]
            scale = jnp.concatenate([scale, scale], -1)
            return (freqs, scale)

        def local_attention(q, k, v):
            b, h, n, d = q.shape
            w = WINDOW
            nw = n // w
            bq = q.reshape(b, h, nw, w, d)
            bk = k.reshape(b, h, nw, w, d)
            bv = v.reshape(b, h, nw, w, d)

            def look(t):
                p = jnp.pad(t, ((0, 0), (0, 0), (1, 0), (0, 0), (0, 0)))
                return jnp.concatenate([p[:, :, :nw], p[:, :, 1:]], axis=3)
            bk2, bv2 = (look(bk), look(bv))
            seq = jnp.arange(n).reshape(nw, w)
            seq_p = jnp.pad(seq, ((1, 0), (0, 0)), constant_values=-1)
            jt = jnp.concatenate([seq_p[:nw], seq_p[1:]], axis=1)
            it = seq[:, :, None]
            jb = jt[:, None, :]
            mask = (it < jb) | (it > jb + w) | (jb == -1)
            sim = jnp.einsum('bhwie,bhwje->bhwij', bq, bk2) * QK_SCALE
            sim = jnp.where(mask, -jnp.finfo(sim.dtype).max, sim)
            attn = jax.nn.softmax(sim, -1)
            out = jnp.einsum('bhwij,bhwje->bhwie', attn, bv2)
            return out.reshape(b, h, n, d)

        def attn_layer(x, Wqkv, qs, ksc, Wo):
            b, n, _ = x.shape
            qkv = x @ Wqkv
            q, k, v = jnp.split(qkv, 3, -1)
            sh = lambda t: t.reshape(b, n, HEADS, DIM_HEAD).transpose(0, 2, 1, 3)
            q, k, v = (sh(q), sh(k), sh(v))
            q = l2norm(q) * qs
            k = l2norm(k) * ksc
            freqs, scale = rotary_tables(n)
            cos, sin = (jnp.cos(freqs), jnp.sin(freqs))
            q = q * cos * scale + rotate_half(q) * sin * scale
            inv = 1.0 / scale
            k = k * cos * inv + rotate_half(k) * sin * inv
            out = local_attention(q, k, v)
            out = out.transpose(0, 2, 1, 3).reshape(b, n, INNER)
            return out @ Wo

        def ffn_layer(x, g, bln, W1, b1, W2, b2):
            mu = x.mean(-1, keepdims=True)
            var = ((x - mu) ** 2).mean(-1, keepdims=True)
            xn = (x - mu) / jnp.sqrt(var + 1e-05) * g + bln
            hg = xn @ W1 + b1
            a, gate = jnp.split(hg, 2, -1)
            return a * jax.nn.gelu(gate, approximate=False) @ W2 + b2
        key = jax.random.key(seed)
        ks = jax.random.split(key, 8)
        B, N = (2, 256)
        init = lambda k, shape: jax.random.normal(k, shape, jnp.float32) * 0.02
        return {'x': jax.random.normal(ks[0], (B, N, DIM), jnp.float32), 'Wqkv': init(ks[1], (DEPTH, DIM, 3 * INNER)), 'q_scale': jnp.ones((DEPTH, DIM_HEAD), jnp.float32), 'k_scale': jnp.ones((DEPTH, DIM_HEAD), jnp.float32), 'Wo': init(ks[2], (DEPTH, INNER, DIM)), 'ln_g': jnp.ones((DEPTH, DIM), jnp.float32), 'ln_b': jnp.zeros((DEPTH, DIM), jnp.float32), 'W1': init(ks[3], (DEPTH, DIM, 2 * DIM_INNER)), 'b1': jnp.zeros((DEPTH, 2 * DIM_INNER), jnp.float32), 'W2': init(ks[4], (DEPTH, DIM_INNER, DIM)), 'b2': jnp.zeros((DEPTH, DIM), jnp.float32)}
    _L2_ffn_all = _L2_ffn_setup()
    _L2_ffn_in = {k: v for k, v in _L2_ffn_all.items() if k in ('Wqkv', 'q_scale', 'k_scale', 'Wo', 'ln_g', 'ln_b', 'W1', 'b1', 'W2', 'b2')}
    del _L2_ffn_all

    def _L3_attn_setup():
        import jax, jax.numpy as jnp
        import numpy as np
        B, T, D, NH = (4, 256, 128, 16)
        HD = D // NH

        def _rwkv7_forward(x, Wr, Wk, Wv, Ww, Wo):
            b, t, d = x.shape
            nh, hd = (NH, d // NH)
            r = jax.nn.sigmoid(x @ Wr.T).reshape(b, t, nh, hd)
            k = (x @ Wk.T).reshape(b, t, nh, hd)
            v = (x @ Wv.T).reshape(b, t, nh, hd)
            w = (jax.nn.sigmoid(x @ Ww.T) * 0.99).reshape(b, t, nh, hd)

            def step(state, inp):
                w_t, k_t, v_t, r_t = inp
                state = state * w_t[..., :, None] + v_t[..., :, None] * k_t[..., None, :]
                out_t = r_t * state.sum(-1)
                return (state, out_t)
            seq = (jnp.moveaxis(w, 1, 0), jnp.moveaxis(k, 1, 0), jnp.moveaxis(v, 1, 0), jnp.moveaxis(r, 1, 0))
            state0 = jnp.zeros((b, nh, hd, hd), dtype=x.dtype)
            _, outs = jax.lax.scan(step, state0, seq)
            out = jnp.moveaxis(outs, 0, 1).reshape(b, t, d)
            eps = jnp.asarray(jnp.finfo(out.dtype).eps, out.dtype)
            out = out * jax.lax.rsqrt(jnp.mean(out * out, axis=-1, keepdims=True) + eps)
            return out @ Wo.T
        key = jax.random.key(seed)
        ks = jax.random.split(key, 6)
        scale = 0.02
        x = jax.random.normal(ks[0], (B, T, D), dtype=jnp.float32)
        Wr = jax.random.normal(ks[1], (D, D), dtype=jnp.float32) * scale
        Wk = jax.random.normal(ks[2], (D, D), dtype=jnp.float32) * scale
        Wv = jax.random.normal(ks[3], (D, D), dtype=jnp.float32) * scale
        Ww = jax.random.normal(ks[4], (D, D), dtype=jnp.float32) * scale
        Wo = jax.random.normal(ks[5], (D, D), dtype=jnp.float32) * scale
        return {'x': x, 'Wr': Wr, 'Wk': Wk, 'Wv': Wv, 'Ww': Ww, 'Wo': Wo}
    _L3_attn_all = _L3_attn_setup()
    _L3_attn_in = {k: v for k, v in _L3_attn_all.items() if k in ('Wr', 'Wk', 'Wv', 'Ww', 'Wo')}
    del _L3_attn_all

    def _L3_xattn_setup():
        import jax, jax.numpy as jnp
        import numpy as np
        B, SD, SE, D, H = (4, 256, 256, 128, 16)
        HD = D // H

        def _mha(xq, xk, xv, Wq, bq, Wk, bk, Wv, bv, Wo, bo, causal):
            q = jnp.einsum('bsd,hde->bhse', xq, Wq) + bq[None, :, None, :]
            k = jnp.einsum('bsd,hde->bhse', xk, Wk) + bk[None, :, None, :]
            v = jnp.einsum('bsd,hde->bhse', xv, Wv) + bv[None, :, None, :]
            scale = 1.0 / jnp.sqrt(jnp.asarray(HD, q.dtype))
            scores = jnp.einsum('bhqe,bhke->bhqk', q, k) * scale
            if causal:
                mask = jnp.tril(jnp.ones((q.shape[2], k.shape[2]), bool))
                scores = jnp.where(mask, scores, jnp.finfo(scores.dtype).min)
            w = jax.nn.softmax(scores, axis=-1)
            out = jnp.einsum('bhqk,bhke->bhqe', w, v)
            out = out.transpose(0, 2, 1, 3).reshape(out.shape[0], out.shape[2], D)
            return out @ Wo + bo
        key = jax.random.key(seed)
        ks = jax.random.split(key, 19)
        sd = 1.0 / np.sqrt(D)
        n = lambda k, shape, s: jax.random.normal(k, shape, jnp.float32) * s
        inp = {'x': n(ks[0], (B, SD, D), 1.0), 'encoder_k': n(ks[1], (B, SE, D), 1.0), 'encoder_v': n(ks[2], (B, SE, D), 1.0), 'Wq1': n(ks[3], (H, D, HD), sd), 'bq1': jnp.zeros((H, HD), jnp.float32), 'Wk1': n(ks[4], (H, D, HD), sd), 'bk1': jnp.zeros((H, HD), jnp.float32), 'Wv1': n(ks[5], (H, D, HD), sd), 'bv1': jnp.zeros((H, HD), jnp.float32), 'Wo1': n(ks[6], (D, D), sd), 'bo1': jnp.zeros((D,), jnp.float32), 'Wq2': n(ks[7], (H, D, HD), sd), 'bq2': jnp.zeros((H, HD), jnp.float32), 'Wk2': n(ks[8], (H, D, HD), sd), 'bk2': jnp.zeros((H, HD), jnp.float32), 'Wv2': n(ks[9], (H, D, HD), sd), 'bv2': jnp.zeros((H, HD), jnp.float32), 'Wo2': n(ks[10], (D, D), sd), 'bo2': jnp.zeros((D,), jnp.float32)}
        return inp
    _L3_xattn_all = _L3_xattn_setup()
    _L3_xattn_in = {k: v for k, v in _L3_xattn_all.items() if k in ('Wq1', 'bq1', 'Wk1', 'bk1', 'Wv1', 'bv1', 'Wo1', 'bo1', 'Wq2', 'bq2', 'Wk2', 'bk2', 'Wv2', 'bv2', 'Wo2', 'bo2')}
    del _L3_xattn_all

    def _L3_ffn_setup():
        import jax, jax.numpy as jnp
        import numpy as np
        EPS = 1e-08

        def _ternary_linear(x, w):
            alpha = jnp.mean(jnp.abs(w))
            w_t = jnp.sign(w) * (jnp.abs(w) > 0.5 * alpha).astype(w.dtype)
            w_q = w + jax.lax.stop_gradient(w_t - w)
            d = x.shape[-1]
            rms = jnp.sqrt(jnp.sum(x * x, axis=-1, keepdims=True)) / jnp.sqrt(jnp.asarray(d, x.dtype))
            x_norm = x / (rms + EPS)
            return jnp.einsum('bsd,fd->bsf', x_norm, w_q)
        key = jax.random.key(seed)
        k1, k2, k3 = jax.random.split(key, 3)
        d_model, d_ff = (128, 512)
        B, S = (4, 512)
        x = jax.random.normal(k1, (B, S, d_model), dtype=jnp.float32)
        w_up = jax.random.normal(k2, (d_ff, d_model), dtype=jnp.float32) * 0.02
        w_down = jax.random.normal(k3, (d_model, d_ff), dtype=jnp.float32) * 0.02
        return {'x': x, 'w_up': w_up, 'w_down': w_down}
    _L3_ffn_all = _L3_ffn_setup()
    _L3_ffn_in = {k: v for k, v in _L3_ffn_all.items() if k in ('w_up', 'w_down')}
    del _L3_ffn_all
    return {'x': x, 'ctx_1024': ctx_1024, 'L0_attn_Wq': _L0_attn_in['Wq'], 'L0_attn_Wk': _L0_attn_in['Wk'], 'L0_attn_Wv': _L0_attn_in['Wv'], 'L0_attn_Wb': _L0_attn_in['Wb'], 'L0_attn_conv_q': _L0_attn_in['conv_q'], 'L0_attn_conv_k': _L0_attn_in['conv_k'], 'L0_attn_conv_v': _L0_attn_in['conv_v'], 'L0_attn_fir_s': _L0_attn_in['fir_s'], 'L0_attn_fir_m': _L0_attn_in['fir_m'], 'L0_attn_fir_l': _L0_attn_in['fir_l'], 'L0_attn_gate_w': _L0_attn_in['gate_w'], 'L0_attn_gate_b': _L0_attn_in['gate_b'], 'L0_attn_log_temp': _L0_attn_in['log_temp'], 'L0_attn_eps_param': _L0_attn_in['eps_param'], 'L0_attn_norm_w': _L0_attn_in['norm_w'], 'L0_attn_Wo': _L0_attn_in['Wo'], 'L0_xattn_w_cq': _L0_xattn_in['w_cq'], 'L0_xattn_b_cq': _L0_xattn_in['b_cq'], 'L0_xattn_w_c': _L0_xattn_in['w_c'], 'L0_xattn_b_c': _L0_xattn_in['b_c'], 'L0_xattn_w_q': _L0_xattn_in['w_q'], 'L0_xattn_b_q': _L0_xattn_in['b_q'], 'L0_xattn_W_l': _L0_xattn_in['W_l'], 'L0_xattn_b_l': _L0_xattn_in['b_l'], 'L0_ffn_gamma': _L0_ffn_in['gamma'], 'L0_ffn_beta': _L0_ffn_in['beta'], 'L0_ffn_Wg': _L0_ffn_in['Wg'], 'L0_ffn_bg': _L0_ffn_in['bg'], 'L0_ffn_W1': _L0_ffn_in['W1'], 'L0_ffn_b1': _L0_ffn_in['b1'], 'L0_ffn_W2': _L0_ffn_in['W2'], 'L0_ffn_b2': _L0_ffn_in['b2'], 'L1_attn_w_qkv': _L1_attn_in['w_qkv'], 'L1_attn_b_qkv': _L1_attn_in['b_qkv'], 'L1_attn_w_out': _L1_attn_in['w_out'], 'L1_attn_b_out': _L1_attn_in['b_out'], 'L1_xattn_g_norm': _L1_xattn_in['g_norm'], 'L1_xattn_null_kv': _L1_xattn_in['null_kv'], 'L1_xattn_Wq': _L1_xattn_in['Wq'], 'L1_xattn_Wkv': _L1_xattn_in['Wkv'], 'L1_xattn_q_scale': _L1_xattn_in['q_scale'], 'L1_xattn_k_scale': _L1_xattn_in['k_scale'], 'L1_xattn_Wout': _L1_xattn_in['Wout'], 'L1_xattn_g_out': _L1_xattn_in['g_out'], 'L1_ffn_gate_w': _L1_ffn_in['gate_w'], 'L1_ffn_gate_b': _L1_ffn_in['gate_b'], 'L1_ffn_w1': _L1_ffn_in['w1'], 'L1_ffn_b1': _L1_ffn_in['b1'], 'L1_ffn_w2': _L1_ffn_in['w2'], 'L1_ffn_b2': _L1_ffn_in['b2'], 'L2_attn_W_disp': _L2_attn_in['W_disp'], 'L2_attn_W_val': _L2_attn_in['W_val'], 'L2_attn_rel_pos_emb': _L2_attn_in['rel_pos_emb'], 'L2_attn_W_strain': _L2_attn_in['W_strain'], 'L2_attn_W_pos': _L2_attn_in['W_pos'], 'L2_attn_W_bond': _L2_attn_in['W_bond'], 'L2_attn_W_dmg': _L2_attn_in['W_dmg'], 'L2_attn_b_dmg': _L2_attn_in['b_dmg'], 'L2_attn_W_dmg_out': _L2_attn_in['W_dmg_out'], 'L2_attn_b_dmg_out': _L2_attn_in['b_dmg_out'], 'L2_attn_W_cproj': _L2_attn_in['W_cproj'], 'L2_xattn_Wq': _L2_xattn_in['Wq'], 'L2_xattn_bq': _L2_xattn_in['bq'], 'L2_xattn_Wk': _L2_xattn_in['Wk'], 'L2_xattn_bk': _L2_xattn_in['bk'], 'L2_xattn_Wv': _L2_xattn_in['Wv'], 'L2_xattn_bv': _L2_xattn_in['bv'], 'L2_xattn_Wo': _L2_xattn_in['Wo'], 'L2_xattn_bo': _L2_xattn_in['bo'], 'L2_ffn_Wqkv': _L2_ffn_in['Wqkv'], 'L2_ffn_q_scale': _L2_ffn_in['q_scale'], 'L2_ffn_k_scale': _L2_ffn_in['k_scale'], 'L2_ffn_Wo': _L2_ffn_in['Wo'], 'L2_ffn_ln_g': _L2_ffn_in['ln_g'], 'L2_ffn_ln_b': _L2_ffn_in['ln_b'], 'L2_ffn_W1': _L2_ffn_in['W1'], 'L2_ffn_b1': _L2_ffn_in['b1'], 'L2_ffn_W2': _L2_ffn_in['W2'], 'L2_ffn_b2': _L2_ffn_in['b2'], 'L3_attn_Wr': _L3_attn_in['Wr'], 'L3_attn_Wk': _L3_attn_in['Wk'], 'L3_attn_Wv': _L3_attn_in['Wv'], 'L3_attn_Ww': _L3_attn_in['Ww'], 'L3_attn_Wo': _L3_attn_in['Wo'], 'L3_xattn_Wq1': _L3_xattn_in['Wq1'], 'L3_xattn_bq1': _L3_xattn_in['bq1'], 'L3_xattn_Wk1': _L3_xattn_in['Wk1'], 'L3_xattn_bk1': _L3_xattn_in['bk1'], 'L3_xattn_Wv1': _L3_xattn_in['Wv1'], 'L3_xattn_bv1': _L3_xattn_in['bv1'], 'L3_xattn_Wo1': _L3_xattn_in['Wo1'], 'L3_xattn_bo1': _L3_xattn_in['bo1'], 'L3_xattn_Wq2': _L3_xattn_in['Wq2'], 'L3_xattn_bq2': _L3_xattn_in['bq2'], 'L3_xattn_Wk2': _L3_xattn_in['Wk2'], 'L3_xattn_bk2': _L3_xattn_in['bk2'], 'L3_xattn_Wv2': _L3_xattn_in['Wv2'], 'L3_xattn_bv2': _L3_xattn_in['bv2'], 'L3_xattn_Wo2': _L3_xattn_in['Wo2'], 'L3_xattn_bo2': _L3_xattn_in['bo2'], 'L3_ffn_w_up': _L3_ffn_in['w_up'], 'L3_ffn_w_down': _L3_ffn_in['w_down']}

def reference(x, ctx_1024, L0_attn_Wq, L0_attn_Wk, L0_attn_Wv, L0_attn_Wb, L0_attn_conv_q, L0_attn_conv_k, L0_attn_conv_v, L0_attn_fir_s, L0_attn_fir_m, L0_attn_fir_l, L0_attn_gate_w, L0_attn_gate_b, L0_attn_log_temp, L0_attn_eps_param, L0_attn_norm_w, L0_attn_Wo, L0_xattn_w_cq, L0_xattn_b_cq, L0_xattn_w_c, L0_xattn_b_c, L0_xattn_w_q, L0_xattn_b_q, L0_xattn_W_l, L0_xattn_b_l, L0_ffn_gamma, L0_ffn_beta, L0_ffn_Wg, L0_ffn_bg, L0_ffn_W1, L0_ffn_b1, L0_ffn_W2, L0_ffn_b2, L1_attn_w_qkv, L1_attn_b_qkv, L1_attn_w_out, L1_attn_b_out, L1_xattn_g_norm, L1_xattn_null_kv, L1_xattn_Wq, L1_xattn_Wkv, L1_xattn_q_scale, L1_xattn_k_scale, L1_xattn_Wout, L1_xattn_g_out, L1_ffn_gate_w, L1_ffn_gate_b, L1_ffn_w1, L1_ffn_b1, L1_ffn_w2, L1_ffn_b2, L2_attn_W_disp, L2_attn_W_val, L2_attn_rel_pos_emb, L2_attn_W_strain, L2_attn_W_pos, L2_attn_W_bond, L2_attn_W_dmg, L2_attn_b_dmg, L2_attn_W_dmg_out, L2_attn_b_dmg_out, L2_attn_W_cproj, L2_xattn_Wq, L2_xattn_bq, L2_xattn_Wk, L2_xattn_bk, L2_xattn_Wv, L2_xattn_bv, L2_xattn_Wo, L2_xattn_bo, L2_ffn_Wqkv, L2_ffn_q_scale, L2_ffn_k_scale, L2_ffn_Wo, L2_ffn_ln_g, L2_ffn_ln_b, L2_ffn_W1, L2_ffn_b1, L2_ffn_W2, L2_ffn_b2, L3_attn_Wr, L3_attn_Wk, L3_attn_Wv, L3_attn_Ww, L3_attn_Wo, L3_xattn_Wq1, L3_xattn_bq1, L3_xattn_Wk1, L3_xattn_bk1, L3_xattn_Wv1, L3_xattn_bv1, L3_xattn_Wo1, L3_xattn_bo1, L3_xattn_Wq2, L3_xattn_bq2, L3_xattn_Wk2, L3_xattn_bk2, L3_xattn_Wv2, L3_xattn_bv2, L3_xattn_Wo2, L3_xattn_bo2, L3_ffn_w_up, L3_ffn_w_down):
    import jax
    import jax.numpy as jnp

    def _L0_attn_ref(hidden_states, Wq, Wk, Wv, Wb, conv_q, conv_k, conv_v, fir_s, fir_m, fir_l, gate_w, gate_b, log_temp, eps_param, norm_w, Wo):
        import jax, jax.numpy as jnp
        import numpy as np
        from jax.scipy.linalg import solve_triangular
        B, L, D, H = (1, 256, 128, 4)
        DK = DV = D // H
        CONV = 4
        FIR_S, FIR_M, FIR_L = (3, 15, 63)
        CHUNK = 32

        def _l2norm(x):
            return x * jax.lax.rsqrt(jnp.sum(x * x, -1, keepdims=True) + 1e-06)

        def _short_conv(x, w):
            K = w.shape[-1]
            l = x.shape[1]
            xp = jnp.pad(x, ((0, 0), (K - 1, 0), (0, 0)))
            y = sum((xp[:, j:j + l, :] * w[:, j] for j in range(K)))
            return jax.nn.silu(y)

        def _fir(x, filt):
            b, l, h, d = x.shape
            K = filt.shape[-1]
            xf = jnp.transpose(x.reshape(b, l, h * d), (0, 2, 1))
            y = jax.lax.conv_general_dilated(xf, filt.reshape(h * d, 1, K), (1,), [(K - 1, 0)], feature_group_count=h * d)
            return jnp.transpose(y, (0, 2, 1)).reshape(b, l, h, d)

        def _delta_rule_chunkwise(q, k, v, beta):
            b, h, Lq, dk = q.shape
            c = CHUNK
            n = Lq // c
            q = _l2norm(q)
            k = _l2norm(k)
            v = v * beta[..., None]
            kb = k * beta[..., None]
            rs = lambda t: t.reshape(b, h, n, c, t.shape[-1])
            qc, kc, vc, kbc = (rs(q), rs(k), rs(v), rs(kb))
            tri_strict = jnp.tril(jnp.ones((c, c), bool), -1)
            A = jnp.where(tri_strict, -(kbc @ jnp.swapaxes(kc, -1, -2)), 0.0)
            eye = jnp.eye(c, dtype=q.dtype)
            M = eye - A
            T = solve_triangular(M, jnp.broadcast_to(eye, M.shape), lower=True)
            u = T @ vc
            w = T @ kbc
            causal = jnp.tril(jnp.ones((c, c), bool))

            def step(S, inp):
                q_i, k_i, u_i, w_i = inp
                attn = jnp.where(causal, q_i @ jnp.swapaxes(k_i, -1, -2), 0.0)
                u_adj = u_i - w_i @ S
                o_i = q_i @ S + attn @ u_adj
                return (S + jnp.swapaxes(k_i, -1, -2) @ u_adj, o_i)
            S0 = jnp.zeros((b, h, dk, v.shape[-1]), q.dtype)
            mv = lambda t: jnp.moveaxis(t, 2, 0)
            _, o = jax.lax.scan(step, S0, (mv(qc), mv(kc), mv(u), mv(w)))
            return jnp.moveaxis(o, 0, 2).reshape(b, h, Lq, -1)

        def _rmsnorm(x, w, eps=1e-05):
            return x * jax.lax.rsqrt(jnp.mean(x * x, -1, keepdims=True) + eps) * w
        b, l, d = hidden_states.shape
        q = _short_conv(hidden_states @ Wq.T, conv_q).reshape(b, l, H, DK)
        k = _short_conv(hidden_states @ Wk.T, conv_k).reshape(b, l, H, DK)
        v_direct = _short_conv(hidden_states @ Wv.T, conv_v).reshape(b, l, H, DV)
        beta = jax.nn.sigmoid(hidden_states @ Wb.T)
        tp = lambda t: jnp.transpose(t, (0, 2, 1, 3))
        delta_out = tp(_delta_rule_chunkwise(tp(q), tp(k), tp(v_direct), jnp.transpose(beta, (0, 2, 1))))
        local_s = _fir(v_direct, fir_s)
        local_m = _fir(v_direct, fir_m)
        local_l = _fir(v_direct, fir_l)
        logits = jnp.einsum('bld,hpd->blhp', hidden_states, gate_w) + gate_b
        temp = jnp.exp(log_temp).reshape(1, 1, H, 1)
        probs = jax.nn.softmax(logits / temp, -1)
        eps = jnp.clip(eps_param, 0.0, 0.2).reshape(1, 1, H, 1)
        probs = probs * (1.0 - 5.0 * eps) + eps
        o = probs[..., 0:1] * local_s + probs[..., 1:2] * local_m + probs[..., 2:3] * local_l + probs[..., 3:4] * delta_out + probs[..., 4:5] * v_direct
        o = _rmsnorm(o, norm_w)
        return o.reshape(b, l, H * DV) @ Wo.T

    def _L0_xattn_ref(c, q, w_cq, b_cq, w_c, b_c, w_q, b_q, W_l, b_l):
        import jax, jax.numpy as jnp
        import numpy as np
        B, C_LEN, Q_LEN, D = (8, 256, 64, 128)
        cq = jnp.einsum('bcd,bqd,d->bcq', c, q, w_cq) + b_cq
        s = (c @ w_c + b_c)[:, :, None] + (q @ w_q + b_q)[:, None, :] + cq
        a = jax.nn.softmax(s, axis=2)
        c2q_att = jnp.einsum('bcq,bqd->bcd', a, q)
        b_att = jax.nn.softmax(jnp.max(s, axis=2), axis=1)
        q2c_att = jnp.einsum('bc,bcd->bd', b_att, c)[:, None, :]
        x = jnp.concatenate([c, c2q_att, c * c2q_att, c * q2c_att], axis=-1)
        z = x @ W_l.T + b_l
        return z

    def _L0_ffn_ref(x, gamma, beta, Wg, bg, W1, b1, W2, b2):
        import jax, jax.numpy as jnp
        import numpy as np
        D = 128
        E = 8
        K = 2
        DF = 512
        B, S = (2, 256)
        EPS_LN = 1e-05
        EPS_TOPK = 1e-08

        def _xavier(key, shape, fan_in, fan_out, dtype=jnp.float32):
            bound = float(np.sqrt(6.0 / (fan_in + fan_out)))
            return jax.random.uniform(key, shape, dtype, -bound, bound)
        b, s, d = x.shape
        mu = jnp.mean(x, axis=-1, keepdims=True)
        var = jnp.mean((x - mu) ** 2, axis=-1, keepdims=True)
        xn = (x - mu) / jnp.sqrt(var + EPS_LN) * gamma + beta
        xf = xn.reshape(-1, d)
        logits = xf @ Wg.T + bg
        probs = jax.nn.softmax(logits, axis=-1)
        tp, ti = jax.lax.top_k(probs, K)
        tp = tp / (jnp.sum(tp, axis=-1, keepdims=True) + EPS_TOPK)
        w = jnp.sum(jax.nn.one_hot(ti, E, dtype=xf.dtype) * tp[..., None], axis=1)
        h = jax.nn.gelu(jnp.einsum('td,efd->tef', xf, W1) + b1, approximate=False)
        y = jnp.einsum('tef,edf->ted', h, W2) + b2
        out = jnp.einsum('ted,te->td', y, w)
        return x + out.reshape(b, s, d)

    def _L1_attn_ref(x, w_qkv, b_qkv, w_out, b_out):
        import jax, jax.numpy as jnp
        import numpy as np
        NUM_HEADS = 16
        STRIDE = 32
        WINDOW = 64

        def _sparse_mask(n: int) -> jnp.ndarray:
            i = jnp.arange(n)[:, None]
            j = jnp.arange(n)[None, :]
            return (j % STRIDE == 0) | (jnp.abs(i - j) <= WINDOW)
        b, n, d = x.shape
        h = NUM_HEADS
        dh = d // h
        scale = dh ** (-0.5)
        qkv = x @ w_qkv + b_qkv
        q, k, v = jnp.split(qkv, 3, axis=-1)
        q = q.reshape(b, n, h, dh).transpose(0, 2, 1, 3)
        k = k.reshape(b, n, h, dh).transpose(0, 2, 1, 3)
        v = v.reshape(b, n, h, dh).transpose(0, 2, 1, 3)
        scores = jnp.einsum('bhid,bhjd->bhij', q, k) * scale
        mask = _sparse_mask(n)
        scores = jnp.where(mask, scores, -jnp.inf)
        attn = jax.nn.softmax(scores, axis=-1)
        out = jnp.einsum('bhij,bhjd->bhid', attn, v)
        out = out.transpose(0, 2, 1, 3).reshape(b, n, d)
        return out @ w_out + b_out

    def _L1_xattn_ref(x, context, g_norm, null_kv, Wq, Wkv, q_scale, k_scale, Wout, g_out):
        import jax, jax.numpy as jnp
        import numpy as np
        B, N, M = (4, 256, 256)
        DIM = 128
        HEADS = 16
        DIM_HEAD = 64
        INNER = HEADS * DIM_HEAD
        SCALE = 8.0

        def layer_norm(x, g, eps=1e-05):
            mean = jnp.mean(x, axis=-1, keepdims=True)
            var = jnp.mean((x - mean) ** 2, axis=-1, keepdims=True)
            return (x - mean) * jax.lax.rsqrt(var + eps) * g

        def l2norm(t, eps=1e-12):
            n = jnp.maximum(jnp.linalg.norm(t, axis=-1, keepdims=True), eps)
            return t / n
        b = x.shape[0]
        xn = layer_norm(x, g_norm)
        ctx = context
        q = xn @ Wq
        kv = ctx @ Wkv
        k, v = jnp.split(kv, 2, axis=-1)
        split_heads = lambda t: t.reshape(b, t.shape[1], HEADS, DIM_HEAD).transpose(0, 2, 1, 3)
        q, k, v = map(split_heads, (q, k, v))
        nk = jnp.broadcast_to(null_kv[0], (b, HEADS, 1, DIM_HEAD))
        nv = jnp.broadcast_to(null_kv[1], (b, HEADS, 1, DIM_HEAD))
        k = jnp.concatenate([nk, k], axis=2)
        v = jnp.concatenate([nv, v], axis=2)
        q = l2norm(q) * q_scale
        k = l2norm(k) * k_scale
        sim = jnp.einsum('bhid,bhjd->bhij', q, k) * SCALE
        attn = jax.nn.softmax(sim.astype(jnp.float32), axis=-1).astype(sim.dtype)
        out = jnp.einsum('bhij,bhjd->bhid', attn, v)
        out = out.transpose(0, 2, 1, 3).reshape(b, -1, INNER)
        out = out @ Wout
        return layer_norm(out, g_out)

    def _L1_ffn_ref(x, gate_w, gate_b, w1, b1, w2, b2):
        import jax, jax.numpy as jnp
        import numpy as np
        from jax import lax
        D_MODEL = 128
        D_FF = 512
        NUM_EXPERTS = 24
        TOP_K = 2
        gate_scores = jnp.einsum('bsd,de->bse', x, gate_w) + gate_b
        topk_val, topk_idx = lax.top_k(gate_scores, TOP_K)
        sparse_gates = jax.nn.softmax(topk_val, axis=-1)
        combine = jnp.sum(jax.nn.one_hot(topk_idx, NUM_EXPERTS, dtype=x.dtype) * sparse_gates[..., None], axis=-2)
        h = jax.nn.gelu(jnp.einsum('bsd,edf->besf', x, w1) + b1[None, :, None, :], approximate=False)
        y = jnp.einsum('besf,efd->besd', h, w2) + b2[None, :, None, :]
        out = jnp.einsum('bse,besd->bsd', combine, y)
        return out + x

    def _L2_attn_ref(x, W_disp, W_val, rel_pos_emb, W_strain, W_pos, W_bond, W_dmg, b_dmg, W_dmg_out, b_dmg_out, W_cproj):
        import jax, jax.numpy as jnp
        import numpy as np
        N_EMBD = 128
        N_HEAD = 16
        HORIZON = 64
        HS = N_EMBD // N_HEAD
        BD = max(HS // 4, 16)

        def _windows(t, delta):
            B, nh, T, D = t.shape
            padded = jnp.pad(t, ((0, 0), (0, 0), (delta - 1, 0), (0, 0)))
            idx = jnp.arange(T)[:, None] + jnp.arange(delta)[None, :]
            return padded[:, :, idx]
        B, T, C = x.shape
        nh, bd, hs = (N_HEAD, BD, HS)
        delta = min(HORIZON, T)
        disp = (x @ W_disp).reshape(B, T, nh, bd).transpose(0, 2, 1, 3)
        val = (x @ W_val).reshape(B, T, nh, hs).transpose(0, 2, 1, 3)
        disp_win = _windows(disp, delta)
        val_win = _windows(val, delta)
        cmask = jnp.arange(T)[:, None] - delta + 1 + jnp.arange(delta)[None, :] >= 0
        strain = disp_win - disp[:, :, :, None, :]
        rel_emb = rel_pos_emb[:delta]
        bond_act = jax.nn.gelu(strain @ W_strain + rel_emb @ W_pos, approximate=False)
        bond_logits = (bond_act @ W_bond)[..., 0]
        damage_act = jax.nn.gelu(strain @ W_dmg + b_dmg, approximate=False)
        damage = jax.nn.sigmoid((damage_act @ W_dmg_out)[..., 0] + b_dmg_out[0])
        logits = bond_logits - 10.0 * damage
        logits = jnp.where(cmask[None, None], logits, -jnp.inf)
        weights = jax.nn.softmax(logits, axis=-1)
        out = jnp.einsum('bntd,bntde->bnte', weights, val_win)
        out = out.transpose(0, 2, 1, 3).reshape(B, T, C)
        return out @ W_cproj

    def _L2_xattn_ref(query, mem_state, top_k, Wq, bq, Wk, bk, Wv, bv, Wo, bo):
        import jax, jax.numpy as jnp
        import numpy as np
        B, T, S, D = (4, 256, 512, 128)
        TOP_K = 32

        def _read(query, mem_state, top_k, Wq, bq, Wk, bk, Wv, bv, Wo, bo):
            b, t, d = query.shape
            s = mem_state.shape[1]
            scale = 1.0 / np.sqrt(d)
            q = query @ Wq.T + bq
            k = mem_state @ Wk.T + bk
            v = mem_state @ Wv.T + bv
            scores = jnp.einsum('btd,bsd->bts', q, k) * scale
            if top_k < s:
                vals, idx = jax.lax.top_k(scores, top_k)
                b_ix = jnp.arange(b)[:, None, None]
                t_ix = jnp.arange(t)[None, :, None]
                masked = jnp.full_like(scores, -jnp.inf)
                scores = masked.at[b_ix, t_ix, idx].set(vals)
            attn = jax.nn.softmax(scores, axis=-1)
            ctx = jnp.einsum('bts,bsd->btd', attn, v)
            return ctx @ Wo.T + bo
        return _read(query, mem_state, top_k, Wq, bq, Wk, bk, Wv, bv, Wo, bo)

    def _L2_ffn_ref(x, Wqkv, q_scale, k_scale, Wo, ln_g, ln_b, W1, b1, W2, b2):
        import jax, jax.numpy as jnp
        import numpy as np
        DIM = 128
        DEPTH = 6
        HEADS = 16
        DIM_HEAD = 64
        WINDOW = 32
        INNER = HEADS * DIM_HEAD
        DIM_INNER = int(DIM * 4 * 2 / 3)
        QK_SCALE = 8.0

        def shift_tokens(t):
            a, s = jnp.split(t, 2, -1)
            s = jnp.pad(s, ((0, 0), (1, 0), (0, 0)))[:, :-1]
            return jnp.concatenate([a, s], -1)

        def l2norm(t):
            return t / jnp.maximum(jnp.linalg.norm(t, axis=-1, keepdims=True), 1e-12)

        def rotate_half(x):
            x1, x2 = jnp.split(x, 2, -1)
            return jnp.concatenate([-x2, x1], -1)

        def rotary_tables(n):
            half = jnp.arange(0, DIM_HEAD, 2, dtype=jnp.float32)
            inv_freq = 1.0 / 10000.0 ** (half / DIM_HEAD)
            t = jnp.arange(n, dtype=jnp.float32)
            freqs = t[:, None] * inv_freq[None, :]
            freqs = jnp.concatenate([freqs, freqs], -1)
            base_scale = (half + 0.4 * DIM_HEAD) / (1.4 * DIM_HEAD)
            power = (t - n // 2) / (WINDOW // 2)
            scale = base_scale[None, :] ** power[:, None]
            scale = jnp.concatenate([scale, scale], -1)
            return (freqs, scale)

        def local_attention(q, k, v):
            b, h, n, d = q.shape
            w = WINDOW
            nw = n // w
            bq = q.reshape(b, h, nw, w, d)
            bk = k.reshape(b, h, nw, w, d)
            bv = v.reshape(b, h, nw, w, d)

            def look(t):
                p = jnp.pad(t, ((0, 0), (0, 0), (1, 0), (0, 0), (0, 0)))
                return jnp.concatenate([p[:, :, :nw], p[:, :, 1:]], axis=3)
            bk2, bv2 = (look(bk), look(bv))
            seq = jnp.arange(n).reshape(nw, w)
            seq_p = jnp.pad(seq, ((1, 0), (0, 0)), constant_values=-1)
            jt = jnp.concatenate([seq_p[:nw], seq_p[1:]], axis=1)
            it = seq[:, :, None]
            jb = jt[:, None, :]
            mask = (it < jb) | (it > jb + w) | (jb == -1)
            sim = jnp.einsum('bhwie,bhwje->bhwij', bq, bk2) * QK_SCALE
            sim = jnp.where(mask, -jnp.finfo(sim.dtype).max, sim)
            attn = jax.nn.softmax(sim, -1)
            out = jnp.einsum('bhwij,bhwje->bhwie', attn, bv2)
            return out.reshape(b, h, n, d)

        def attn_layer(x, Wqkv, qs, ksc, Wo):
            b, n, _ = x.shape
            qkv = x @ Wqkv
            q, k, v = jnp.split(qkv, 3, -1)
            sh = lambda t: t.reshape(b, n, HEADS, DIM_HEAD).transpose(0, 2, 1, 3)
            q, k, v = (sh(q), sh(k), sh(v))
            q = l2norm(q) * qs
            k = l2norm(k) * ksc
            freqs, scale = rotary_tables(n)
            cos, sin = (jnp.cos(freqs), jnp.sin(freqs))
            q = q * cos * scale + rotate_half(q) * sin * scale
            inv = 1.0 / scale
            k = k * cos * inv + rotate_half(k) * sin * inv
            out = local_attention(q, k, v)
            out = out.transpose(0, 2, 1, 3).reshape(b, n, INNER)
            return out @ Wo

        def ffn_layer(x, g, bln, W1, b1, W2, b2):
            mu = x.mean(-1, keepdims=True)
            var = ((x - mu) ** 2).mean(-1, keepdims=True)
            xn = (x - mu) / jnp.sqrt(var + 1e-05) * g + bln
            hg = xn @ W1 + b1
            a, gate = jnp.split(hg, 2, -1)
            return a * jax.nn.gelu(gate, approximate=False) @ W2 + b2
        for i in range(DEPTH):
            x = attn_layer(shift_tokens(x), Wqkv[i], q_scale[i], k_scale[i], Wo[i]) + x
            x = ffn_layer(shift_tokens(x), ln_g[i], ln_b[i], W1[i], b1[i], W2[i], b2[i]) + x
        return x

    def _L3_attn_ref(x, Wr, Wk, Wv, Ww, Wo):
        import jax, jax.numpy as jnp
        import numpy as np
        B, T, D, NH = (4, 256, 128, 16)
        HD = D // NH

        def _rwkv7_forward(x, Wr, Wk, Wv, Ww, Wo):
            b, t, d = x.shape
            nh, hd = (NH, d // NH)
            r = jax.nn.sigmoid(x @ Wr.T).reshape(b, t, nh, hd)
            k = (x @ Wk.T).reshape(b, t, nh, hd)
            v = (x @ Wv.T).reshape(b, t, nh, hd)
            w = (jax.nn.sigmoid(x @ Ww.T) * 0.99).reshape(b, t, nh, hd)

            def step(state, inp):
                w_t, k_t, v_t, r_t = inp
                state = state * w_t[..., :, None] + v_t[..., :, None] * k_t[..., None, :]
                out_t = r_t * state.sum(-1)
                return (state, out_t)
            seq = (jnp.moveaxis(w, 1, 0), jnp.moveaxis(k, 1, 0), jnp.moveaxis(v, 1, 0), jnp.moveaxis(r, 1, 0))
            state0 = jnp.zeros((b, nh, hd, hd), dtype=x.dtype)
            _, outs = jax.lax.scan(step, state0, seq)
            out = jnp.moveaxis(outs, 0, 1).reshape(b, t, d)
            eps = jnp.asarray(jnp.finfo(out.dtype).eps, out.dtype)
            out = out * jax.lax.rsqrt(jnp.mean(out * out, axis=-1, keepdims=True) + eps)
            return out @ Wo.T
        return _rwkv7_forward(x, Wr, Wk, Wv, Ww, Wo)

    def _L3_xattn_ref(x, encoder_k, encoder_v, Wq1, bq1, Wk1, bk1, Wv1, bv1, Wo1, bo1, Wq2, bq2, Wk2, bk2, Wv2, bv2, Wo2, bo2):
        import jax, jax.numpy as jnp
        import numpy as np
        B, SD, SE, D, H = (4, 256, 256, 128, 16)
        HD = D // H

        def _mha(xq, xk, xv, Wq, bq, Wk, bk, Wv, bv, Wo, bo, causal):
            q = jnp.einsum('bsd,hde->bhse', xq, Wq) + bq[None, :, None, :]
            k = jnp.einsum('bsd,hde->bhse', xk, Wk) + bk[None, :, None, :]
            v = jnp.einsum('bsd,hde->bhse', xv, Wv) + bv[None, :, None, :]
            scale = 1.0 / jnp.sqrt(jnp.asarray(HD, q.dtype))
            scores = jnp.einsum('bhqe,bhke->bhqk', q, k) * scale
            if causal:
                mask = jnp.tril(jnp.ones((q.shape[2], k.shape[2]), bool))
                scores = jnp.where(mask, scores, jnp.finfo(scores.dtype).min)
            w = jax.nn.softmax(scores, axis=-1)
            out = jnp.einsum('bhqk,bhke->bhqe', w, v)
            out = out.transpose(0, 2, 1, 3).reshape(out.shape[0], out.shape[2], D)
            return out @ Wo + bo
        h = _mha(x, x, x, Wq1, bq1, Wk1, bk1, Wv1, bv1, Wo1, bo1, causal=True)
        out = _mha(h, encoder_k, encoder_v, Wq2, bq2, Wk2, bk2, Wv2, bv2, Wo2, bo2, causal=False)
        return out

    def _L3_ffn_ref(x, w_up, w_down):
        import jax, jax.numpy as jnp
        import numpy as np
        EPS = 1e-08

        def _ternary_linear(x, w):
            alpha = jnp.mean(jnp.abs(w))
            w_t = jnp.sign(w) * (jnp.abs(w) > 0.5 * alpha).astype(w.dtype)
            w_q = w + jax.lax.stop_gradient(w_t - w)
            d = x.shape[-1]
            rms = jnp.sqrt(jnp.sum(x * x, axis=-1, keepdims=True)) / jnp.sqrt(jnp.asarray(d, x.dtype))
            x_norm = x / (rms + EPS)
            return jnp.einsum('bsd,fd->bsf', x_norm, w_q)
        h = jax.nn.gelu(_ternary_linear(x, w_up), approximate=False)
        return _ternary_linear(h, w_down)
    x = _layernorm(x + _L0_attn_ref(x, L0_attn_Wq, L0_attn_Wk, L0_attn_Wv, L0_attn_Wb, L0_attn_conv_q, L0_attn_conv_k, L0_attn_conv_v, L0_attn_fir_s, L0_attn_fir_m, L0_attn_fir_l, L0_attn_gate_w, L0_attn_gate_b, L0_attn_log_temp, L0_attn_eps_param, L0_attn_norm_w, L0_attn_Wo), axis=-1)
    x = _layernorm(x + _L0_xattn_ref(x, ctx_1024, L0_xattn_w_cq, L0_xattn_b_cq, L0_xattn_w_c, L0_xattn_b_c, L0_xattn_w_q, L0_xattn_b_q, L0_xattn_W_l, L0_xattn_b_l), axis=-1)
    x = _layernorm(x + _L0_ffn_ref(x, L0_ffn_gamma, L0_ffn_beta, L0_ffn_Wg, L0_ffn_bg, L0_ffn_W1, L0_ffn_b1, L0_ffn_W2, L0_ffn_b2), axis=-1)
    x = _layernorm(x + _L1_attn_ref(x, L1_attn_w_qkv, L1_attn_b_qkv, L1_attn_w_out, L1_attn_b_out), axis=-1)
    x = _layernorm(x + _L1_xattn_ref(x, ctx_1024, L1_xattn_g_norm, L1_xattn_null_kv, L1_xattn_Wq, L1_xattn_Wkv, L1_xattn_q_scale, L1_xattn_k_scale, L1_xattn_Wout, L1_xattn_g_out), axis=-1)
    x = _layernorm(x + _L1_ffn_ref(x, L1_ffn_gate_w, L1_ffn_gate_b, L1_ffn_w1, L1_ffn_b1, L1_ffn_w2, L1_ffn_b2), axis=-1)
    x = _layernorm(x + _L2_attn_ref(x, L2_attn_W_disp, L2_attn_W_val, L2_attn_rel_pos_emb, L2_attn_W_strain, L2_attn_W_pos, L2_attn_W_bond, L2_attn_W_dmg, L2_attn_b_dmg, L2_attn_W_dmg_out, L2_attn_b_dmg_out, L2_attn_W_cproj), axis=-1)
    x = _layernorm(x + _L2_xattn_ref(x, ctx_1024, 32, L2_xattn_Wq, L2_xattn_bq, L2_xattn_Wk, L2_xattn_bk, L2_xattn_Wv, L2_xattn_bv, L2_xattn_Wo, L2_xattn_bo), axis=-1)
    x = _layernorm(x + _L2_ffn_ref(x, L2_ffn_Wqkv, L2_ffn_q_scale, L2_ffn_k_scale, L2_ffn_Wo, L2_ffn_ln_g, L2_ffn_ln_b, L2_ffn_W1, L2_ffn_b1, L2_ffn_W2, L2_ffn_b2), axis=-1)
    x = _layernorm(x + _L3_attn_ref(x, L3_attn_Wr, L3_attn_Wk, L3_attn_Wv, L3_attn_Ww, L3_attn_Wo), axis=-1)
    x = _layernorm(x + _L3_xattn_ref(x, ctx_1024, ctx_1024, L3_xattn_Wq1, L3_xattn_bq1, L3_xattn_Wk1, L3_xattn_bk1, L3_xattn_Wv1, L3_xattn_bv1, L3_xattn_Wo1, L3_xattn_bo1, L3_xattn_Wq2, L3_xattn_bq2, L3_xattn_Wk2, L3_xattn_bk2, L3_xattn_Wv2, L3_xattn_bv2, L3_xattn_Wo2, L3_xattn_bo2), axis=-1)
    x = _layernorm(x + _L3_ffn_ref(x, L3_ffn_w_up, L3_ffn_w_down), axis=-1)
    return x

_drawn_inputs = setup_inputs


def setup_inputs(seed=0):
    import zlib

    import numpy as np

    out = dict(_drawn_inputs(seed))
    spreads = {'L0_attn_gate_b': (0.0, 0.8),
     'L0_attn_log_temp': (0.0, 0.8),
     'L0_attn_eps_param': (0.019999999552965164, 0.6),
     'L0_attn_norm_w': (1.0, 0.2),
     'L0_ffn_gamma': (1.0, 0.2),
     'L0_ffn_beta': (0.0, 0.1),
     'L0_ffn_bg': (0.0, 0.33),
     'L0_ffn_b1': (0.0, 0.327),
     'L0_ffn_b2': (0.0, 0.1),
     'L1_attn_b_qkv': (0.0, 0.1),
     'L1_attn_b_out': (0.0, 0.1),
     'L1_xattn_g_norm': (1.0, 0.2),
     'L1_xattn_q_scale': (1.0, 0.2),
     'L1_xattn_k_scale': (1.0, 0.2),
     'L1_xattn_g_out': (1.0, 0.2),
     'L2_attn_b_dmg': (0.0, 2.0),
     'L2_xattn_bq': (0.0, 0.484),
     'L2_xattn_bk': (0.0, 2.0),
     'L2_xattn_bv': (0.0, 0.372),
     'L2_xattn_bo': (0.0, 0.1),
     'L2_ffn_q_scale': (1.0, 0.6),
     'L2_ffn_k_scale': (1.0, 0.6),
     'L2_ffn_ln_g': (1.0, 0.6),
     'L2_ffn_ln_b': (0.0, 0.8),
     'L2_ffn_b1': (0.0, 0.8),
     'L2_ffn_b2': (0.0, 0.1),
     'L3_xattn_bq1': (0.0, 0.8),
     'L3_xattn_bk1': (0.0, 2.0),
     'L3_xattn_bv1': (0.0, 0.411),
     'L3_xattn_bo1': (0.0, 0.35),
     'L3_xattn_bq2': (0.0, 0.514),
     'L3_xattn_bk2': (0.0, 2.0),
     'L3_xattn_bv2': (0.0, 0.1),
     'L3_xattn_bo2': (0.0, 0.1)}
    factors = {'L0_attn_Wb': 5.938,
     'L0_attn_fir_s': 36.777,
     'L1_xattn_null_kv': 8.0,
     'L1_ffn_gate_b': 3.043,
     'L1_ffn_b1': 8.0,
     'L1_ffn_b2': 6.7,
     'L2_attn_W_disp': 64.0,
     'L2_attn_rel_pos_emb': 64.0,
     'L2_attn_W_strain': 64.0,
     'L2_attn_W_pos': 64.0,
     'L2_attn_W_bond': 64.0,
     'L2_attn_W_dmg': 64.0,
     'L2_attn_W_dmg_out': 64.0,
     'L2_ffn_W1': 3.754,
     'L2_ffn_W2': 3.822,
     'L3_attn_Ww': 3.22,
     'L3_xattn_Wq1': 3.363,
     'L3_xattn_Wk1': 3.369}
    for name, (base, spread) in spreads.items():
        noise = np.random.default_rng([zlib.crc32(name.encode()), seed]).standard_normal(out[name].shape)
        drawn = base * np.exp(spread * noise) if base else spread * noise
        out[name] = jnp.asarray(drawn.astype(out[name].dtype))
    for name, factor in factors.items():
        out[name] = (out[name] * factor).astype(out[name].dtype)
    return out
```

```python
from contextlib import ExitStack

import numpy as np

import concourse.bass as bass
from concourse import mybir

F32 = mybir.dt.float32
U32 = mybir.dt.uint32
ALU = mybir.AluOpType
ACT = mybir.ActivationFunctionType
AX = mybir.AxisListType

P = 128
B = 4
T = 256
D = 128
NT = B * T // P
TB = T // P
S = 1601
BANK = 512


class Counter:

    def __init__(self, place, name, per=1, ahead=0):
        self.sem = place.semaphore(name)
        self.per, self.ahead = per, ahead

    def nth(self, n, it=0):
        return it * self.per + (n + self.ahead)


class Place:

    count = 0

    def __init__(self, nc, ctx, name):
        Place.count += 1
        self.nc, self.ctx, self.name = nc, ctx, f"{name}{Place.count}"
        self.semaphores = []
        ctx.callback(self.close)

    def close(self):
        if self.semaphores:
            self.nc.clear_and_free_semaphores(self.semaphores)
            self.nc.all_engine_barrier()

    def sbuf(self, name, shape, dt=F32):
        return self.ctx.enter_context(self.nc.sbuf_tensor(f"{self.name}_{name}", shape, dt))

    def psum(self, name, shape, dt=F32):
        return self.ctx.enter_context(self.nc.psum_tensor(f"{self.name}_{name}", shape, dt))

    def semaphore(self, name):
        self.semaphores.append(self.nc.alloc_semaphore(f"{self.name}_{name}"))
        return self.semaphores[-1]

    def counter(self, name, per=1, ahead=0):
        return Counter(self, name, per, ahead)


class Model:

    def __init__(self, nc, ctx, dram):
        place = Place(nc, ctx, "model")
        self.nc, self.dram = nc, dram
        self.X = place.sbuf("X", [P, NT, D])
        self.XT = place.sbuf("XT", [P, B * T])
        self.Y = place.sbuf("Y", [P, NT, D])
        self.ident = place.sbuf("ident", [P, P])
        self.ones = place.sbuf("ones", [P, P])


def load_model(m):
    nc = m.nc
    with ExitStack() as ctx:
        place = Place(nc, ctx, "load")
        loaded = place.counter("loaded")
        turned = place.counter("turned")
        ps = place.psum("ps", [P, NT * P])
        block = ctx.enter_context(nc.Block())

        @block.sync
        def _(sp):
            sp.dma_start(m.X[:, :, :], m.dram["x"].rearrange("b (u p) d -> p (b u) d", p=P)).then_inc(loaded.sem, 16)
            sp.dma_start(m.ident[:, :], m.dram["c_ident"]).then_inc(loaded.sem, 16)

        @block.gpsimd
        def _(pool):
            pool.memset(m.ones[:, :], 1.0)

        @block.tensor
        def _(pe):
            pe.wait_ge(loaded.sem, loaded.nth(32))
            for t in range(NT):
                mm = pe.transpose(ps[:, t * P:(t + 1) * P], m.X[:, t, :], m.ident[:, :])
            mm.then_inc(turned.sem, 1)

        @block.vector
        def _(dve):
            dve.wait_ge(turned.sem, turned.nth(1))
            dve.tensor_copy(m.XT[:, :], ps[:, :])


def post_norm(m, last=False):
    nc = m.nc
    with ExitStack() as ctx:
        place = Place(nc, ctx, "norm")
        stats = place.sbuf("stats", [P, NT, 6])
        mv = place.sbuf("mv", [P, NT, 2])
        rstd = place.sbuf("rstd", [P, NT])
        ps = place.psum("ps", [P, NT * P])
        var_ready = place.counter("var_ready")
        root_ready = place.counter("root_ready")
        x_ready = place.counter("x_ready")
        turned = place.counter("turned")
        stored = place.counter("stored")
        block = ctx.enter_context(nc.Block())

        @block.vector
        def _(dve):
            dve.tensor_tensor(m.Y[:, :, :], m.Y[:, :, :], m.X[:, :, :], ALU.add)
            dve.drain()
            for t in range(NT):
                dve.bn_stats(stats[:, t, :], m.Y[:, t, :])
            dve.drain()
            for t in range(NT):
                dve.bn_aggr(mv[:, t, :], stats[:, t, :])
            dve.drain()
            dve.tensor_scalar(rstd[:, :], mv[:, :, 1], 1e-5, None, ALU.add).then_inc(var_ready.sem, 1)
            dve.wait_ge(root_ready.sem, root_ready.nth(1))
            dve.reciprocal(rstd[:, :], rstd[:, :])
            dve.drain()
            for t in range(NT):
                dve.tensor_scalar(m.X[:, t, :], m.Y[:, t, :], mv[:, t, 0:1], rstd[:, t:t + 1],
                                  ALU.subtract, ALU.mult).then_inc(x_ready.sem, 1)
            if not last:
                for half in range(2):
                    dve.wait_ge(turned.sem, turned.nth(half + 1))
                    dve.tensor_copy(m.XT[:, half * BANK:(half + 1) * BANK], ps[:, half * BANK:(half + 1) * BANK])

        @block.scalar
        def _(act):
            act.wait_ge(var_ready.sem, var_ready.nth(1))
            act.activation(rstd[:, :], rstd[:, :], ACT.Sqrt).then_inc(root_ready.sem, 1)

        if last:
            @block.sync
            def _(sp):
                sp.wait_ge(x_ready.sem, x_ready.nth(NT))
                sp.dma_start(m.dram["out"].rearrange("b (u p) d -> p (b u) d", p=P), m.X[:, :, :])\
                  .then_inc(stored.sem, 16)
                sp.wait_ge(stored.sem, stored.nth(16))
        else:
            @block.tensor
            def _(pe):
                for t in range(NT):
                    pe.wait_ge(x_ready.sem, x_ready.nth(t + 1))
                    mm = pe.transpose(ps[:, t * P:(t + 1) * P], m.X[:, t, :], m.ident[:, :])
                    if t % 4 == 3:
                        mm.then_inc(turned.sem, 1)


def after(u, back, count):
    return (u - back) % count, (u - back) // count


class Heads:

    def __init__(self, name, keys, heads, stride, dv, scale=1.0, context=False, biased=False, cosine=False, masked=False,
                 n_heads=16, choose=0, rotary=False, null=False):
        self.name, self.keys, self.heads, self.stride, self.dv = name, keys, heads, stride, dv
        self.scale, self.context, self.biased, self.cosine, self.masked = scale, context, biased, cosine, masked
        self.groups = n_heads // heads
        self.rotary, self.null = rotary, null
        self.choose = choose


def attention(m, a, xT, accT, neg_max_out=None, layer=0, add=False):
    nc = m.nc
    K = a.keys
    real = S if a.context else T
    KC = -(-K // P)
    W = K + T
    pieces = [(c, min(c + BANK, W)) for c in range(0, W, BANK)]
    per_turn = 4 if K > BANK else 2
    v_turn = 4 if K > BANK else 1
    turns = [(c, min(c + per_turn, KC)) for c in range(0, KC, per_turn)]
    v_turns = [(c, min(c + v_turn, KC)) for c in range(0, KC, v_turn)]
    GC = a.heads * a.dv
    U = a.heads * TB
    NV, G = len(v_turns), len(turns)
    R = NV + U * G + 2
    assert R % 2 == 0 and NV % 2 == 0
    NP = len(pieces)
    WC = 2 * P + GC + 4
    score_bufs = 1 if K > BANK else 2

    def ring_of(u, g):
        return NV + u * G + g

    with ExitStack() as ctx:
        place = Place(nc, ctx, "heads")
        source = place.sbuf("source", [P, real])
        w = place.sbuf("w", [P, WC])
        wo = place.sbuf("wo", [GC, D])
        bv = place.sbuf("bv", [1, GC]) if a.biased else None
        raw = place.sbuf("raw", [P, W])
        KQ = place.sbuf("KQ", [P, W]) if a.cosine else raw
        squares = place.sbuf("squares", [P, W]) if a.cosine else None
        together = place.sbuf("together", [P, P]) if a.cosine else None
        mask = place.sbuf("mask", [P, TB, K]) if a.masked else None
        rotation = place.sbuf("rotation", [P, P]) if a.rotary else None
        cos = place.sbuf("cos", [P, W]) if a.rotary else None
        sin = place.sbuf("sin", [P, W]) if a.rotary else None
        V = place.sbuf("V", [P, KC, GC])
        probs = place.sbuf("probs", [P, 2, KC * P])
        probsT = place.sbuf("probsT", [P, 2, KC * P])
        neg_max = place.sbuf("neg_max", [P, 2])
        total = place.sbuf("total", [P, 2])
        inv = place.sbuf("inv", [P, 2])
        rest = place.sbuf("rest", [P, K]) if a.choose else None
        top = place.sbuf("top", [P, 2, 8]) if a.choose else None
        O = place.sbuf("O", [P, TB, GC])
        OT = place.sbuf("OT", [GC, T])
        ps_s = place.psum("ps_s", [P, 4 * BANK])
        ps_r = place.psum("ps_r", [P, 2, BANK])
        ps_o = place.psum("ps_o", [P, 2, BANK])

        ONCE = 16 * (a.cosine + 3 * a.rotary + 2 * a.null + a.masked)
        once_in = place.counter("once_in")
        cleared = place.counter("cleared")
        source_in = place.counter("source_in", per=16 if a.context else 1)
        weights_in = place.counter("weights_in", per=48 if a.biased else 32)
        projected = place.counter("projected", per=NP)
        k_raw = place.counter("k_raw", per=NP, ahead=NP)
        q_raw = place.counter("q_raw", per=1, ahead=1)
        squared = place.counter("squared", per=NP)
        sums_ready = place.counter("sums_ready", per=NP)
        sums_taken = place.counter("sums_taken", per=NP)
        norm_ready = place.counter("norm_ready", per=NP)
        scaled = place.counter("scaled", per=NP)
        rotated = place.counter("rotated")
        roped = place.counter("roped")
        scores_ready = place.counter("scores_ready", per=U)
        chosen = place.counter("chosen", per=U, ahead=U) if a.choose else None
        max_ready = place.counter("max_ready", per=U)
        probs_ready = place.counter("probs_ready", per=U, ahead=U)
        turned = place.counter("turned", per=R, ahead=R)
        taken_out = [place.counter(f"taken_out_{j}", per=R // 2, ahead=R // 2) for j in range(2)]
        out_ready = place.counter("out_ready", per=U, ahead=U)
        out_taken = place.counter("out_taken", per=U, ahead=U)
        block = ctx.enter_context(nc.Block())

        def emptied(i):
            return taken_out[i % 2], i // 2 + 1

        @block.sync
        def _(sp):
            if a.cosine:
                sp.dma_start(together[:, :], m.dram["c_same_head64"]).then_inc(once_in.sem, 16)
            if a.rotary:
                sp.dma_start(rotation[:, :], m.dram["c_rotation"]).then_inc(once_in.sem, 16)
                sp.dma_start(cos[:, :], m.dram["c_cos"]).then_inc(once_in.sem, 16)
                sp.dma_start(sin[:, :], m.dram["c_sin"]).then_inc(once_in.sem, 16)
            if a.null:
                sp.dma_start(raw[:, real:K], m.dram[a.name + "_null_k"]).then_inc(once_in.sem, 16)
                sp.wait_ge(cleared.sem, cleared.nth(1))
                sp.dma_start(V[real % P:real % P + 1, KC - 1, :], m.dram[a.name + "_null_v"]).then_inc(once_in.sem, 16)
            if a.masked:
                sp.dma_start(mask[:, :, :], m.dram[a.name + "_mask"]).then_inc(once_in.sem, 16)
            with sp.Fori(0, B) as b:
                if a.context:
                    sp.wait_ge(turned.sem, turned.nth(NV, b * a.groups - 1))
                    sp.dma_start(source[:, :], m.dram["ctx_T"][bass.ds(b, 1), :, :].rearrange("b d s -> (b d) s"))\
                      .then_inc(source_in.sem, 16)
                with sp.Fori(0, a.groups) as g:
                    it, row = b * a.groups + g, layer * a.groups + g
                    sp.wait_ge(turned.sem, turned.nth(0, it))
                    sp.dma_start(w[:, :], m.dram[a.name + "_w"][bass.ds(row, 1), :, :].rearrange("g p c -> (g p) c"))\
                      .then_inc(weights_in.sem, 16)
                    sp.dma_start(wo[:, :], m.dram[a.name + "_wo"][bass.ds(row, 1), :, :].rearrange("g c d -> (g c) d"))\
                      .then_inc(weights_in.sem, 16)
                    if a.biased:
                        sp.dma_start(bv[:, :], m.dram[a.name + "_bv"][bass.ds(row, 1), :]).then_inc(weights_in.sem, 16)

        if a.cosine:
            @block.gpsimd
            def _(pool):
                pool.wait_ge(once_in.sem, once_in.nth(ONCE))
                with pool.Fori(0, B * a.groups) as it:
                    for n, (c0, c1) in enumerate(pieces):
                        pool.wait_ge(k_raw.sem, k_raw.nth(n + 1, it))
                        if c1 > K:
                            pool.wait_ge(q_raw.sem, q_raw.nth(1, it))
                        pool.tensor_tensor(squares[:, c0:c1], raw[:, c0:c1], raw[:, c0:c1], ALU.mult)\
                            .then_inc(squared.sem, 1)

        @block.tensor
        def _(pe):
            pe.sem_inc(turned.sem, turned.ahead)
            pe.sem_inc(out_ready.sem, out_ready.ahead)
            if ONCE:
                pe.wait_ge(once_in.sem, once_in.nth(ONCE))
            with pe.Fori(0, B) as b, pe.Fori(0, a.groups) as g:
                it = b * a.groups + g
                pe.wait_ge(source_in.sem, source_in.nth(source_in.per, b if a.context else it))
                pe.wait_ge(weights_in.sem, weights_in.nth(weights_in.per, it))
                pe.wait_ge(probs_ready.sem, probs_ready.nth(0, it))
                pe.wait_ge(k_raw.sem, k_raw.nth(0, it))
                pe.wait_ge(q_raw.sem, q_raw.nth(0, it))
                for n, (c0, c1) in enumerate(pieces):
                    if c0 < real:
                        c = min(c1, real)
                        mm = pe.matmul(ps_s[:, c0:c], w[:, P:2 * P], source[:, c0:c], start=True, stop=True)
                    if c1 > K:
                        mm = pe.matmul(ps_s[:, K:W], w[:, 0:P], xT[:, bass.ds(b * T, T)], start=True, stop=True)
                    mm.then_inc(projected.sem, 1)
                for i, (c0, c1) in enumerate(v_turns):
                    side, nth = emptied(i - 2)
                    pe.wait_ge(side.sem, side.nth(nth, it))
                    for c in range(c0, c1):
                        rows = min(P, real - c * P)
                        out = ps_r[0:rows, i % 2, (c - c0) * GC:(c - c0 + 1) * GC]
                        mm = pe.matmul(out, source[:, c * P:c * P + rows], w[:, 2 * P:2 * P + GC], start=True, stop=not a.biased)
                        if a.biased:
                            mm = pe.matmul(out, m.ones[0:1, 0:rows], bv[:, :], start=False, stop=True)
                    mm.then_inc(turned.sem, 1)
                if a.cosine:
                    for n, (c0, c1) in enumerate(pieces):
                        pe.wait_ge(squared.sem, squared.nth(n + 1, it))
                        if c1 > K:
                            pe.wait_ge(q_raw.sem, q_raw.nth(1, it))
                        pe.matmul(ps_s[:, c0:c1], together[:, :], squares[:, c0:c1], start=True, stop=True)\
                          .then_inc(sums_ready.sem, 1)
                    pe.wait_ge(scaled.sem, scaled.nth(NP, it))
                    if a.rotary:
                        pe.matmul(ps_s[:, 0:W], rotation[:, :], KQ[:, :], start=True, stop=True).then_inc(rotated.sem, 1)
                        pe.wait_ge(roped.sem, roped.nth(1, it))
                else:
                    pe.wait_ge(k_raw.sem, k_raw.nth(NP, it))
                    pe.wait_ge(q_raw.sem, q_raw.nth(1, it))

                def scores(u):
                    h, t = u // TB, u % TB
                    rows = slice(h * a.stride, (h + 1) * a.stride)
                    pe.wait_ge(probs_ready.sem, probs_ready.nth(u + 1 - score_bufs, it))
                    first = 0 if score_bufs == 1 else (2 + u % 2) * BANK
                    for c0 in range(0, K, BANK):
                        c1 = min(c0 + BANK, K)
                        mm = pe.matmul(ps_s[:, first + c0:first + c1], KQ[rows, K + t * P:K + (t + 1) * P], KQ[rows, c0:c1],
                                       start=True, stop=not a.masked)
                        if a.masked:
                            mm = pe.matmul(ps_s[:, first + c0:first + c1], m.ident[:, :], mask[:, t, c0:c1],
                                           start=False, stop=True)
                    mm.then_inc(scores_ready.sem, 1)

                def turn(u, j):
                    i = ring_of(u, j)
                    if j == 0:
                        pe.wait_ge((chosen or probs_ready).sem, (chosen or probs_ready).nth(u + 1, it))
                    side, nth = emptied(i - 2)
                    pe.wait_ge(side.sem, side.nth(nth, it))
                    c0, c1 = turns[j]
                    for c in range(c0, c1):
                        mm = pe.transpose(ps_r[:, i % 2, (c - c0) * P:(c - c0 + 1) * P], probs[:, u % 2, c * P:(c + 1) * P],
                                          m.ident[:, :])
                    mm.then_inc(turned.sem, 1)

                def times_v(u, j):
                    i, h = ring_of(u, j), u // TB
                    if j == 0:
                        side, nth = emptied(NV - 1 if NV % 2 == i % 2 else NV - 2)
                        pe.wait_ge(side.sem, side.nth(nth, it))
                        pe.wait_ge(out_taken.sem, out_taken.nth(u - 1, it))
                    side, nth = emptied(i)
                    pe.wait_ge(side.sem, side.nth(nth, it))
                    c0, c1 = turns[j]
                    for c in range(c0, c1):
                        mm = pe.matmul(ps_o[:, u % 2, 0:a.dv], probsT[:, u % 2, c * P:(c + 1) * P], V[:, c, h * a.dv:(h + 1) * a.dv],
                                       start=(c == 0), stop=(c == KC - 1))
                    if j == G - 1:
                        mm.then_inc(out_ready.sem, 1)

                scores(0)
                for u in range(U):
                    if u + 1 < U:
                        scores(u + 1)
                    for j in range(G):
                        turn(u, j)
                        if j >= 1:
                            times_v(u, j - 1)
                    times_v(u, G - 1)
                i = R - 2
                pe.wait_ge(out_taken.sem, out_taken.nth(U, it))
                side, nth = emptied(i - 2)
                pe.wait_ge(side.sem, side.nth(nth, it))
                for t in range(TB):
                    mm = pe.transpose(ps_r[0:GC, i % 2, t * P:(t + 1) * P], O[:, t, :], m.ident[:, :])
                mm.then_inc(turned.sem, 1)
                side, nth = emptied(i)
                pe.wait_ge(side.sem, side.nth(nth, it))
                side, nth = emptied(i - 1)
                pe.wait_ge(side.sem, side.nth(nth, it))
                pe.matmul(ps_r[:, (i + 1) % 2, 0:T], wo[:, :], OT[:, :], start=True, stop=True).then_inc(turned.sem, 1)

        def take_values(engine, copy, i, it):
            c0, c1 = v_turns[i]
            engine.wait_ge(turned.sem, turned.nth(i + 1, it))
            engine.wait_ge(out_ready.sem, out_ready.nth(0, it))
            full = min(c1, real // P)
            if full > c0:
                ins = copy(V[:, c0:full, :], ps_r[:, i % 2, 0:(full - c0) * GC].rearrange("p (c v) -> p c v", v=GC))
            if full < c1:
                rows = real - full * P
                ins = copy(V[0:rows, full, :], ps_r[0:rows, i % 2, (full - c0) * GC:(full - c0 + 1) * GC])
            ins.then_inc(taken_out[i % 2].sem, 1)

        def take_turned(engine, copy, u, parity, it):
            for j, (c0, c1) in enumerate(turns):
                i = ring_of(u, j)
                if i % 2 == parity:
                    engine.wait_ge(turned.sem, turned.nth(i + 1, it))
                    engine.wait_ge(out_ready.sem, out_ready.nth(u - 1, it))
                    copy(probsT[:, u % 2, c0 * P:c1 * P], ps_r[:, i % 2, 0:(c1 - c0) * P])\
                        .then_inc(taken_out[parity].sem, 1)

        @block.scalar
        def _(act):
            def copy(out, in_):
                return act.activation(out, in_, ACT.Copy)

            act.sem_inc(probs_ready.sem, probs_ready.ahead)
            act.sem_inc(taken_out[0].sem, taken_out[0].ahead)
            act.sem_inc(k_raw.sem, k_raw.ahead)
            act.wait_ge(cleared.sem, cleared.nth(1))
            if ONCE:
                act.wait_ge(once_in.sem, once_in.nth(ONCE))
            with act.Fori(0, B) as b, act.Fori(0, a.groups) as g:
                it = b * a.groups + g
                if not a.context:
                    act.wait_ge(turned.sem, turned.nth(0, it))
                    act.activation(source[:, :], xT[:, bass.ds(b * T, T)], ACT.Copy).then_inc(source_in.sem, 1)
                act.wait_ge(weights_in.sem, weights_in.nth(weights_in.per, it))
                for n, (c0, c1) in enumerate(pieces):
                    act.wait_ge(projected.sem, projected.nth(n + 1, it))
                    c = min(c1, real)
                    if a.biased:
                        act.activation(raw[:, c0:c], ps_s[:, c0:c], ACT.Identity, bias=w[:, 2 * P + GC + 1:2 * P + GC + 2])\
                           .then_inc(k_raw.sem, 1)
                    else:
                        act.activation(raw[:, c0:c], ps_s[:, c0:c], ACT.Copy).then_inc(k_raw.sem, 1)
                for i in range(0, NV, 2):
                    take_values(act, copy, i, it)
                if a.cosine:
                    for n, (c0, c1) in enumerate(pieces):
                        act.wait_ge(sums_taken.sem, sums_taken.nth(n + 1, it))
                        act.activation(squares[:, c0:c1], squares[:, c0:c1], ACT.Ln, scale=NORM_RANGE)
                        act.drain()
                        act.activation(squares[:, c0:c1], squares[:, c0:c1], ACT.Exp, scale=-0.5).then_inc(norm_ready.sem, 1)

                def exps(u):
                    act.wait_ge(max_ready.sem, max_ready.nth(u + 1, it))
                    back, steps = after(u, 2, U)
                    act.wait_ge(turned.sem, turned.nth(ring_of(back, G - 1) + 1 + steps * R, it))
                    act.wait_ge(out_taken.sem, out_taken.nth(u - 1, it))
                    first = 0 if score_bufs == 1 else (2 + u % 2) * BANK
                    act.activation(probs[:, u % 2, 0:K], ps_s[:, first:first + K], ACT.Exp, bias=neg_max[:, u % 2:u % 2 + 1],
                                   accum_out=None if a.choose else total[:, u % 2:u % 2 + 1]).then_inc(probs_ready.sem, 1)

                exps(0)
                for u in range(U):
                    if u + 1 < U:
                        exps(u + 1)
                    take_turned(act, copy, u, 0, it)
                act.wait_ge(turned.sem, turned.nth(R - 2 + 1, it))
                copy(OT[:, :], ps_r[0:GC, 0, 0:T]).then_inc(taken_out[0].sem, 1)

        @block.vector
        def _(dve):
            dve.sem_inc(taken_out[1].sem, taken_out[1].ahead)
            dve.sem_inc(out_taken.sem, out_taken.ahead)
            if a.choose:
                dve.sem_inc(chosen.sem, chosen.ahead)
            dve.sem_inc(q_raw.sem, q_raw.ahead)
            dve.memset(V[:, :, :], 0.0)
            if KC * P > K:
                dve.memset(probs[:, :, K:], 0.0)
            if not add:
                dve.memset(accT[:, :], 0.0)
            dve.drain()
            dve.sem_inc(cleared.sem, 1)
            if ONCE:
                dve.wait_ge(once_in.sem, once_in.nth(ONCE))
            with dve.Fori(0, B) as b, dve.Fori(0, a.groups) as g:
                it = b * a.groups + g
                dve.wait_ge(weights_in.sem, weights_in.nth(weights_in.per, it))
                dve.wait_ge(k_raw.sem, k_raw.nth(NP, it))
                if a.biased:
                    dve.tensor_scalar(raw[:, K:W], ps_s[:, K:W], w[:, 2 * P + GC:2 * P + GC + 1], a.scale, ALU.add, ALU.mult)\
                       .then_inc(q_raw.sem, 1)
                else:
                    dve.tensor_copy(raw[:, K:W], ps_s[:, K:W]).then_inc(q_raw.sem, 1)
                for i in range(1, NV, 2):
                    take_values(dve, dve.tensor_copy, i, it)
                if a.cosine:
                    for n, (c0, c1) in enumerate(pieces):
                        dve.wait_ge(sums_ready.sem, sums_ready.nth(n + 1, it))
                        dve.tensor_scalar(squares[:, c0:c1], ps_s[:, c0:c1], 1e-24, None, ALU.max).then_inc(sums_taken.sem, 1)
                    for n, (c0, c1) in enumerate(pieces):
                        dve.wait_ge(norm_ready.sem, norm_ready.nth(n + 1, it))
                        for lo, hi, col in ((c0, min(c1, K), 3), (max(c0, K), c1, 2)):
                            if lo < hi:
                                ins = dve.scalar_tensor_tensor(out=KQ[:, lo:hi], in0=raw[:, lo:hi],
                                                               scalar=w[:, 2 * P + GC + col:2 * P + GC + col + 1],
                                                               in1=squares[:, lo:hi], op0=ALU.mult, op1=ALU.mult)
                        if c1 == W:
                            dve.drain()
                            ins = dve.tensor_scalar(KQ[:, K:W], KQ[:, K:W], a.scale * NORM_RANGE, None, ALU.mult)
                        ins.then_inc(scaled.sem, 1)
                    if a.rotary:
                        dve.wait_ge(rotated.sem, rotated.nth(1, it))
                        dve.tensor_tensor(squares[:, :], ps_s[:, 0:W], sin[:, :], ALU.mult)
                        dve.tensor_tensor(KQ[:, :], KQ[:, :], cos[:, :], ALU.mult)
                        dve.drain()
                        dve.tensor_tensor(KQ[:, :], KQ[:, :], squares[:, :], ALU.add).then_inc(roped.sem, 1)

                def maxima(u):
                    dve.wait_ge(scores_ready.sem, scores_ready.nth(u + 1, it))
                    first = 0 if score_bufs == 1 else (2 + u % 2) * BANK
                    dve.wait_ge(probs_ready.sem, probs_ready.nth(u - 1, it))
                    if a.choose:
                        dve.memset(top[:, 0, :], 0.0)
                        dve.drain()
                        dve.max(top[:, 0, :], ps_s[:, first:first + K])
                        dve.drain()
                        dve.match_replace(rest[:, :], top[:, 0, :], ps_s[:, first:first + K], TAKEN)
                        dve.tensor_scalar(neg_max[:, u % 2:u % 2 + 1], top[:, 0, 0:1], -1.0, None, ALU.mult)\
                           .then_inc(max_ready.sem, 1)
                        for r in range(1, a.choose // 8):
                            dve.drain()
                            dve.max(top[:, r % 2, :], rest[:, :])
                            dve.drain()
                            dve.match_replace(rest[:, :], top[:, r % 2, :], rest[:, :], TAKEN)
                        dve.drain()
                        dve.wait_ge(probs_ready.sem, probs_ready.nth(u + 1, it))
                        dve.scalar_tensor_tensor(out=probs[:, u % 2, 0:K], in0=rest[:, :], scalar=TAKEN, in1=probs[:, u % 2, 0:K],
                                                 op0=ALU.is_equal, op1=ALU.mult, accum_out=total[:, u % 2:u % 2 + 1])\
                           .then_inc(chosen.sem, 1)
                        return
                    dve.tensor_reduce(neg_max[:, u % 2:u % 2 + 1], ps_s[:, first:first + K], AX.X, ALU.max, negate=True)\
                       .then_inc(max_ready.sem, 1)
                    if neg_max_out is not None:
                        dve.drain()
                        dve.tensor_copy(neg_max_out[:, bass.ds(b * TB + u, 1)], neg_max[:, u % 2:u % 2 + 1])

                maxima(0)
                for u in range(U):
                    if u + 1 < U:
                        maxima(u + 1)
                    take_turned(dve, dve.tensor_copy, u, 1, it)
                    h, t = u // TB, u % TB
                    if a.choose:
                        dve.drain()
                    else:
                        dve.wait_ge(probs_ready.sem, probs_ready.nth(u + 1, it))
                    dve.reciprocal(inv[:, u % 2:u % 2 + 1], total[:, u % 2:u % 2 + 1])
                    dve.drain()
                    dve.wait_ge(out_ready.sem, out_ready.nth(u + 1, it))
                    dve.wait_ge(turned.sem, turned.nth(R - 2 + 1 - R, it))
                    dve.tensor_scalar(O[:, t, h * a.dv:(h + 1) * a.dv], ps_o[:, u % 2, 0:a.dv], inv[:, u % 2:u % 2 + 1], None,
                                      ALU.mult).then_inc(out_taken.sem, 1)
                dve.drain()
                dve.wait_ge(turned.sem, turned.nth(R - 1 + 1, it))
                dve.tensor_tensor(accT[:, bass.ds(b * T, T)], accT[:, bass.ds(b * T, T)], ps_r[:, 1, 0:T], ALU.add)\
                   .then_inc(taken_out[1].sem, 1)


TAKEN = -3.0e38
NORM_RANGE = float(2 ** 20)


def to_rows(m, accT, norm=None, bias=None):
    nc = m.nc
    with ExitStack() as ctx:
        place = Place(nc, ctx, "rows")
        ps = place.psum("ps", [P, NT * P])
        turned = place.counter("turned")
        stats = place.sbuf("stats", [P, NT, 6])
        mv = place.sbuf("mv", [P, NT, 2])
        rstd = place.sbuf("rstd", [P, NT])
        gain = place.sbuf("gain", [P, D])
        gain_in = place.counter("gain_in")
        var_ready = place.counter("var_ready")
        root_ready = place.counter("root_ready")
        block = ctx.enter_context(nc.Block())

        @block.tensor
        def _(pe):
            for t in range(NT):
                mm = pe.transpose(ps[:, t * P:(t + 1) * P], accT[:, t * P:(t + 1) * P], m.ident[:, :])
            mm.then_inc(turned.sem, 1)

        if norm is not None:
            @block.sync
            def _(sp):
                sp.dma_start(gain[:, :], norm.rearrange("(o d) -> o d", o=1).broadcast_to([P, D])).then_inc(gain_in.sem, 16)

            @block.scalar
            def _(act):
                act.wait_ge(var_ready.sem, var_ready.nth(1))
                act.activation(rstd[:, :], rstd[:, :], ACT.Sqrt).then_inc(root_ready.sem, 1)

        @block.vector
        def _(dve):
            dve.wait_ge(turned.sem, turned.nth(1))
            dve.tensor_copy(m.Y[:, :, :], ps[:, :].rearrange("p (t d) -> p t d", d=D))
            if norm is None:
                return
            dve.drain()
            for t in range(NT):
                dve.bn_stats(stats[:, t, :], m.Y[:, t, :])
            dve.drain()
            for t in range(NT):
                dve.bn_aggr(mv[:, t, :], stats[:, t, :])
            dve.drain()
            dve.tensor_scalar(rstd[:, :], mv[:, :, 1], 1e-5, None, ALU.add).then_inc(var_ready.sem, 1)
            dve.wait_ge(root_ready.sem, root_ready.nth(1))
            dve.reciprocal(rstd[:, :], rstd[:, :])
            dve.wait_ge(gain_in.sem, gain_in.nth(16))
            dve.drain()
            for t in range(NT):
                dve.tensor_scalar(m.Y[:, t, :], m.Y[:, t, :], mv[:, t, 0:1], rstd[:, t:t + 1], ALU.subtract, ALU.mult)
            dve.drain()
            for t in range(NT):
                dve.tensor_tensor(m.Y[:, t, :], m.Y[:, t, :], gain[:, :], ALU.mult)


def add_column(m, accT, column):
    nc = m.nc
    with ExitStack() as ctx:
        place = Place(nc, ctx, "bias")
        bias = place.sbuf("bias", [P, 1])
        bias_in = place.counter("bias_in")
        block = ctx.enter_context(nc.Block())

        @block.sync
        def _(sp):
            sp.dma_start(bias[:, :], column.rearrange("(p o) -> p o", o=1)).then_inc(bias_in.sem, 16)

        @block.vector
        def _(dve):
            dve.wait_ge(bias_in.sem, bias_in.nth(16))
            dve.tensor_scalar(accT[:, :], accT[:, :], bias[:, 0:1], None, ALU.add)


def gated_delta(m):
    nc = m.nc
    with ExitStack() as outer:
        keep = Place(nc, outer, "delta")
        vT = keep.sbuf("vT", [P, B, FIR_PAD + T])
        taps = keep.sbuf("taps", [P, 12 + 81])
        delta = keep.sbuf("delta", [P, NT, D])
        with ExitStack() as mid:
            inner = Place(nc, mid, "chunks")
            qT = inner.sbuf("qT", [P, B * T])
            kT = inner.sbuf("kT", [P, B * T])
            kbT = inner.sbuf("kbT", [P, B * T])
            vbT = inner.sbuf("vbT", [P, B * T])
            u = inner.sbuf("u", [P, NT, D])
            k = inner.sbuf("k", [P, NT, D])
            wT = inner.sbuf("wT", [P, B * T])
            attnT = inner.sbuf("attnT", [P, NT, 4, P])
            delta_project(m, taps, qT, kT, kbT, vT, vbT)
            delta_chunks(m, qT, kT, kbT, vbT, u, k, wT, attnT)
            delta_scan(m, qT, k, u, wT, attnT, delta)
        delta_mix(m, vT, taps, delta)


FIR_PAD = 62


def delta_project(m, taps, qT, kT, kbT, vT, vbT):
    nc = m.nc
    with ExitStack() as ctx:
        place = Place(nc, ctx, "proj")
        w = place.sbuf("w", [P, 4, D])
        same = place.sbuf("same", [P, P])
        raw = place.sbuf("raw", [P, 3, B, 3 + T])
        conv = place.sbuf("conv", [P, 3, B, T])
        beta = place.sbuf("beta", [P, B * T])
        sq = place.sbuf("sq", [P, 2, B * T])
        ps = place.psum("ps", [P, 2, BANK])
        ps_n = place.psum("ps_n", [P, 4, BANK])
        w_in = place.counter("w_in")
        product_ready = place.counter("product_ready")
        product_taken = place.counter("product_taken")
        conv_ready = place.counter("conv_ready")
        silu_ready = place.counter("silu_ready")
        beta_ready = place.counter("beta_ready")
        sq_ready = place.counter("sq_ready")
        sum_ready = place.counter("sum_ready")
        sum_taken = place.counter("sum_taken")
        root_ready = place.counter("root_ready")
        block = ctx.enter_context(nc.Block())

        def cols(half):
            return slice(half * BANK, (half + 1) * BANK)

        @block.sync
        def _(sp):
            sp.dma_start(w[:, :, :], m.dram["L0_attn_proj"]).then_inc(w_in.sem, 16)
            sp.dma_start(same[:, :], m.dram["c_same_head32"]).then_inc(w_in.sem, 16)
            sp.dma_start(taps[:, :], m.dram["L0_attn_taps"]).then_inc(w_in.sem, 16)

        @block.tensor
        def _(pe):
            pe.wait_ge(w_in.sem, w_in.nth(48))
            for n in range(8):
                i, half = n // 2, n % 2
                if n >= 2:
                    pe.wait_ge(product_taken.sem, product_taken.nth(n - 1))
                pe.matmul(ps[:, n % 2, :], w[:, i, :], m.XT[:, cols(half)], start=True, stop=True).then_inc(product_ready.sem, 1)
            for n in range(4):
                pe.wait_ge(sq_ready.sem, sq_ready.nth(n // 2 + 1))
                pe.matmul(ps_n[:, n, :], same[:, :], sq[:, n // 2, cols(n % 2)], start=True, stop=True).then_inc(sum_ready.sem, 1)

        @block.scalar
        def _(act):
            for n in range(8):
                i, half = n // 2, n % 2
                act.wait_ge(product_ready.sem, product_ready.nth(n + 1))
                if i < 3:
                    act.activation(raw[:, i, 2 * half:2 * half + 2, 3:], ps[:, n % 2, :].rearrange("p (b t) -> p b t", t=T),
                                   ACT.Copy).then_inc(product_taken.sem, 1)
                else:
                    act.activation(beta[:, cols(half)], ps[:, n % 2, :], ACT.Sigmoid).then_inc(product_taken.sem, 1)
            for i in range(3):
                act.wait_ge(conv_ready.sem, conv_ready.nth(i + 1))
                act.activation(raw[:, i, :, 3:], conv[:, i, :, :], ACT.Sigmoid).then_inc(silu_ready.sem, 1)
            for i in range(2):
                act.wait_ge(sum_taken.sem, sum_taken.nth(i + 1))
                act.activation(sq[:, i, :], sq[:, i, :], ACT.Sqrt).then_inc(root_ready.sem, 1)

        @block.vector
        def _(dve):
            dve.memset(raw[:, :, :, 0:3], 0.0)
            dve.memset(vT[:, :, 0:FIR_PAD], 0.0)
            dve.wait_ge(w_in.sem, w_in.nth(48))
            for i in range(3):
                dve.wait_ge(product_taken.sem, product_taken.nth(2 * i + 2))
                for j in range(4):
                    tap = taps[:, 4 * i + j:4 * i + j + 1]
                    if j == 0:
                        dve.drain()
                        dve.tensor_scalar(conv[:, i, :, :], raw[:, i, :, 0:T], tap, None, ALU.mult)
                    else:
                        dve.drain()
                        ins = dve.scalar_tensor_tensor(out=conv[:, i, :, :], in0=raw[:, i, :, j:j + T], scalar=tap,
                                                       in1=conv[:, i, :, :], op0=ALU.mult, op1=ALU.add)
                ins.then_inc(conv_ready.sem, 1)
            for i, v in enumerate((qT, kT)):
                dve.wait_ge(silu_ready.sem, silu_ready.nth(i + 1))
                dve.tensor_tensor(v[:, :].rearrange("p (b t) -> p b t", t=T), conv[:, i, :, :], raw[:, i, :, 3:], ALU.mult)
                dve.drain()
                dve.tensor_tensor(sq[:, i, :], v[:, :], v[:, :], ALU.mult).then_inc(sq_ready.sem, 1)
            dve.wait_ge(product_taken.sem, product_taken.nth(8))
            dve.wait_ge(silu_ready.sem, silu_ready.nth(3))
            dve.tensor_tensor(vT[:, :, FIR_PAD:], conv[:, 2, :, :], raw[:, 2, :, 3:], ALU.mult)
            dve.drain()
            dve.tensor_tensor(vbT[:, :].rearrange("p (b t) -> p b t", t=T), vT[:, :, FIR_PAD:],
                              beta[:, :].rearrange("p (b t) -> p b t", t=T), ALU.mult)
            for i in range(2):
                dve.wait_ge(sum_ready.sem, sum_ready.nth(2 * i + 2))
                dve.tensor_scalar(sq[:, i, :], ps_n[:, 2 * i:2 * i + 2, :].rearrange("p h c -> p (h c)"), 1e-6, None, ALU.add)\
                   .then_inc(sum_taken.sem, 1)
            for i, v in enumerate((qT, kT)):
                dve.wait_ge(root_ready.sem, root_ready.nth(i + 1))
                dve.reciprocal(sq[:, i, :], sq[:, i, :])
                dve.drain()
                dve.tensor_tensor(v[:, :], v[:, :], sq[:, i, :], ALU.mult)
            dve.drain()
            dve.tensor_tensor(kbT[:, :], kT[:, :], beta[:, :], ALU.mult)


def delta_chunks(m, qT, kT, kbT, vbT, u, k, wT, attnT):
    nc = m.nc
    H = 4
    LEVELS = 5
    STEPS = 3 * (LEVELS - 1) - 1
    with ExitStack() as ctx:
        place = Place(nc, ctx, "tiles")
        below = place.sbuf("below", [P, 2 * LEVELS, P])
        causal = place.sbuf("causal", [P, P])
        now = place.sbuf("now", [P, 4, P])
        rows = place.sbuf("rows", [P, 3, P])
        A_t = place.sbuf("A_t", [P, LEVELS, H, P])
        T_ = place.sbuf("T_", [P, H, P])
        Tt = place.sbuf("Tt", [P, H, P])
        AT = place.sbuf("AT", [P, H, P])
        ps_a = place.psum("ps_a", [P, H, BANK])
        ps_r = place.psum("ps_r", [P, BANK])
        ps_1 = place.psum("ps_1", [P, BANK])
        ps_2 = place.psum("ps_2", [P, BANK])
        ps_3 = place.psum("ps_3", [P, BANK])
        ps_u = ps_2[:, 0:2 * P].rearrange("p (i c) -> p i c", c=P)
        const_in = place.counter("const_in")
        now_ready = place.counter("now_ready", per=1)
        grams_ready = place.counter("grams_ready", per=3)
        rows_turned = place.counter("rows_turned", per=1)
        rows_ready = place.counter("rows_ready", per=1)
        first_ready = place.counter("first_ready", per=1)
        AT_made = place.counter("AT_made", per=LEVELS - 1)
        AT_ready = place.counter("AT_ready", per=LEVELS - 1)
        joined = place.counter("joined", per=LEVELS - 1)
        T_ready = place.counter("T_ready", per=LEVELS - 1)
        uw_made = place.counter("uw_made", per=1, ahead=1)
        uw_taken = place.counter("uw_taken", per=1, ahead=1)
        block = ctx.enter_context(nc.Block())

        def head(ps, h):
            return ps[:, h * P:(h + 1) * P]

        def heads(ps):
            return ps[:, :].rearrange("p (h c) -> p h c", c=P)

        def spread(mask):
            return mask.rearrange("p (o c) -> p o c", o=1).broadcast_to([P, H, P])

        @block.sync
        def _(sp):
            sp.dma_start(below[:, :, :], m.dram["c_below"]).then_inc(const_in.sem, 16)
            sp.dma_start(causal[:, :], m.dram["c_causal32"]).then_inc(const_in.sem, 16)

        @block.scalar
        def _(act):
            with act.Fori(0, NT) as t:
                act.wait_ge(uw_made.sem, uw_made.nth(0, t))
                for i, v in enumerate((qT, kT, kbT, vbT)):
                    ins = act.activation(now[:, i, :], v[:, bass.ds(t * P, P)], ACT.Copy)
                ins.then_inc(now_ready.sem, 1)
                act.wait_ge(rows_turned.sem, rows_turned.nth(1, t))
                act.activation(k[:, bass.ds(t, 1), :].rearrange("p o c -> p (o c)"), ps_r[:, 0:P], ACT.Copy)
                act.activation(rows[:, 1:3, :], ps_r[:, P:3 * P].rearrange("p (i c) -> p i c", c=P), ACT.Copy)\
                   .then_inc(rows_ready.sem, 1)

        @block.tensor
        def _(pe):
            with pe.Fori(0, NT) as t:
                pe.wait_ge(now_ready.sem, now_ready.nth(1, t))
                for i, (a, b) in enumerate(((1, 2), (2, 1), (1, 0))):
                    for h in range(H):
                        part = slice(32 * h, 32 * (h + 1))
                        mm = pe.matmul(ps_a[:, h, i * P:(i + 1) * P], now[part, a, :], now[part, b, :], start=True, stop=True)
                    mm.then_inc(grams_ready.sem, 1)
                for i in range(3):
                    mm = pe.transpose(ps_r[:, i * P:(i + 1) * P], now[:, i + 1, :], m.ident[:, :])
                mm.then_inc(rows_turned.sem, 1)
                for s in range(1, LEVELS):
                    if s == 1:
                        pe.wait_ge(first_ready.sem, first_ready.nth(1, t))
                    else:
                        pe.wait_ge(T_ready.sem, T_ready.nth(s - 1, t))
                    for h in range(H):
                        mm = pe.matmul(head(ps_1, h), A_t[:, s, h, :], T_[:, h, :], start=True, stop=True)
                    mm.then_inc(AT_made.sem, 1)
                    pe.wait_ge(AT_ready.sem, AT_ready.nth(s, t))
                    for h in range(H):
                        mm = pe.matmul(head(ps_3, h), AT[:, h, :], Tt[:, h, :], start=True, stop=True)
                    if s < LEVELS - 1:
                        for h in range(H):
                            mm = pe.matmul(head(ps_2, h), Tt[:, h, :], AT[:, h, :], start=True, stop=True)
                    mm.then_inc(joined.sem, 1)
                pe.wait_ge(T_ready.sem, T_ready.nth(LEVELS - 1, t))
                pe.wait_ge(rows_ready.sem, rows_ready.nth(1, t))
                pe.wait_ge(uw_taken.sem, uw_taken.nth(0, t))
                for h in range(H):
                    ch = slice(32 * h, 32 * (h + 1))
                    pe.matmul(ps_u[:, 0, ch], Tt[:, h, :], rows[:, 2, ch], start=True, stop=True)
                    mm = pe.matmul(ps_u[ch, 1, :], rows[:, 1, ch], Tt[:, h, :], start=True, stop=True)
                mm.then_inc(uw_made.sem, 1)

        @block.vector
        def _(dve):
            dve.sem_inc(uw_taken.sem, uw_taken.ahead)
            dve.sem_inc(uw_made.sem, uw_made.ahead)
            dve.wait_ge(const_in.sem, const_in.nth(32))
            with dve.Fori(0, NT) as t:
                dve.wait_ge(grams_ready.sem, grams_ready.nth(3, t))
                for i in range(3):
                    if i == 0:
                        for s in range(LEVELS):
                            ins = dve.tensor_tensor(A_t[:, s, :, :], ps_a[:, :, 0:P], spread(below[:, 2 * s + 1, :]), ALU.mult)
                        dve.drain()
                        dve.tensor_tensor(Tt[:, :, :], A_t[:, 0, :, :], spread(m.ident[:, :]), ALU.add)
                    elif i == 1:
                        dve.tensor_tensor(T_[:, :, :], ps_a[:, :, P:2 * P], spread(below[:, 0, :]), ALU.mult)
                        dve.drain()
                        dve.tensor_tensor(T_[:, :, :], T_[:, :, :], spread(m.ident[:, :]), ALU.add).then_inc(first_ready.sem, 1)
                    else:
                        dve.tensor_tensor(attnT[:, bass.ds(t, 1), :, :].rearrange("p o h c -> p (o h) c"), ps_a[:, :, 2 * P:3 * P],
                                          spread(causal[:, :]), ALU.mult)
                for s in range(1, LEVELS):
                    dve.wait_ge(AT_made.sem, AT_made.nth(s, t))
                    dve.tensor_copy(AT[:, :, :], heads(ps_1)).then_inc(AT_ready.sem, 1)
                    dve.wait_ge(joined.sem, joined.nth(s, t))
                    if s < LEVELS - 1:
                        dve.tensor_tensor(T_[:, :, :], T_[:, :, :], heads(ps_2), ALU.add)
                    dve.tensor_tensor(Tt[:, :, :], Tt[:, :, :], heads(ps_3), ALU.add).then_inc(T_ready.sem, 1)
                dve.wait_ge(uw_made.sem, uw_made.nth(1, t))
                dve.tensor_copy(u[:, bass.ds(t, 1), :].rearrange("p o c -> p (o c)"), ps_u[:, 0, :])
                dve.tensor_copy(wT[:, bass.ds(t * P, P)], ps_u[:, 1, :]).then_inc(uw_taken.sem, 1)


def delta_scan(m, qT, k, u, wT, attnT, delta):
    nc = m.nc
    C = T // 32
    with ExitStack() as ctx:
        place = Place(nc, ctx, "scan")
        same = place.sbuf("same", [P, P])
        state = place.sbuf("state", [P, B, P])
        grown = place.sbuf("grown", [P, B, P])
        ps_w = place.psum("ps_w", [P, BANK])
        ps_o = place.psum("ps_o", [P, BANK])
        ps_s = place.psum("ps_s", [P, BANK])
        same_in = place.counter("same_in")
        state_ready = place.counter("state_ready")
        w_made = place.counter("w_made")
        u_ready = place.counter("u_ready")
        o_made = place.counter("o_made")
        o_taken = place.counter("o_taken")
        s_made = place.counter("s_made")
        block = ctx.enter_context(nc.Block())

        @block.sync
        def _(sp):
            sp.dma_start(same[:, :], m.dram["c_same_head32"]).then_inc(same_in.sem, 16)

        @block.tensor
        def _(pe):
            for c in range(C):
                t, r = c // 4, slice(32 * (c % 4), 32 * (c % 4 + 1))
                pe.wait_ge(state_ready.sem, state_ready.nth(c + 1))
                for b in range(B):
                    tok = slice(b * T + 32 * c, b * T + 32 * (c + 1))
                    mm = pe.matmul(ps_w[r, b * P:(b + 1) * P], wT[:, tok], state[:, b, :], start=True, stop=True)
                mm.then_inc(w_made.sem, 1)
                pe.wait_ge(u_ready.sem, u_ready.nth(c + 1))
                for b in range(B):
                    mm = pe.matmul(ps_s[:, b * P:(b + 1) * P], k[r, b * TB + t, :], u[r, b * TB + t, :], start=True, stop=True,
                                   tile_position=(r.start, 0))
                mm.then_inc(s_made.sem, 1)
                if c >= 1:
                    pe.wait_ge(o_taken.sem, o_taken.nth(c))
                for b in range(B):
                    tok = slice(b * T + 32 * c, b * T + 32 * (c + 1))
                    pe.matmul(ps_o[r, b * P:(b + 1) * P], qT[:, tok], state[:, b, :], start=True, stop=False, skip_group_check=True)
                    for h in range(4):
                        ch = slice(32 * h, 32 * (h + 1))
                        mm = pe.matmul(ps_o[r, b * P + 32 * h:b * P + 32 * (h + 1)], attnT[r, b * TB + t, h, r],
                                       u[r, b * TB + t, ch], start=False, stop=(h == 3), skip_group_check=True,
                                       tile_position=(r.start, r.start))
                mm.then_inc(o_made.sem, 1)

        @block.vector
        def _(dve):
            dve.memset(state[:, :, :], 0.0).then_inc(state_ready.sem, 1)
            dve.wait_ge(same_in.sem, same_in.nth(16))
            for c in range(C):
                t, r = c // 4, slice(32 * (c % 4), 32 * (c % 4 + 1))
                dve.wait_ge(w_made.sem, w_made.nth(c + 1))
                here = u[:, :, :].rearrange("p (b u) d -> p b u d", u=TB)[r, :, t, :]
                dve.tensor_tensor(here, here, ps_w[r, :].rearrange("p (b d) -> p b d", d=P), ALU.subtract).then_inc(u_ready.sem, 1)
                dve.wait_ge(s_made.sem, s_made.nth(c + 1))
                dve.tensor_tensor(grown[:, :, :], ps_s[:, :].rearrange("p (b d) -> p b d", d=P),
                                  same[:, :].rearrange("p (o d) -> p o d", o=1).broadcast_to([P, B, P]), ALU.mult)
                dve.drain()
                dve.wait_ge(o_made.sem, o_made.nth(c + 1))
                dve.tensor_tensor(state[:, :, :], state[:, :, :], grown[:, :, :], ALU.add).then_inc(state_ready.sem, 1)

        @block.scalar
        def _(act):
            for c in range(C):
                t, r = c // 4, slice(32 * (c % 4), 32 * (c % 4 + 1))
                act.wait_ge(o_made.sem, o_made.nth(c + 1))
                act.activation(delta[:, :, :].rearrange("p (b u) d -> p b u d", u=TB)[r, :, t, :],
                               ps_o[r, :].rearrange("p (b d) -> p b d", d=P), ACT.Copy).then_inc(o_taken.sem, 1)


def delta_mix(m, vT, taps, delta):
    nc = m.nc
    H = 4
    FIRS = ((12, 3), (15, 15), (30, 63))
    with ExitStack() as ctx:
        place = Place(nc, ctx, "mix")
        gate_w = place.sbuf("gate_w", [P, 20])
        row = place.sbuf("row", [P, 20 + 4 + 4 + 32])
        Wo = place.sbuf("Wo", [P, D])
        fir = place.sbuf("fir", [P, 3, B, T])
        local = place.sbuf("local", [P, 2, NT, D])
        gates = place.sbuf("gates", [P, NT, H, 5])
        stat = place.sbuf("stat", [P, NT, H])
        keep = place.sbuf("keep", [P, H])
        total = place.sbuf("total", [P, NT, D])
        oT = place.sbuf("oT", [P, B * T])
        ps_g = place.psum("ps_g", [P, BANK])
        ps_t = place.psum("ps_t", [P, 2, BANK])
        ps_y = place.psum("ps_y", [P, 2, BANK])
        small_in = place.counter("small_in")
        gate_made = place.counter("gate_made")
        temp_ready = place.counter("temp_ready")
        shifted = place.counter("shifted")
        exp_ready = place.counter("exp_ready")
        fir_ready = place.counter("fir_ready")
        turned = place.counter("turned")
        local_ready = place.counter("local_ready")
        local_used = place.counter("local_used")
        mean_ready = place.counter("mean_ready")
        root_ready = place.counter("root_ready")
        normed = place.counter("normed")
        o_turned = place.counter("o_turned")
        oT_ready = place.counter("oT_ready")
        y_ready = place.counter("y_ready")
        block = ctx.enter_context(nc.Block())
        rows = lambda v: v.rearrange("p t (h c) -> p (t h) c", c=32)

        @block.sync
        def _(sp):
            sp.dma_start(gate_w[:, :], m.dram["L0_attn_gate"]).then_inc(small_in.sem, 16)
            sp.dma_start(row[:, :], m.dram["L0_attn_row"].broadcast_to([P, 60])).then_inc(small_in.sem, 16)
            sp.dma_start(Wo[:, :], m.dram["L0_attn_WoT"]).then_inc(small_in.sem, 16)

        @block.tensor
        def _(pe):
            pe.wait_ge(small_in.sem, small_in.nth(48))
            for t in range(NT):
                mm = pe.matmul(ps_g[:, t * 20:(t + 1) * 20], m.XT[:, t * P:(t + 1) * P], gate_w[:, :], start=True, stop=True)
            mm.then_inc(gate_made.sem, 1)
            for n in range(8):
                i, half = n // 2, n % 2
                if i >= 1:
                    pe.wait_ge(fir_ready.sem, fir_ready.nth(i))
                if n >= 2:
                    pe.wait_ge(local_ready.sem, local_ready.nth(n - 1))
                for t in range(4 * half, 4 * half + 4):
                    b, at = t // TB, t % TB * P
                    src = vT[:, b, FIR_PAD + at:FIR_PAD + at + P] if i == 0 else fir[:, i - 1, b, at:at + P]
                    mm = pe.transpose(ps_t[:, n % 2, (t % 4) * P:(t % 4 + 1) * P], src, m.ident[:, :])
                mm.then_inc(turned.sem, 1)
            for half in range(2):
                pe.wait_ge(normed.sem, normed.nth(1))
                if half == 0:
                    pe.wait_ge(local_ready.sem, local_ready.nth(8))
                for t in range(4 * half, 4 * half + 4):
                    mm = pe.transpose(ps_t[:, half, (t % 4) * P:(t % 4 + 1) * P], total[:, t, :], m.ident[:, :])
                mm.then_inc(o_turned.sem, 1)
            for t in range(NT):
                pe.wait_ge(oT_ready.sem, oT_ready.nth(t // 4 + 1))
                mm = pe.matmul(ps_y[:, t // 4, (t % 4) * P:(t % 4 + 1) * P], oT[:, t * P:(t + 1) * P], Wo[:, :], start=True, stop=True)
            mm.then_inc(y_ready.sem, 1)

        @block.scalar
        def _(act):
            act.wait_ge(small_in.sem, small_in.nth(48))
            act.activation(row[:, 20:24], row[:, 20:24], ACT.Exp, scale=-1.0).then_inc(temp_ready.sem, 1)
            act.wait_ge(shifted.sem, shifted.nth(1))
            act.activation(gates[:, :, :, :], gates[:, :, :, :], ACT.Exp).then_inc(exp_ready.sem, 1)
            for n in range(8):
                i, half = n // 2, n % 2
                act.wait_ge(turned.sem, turned.nth(n + 1))
                if i >= 2:
                    act.wait_ge(local_used.sem, local_used.nth(i - 1))
                act.activation(local[:, i % 2, 4 * half:4 * half + 4, :], ps_t[:, n % 2, :].rearrange("p (t d) -> p t d", d=D), ACT.Copy)\
                   .then_inc(local_ready.sem, 1)
            act.wait_ge(mean_ready.sem, mean_ready.nth(1))
            act.activation(stat[:, :, :], stat[:, :, :], ACT.Sqrt).then_inc(root_ready.sem, 1)
            for half in range(2):
                act.wait_ge(o_turned.sem, o_turned.nth(half + 1))
                act.activation(oT[:, half * BANK:(half + 1) * BANK], ps_t[:, half, :], ACT.Copy).then_inc(oT_ready.sem, 1)

        @block.vector
        def _(dve):
            def over(v, n):
                return v.rearrange("p t (h o) -> p (t h) o", o=1).broadcast_to([P, NT * H, n])

            dve.wait_ge(small_in.sem, small_in.nth(48))
            dve.wait_ge(gate_made.sem, gate_made.nth(1))
            b20 = row[:, 0:20].rearrange("p (o h) -> p o h", o=1).broadcast_to([P, NT, 20])
            flat = gates[:, :, :, :].rearrange("p t h g -> p (t h) g")
            dve.tensor_tensor(gates[:, :, :, :].rearrange("p t h g -> p t (h g)"), ps_g[:, 0:160].rearrange("p (t g) -> p t g", g=20),
                              b20, ALU.add)
            dve.wait_ge(temp_ready.sem, temp_ready.nth(1))
            dve.drain()
            for h in range(H):
                dve.tensor_scalar(gates[:, :, h, :], gates[:, :, h, :], row[:, 20 + h:21 + h], None, ALU.mult)
            dve.drain()
            dve.tensor_reduce(stat[:, :, :].rearrange("p t h -> p (t h)"), flat, AX.X, ALU.max)
            dve.drain()
            dve.tensor_tensor(flat, flat, over(stat[:, :, :], 5), ALU.subtract).then_inc(shifted.sem, 1)
            dve.tensor_scalar(row[:, 24:28], row[:, 24:28], 0.0, 0.2, ALU.max, ALU.min)
            dve.drain()
            dve.tensor_scalar(keep[:, :], row[:, 24:28], -5.0, 1.0, ALU.mult, ALU.add)
            dve.wait_ge(exp_ready.sem, exp_ready.nth(1))
            dve.tensor_reduce(stat[:, :, :].rearrange("p t h -> p (t h)"), flat, AX.X, ALU.add)
            dve.drain()
            dve.reciprocal(stat[:, :, :], stat[:, :, :])
            dve.drain()
            dve.tensor_tensor(flat, flat, over(stat[:, :, :], 5), ALU.mult)
            dve.drain()
            for h in range(H):
                dve.tensor_scalar(gates[:, :, h, :], gates[:, :, h, :], keep[:, h:h + 1], row[:, 24 + h:25 + h], ALU.mult, ALU.add)
            for i, (first, n) in enumerate(FIRS):
                for j in range(n):
                    tap = taps[:, first + j:first + j + 1]
                    src = vT[:, :, FIR_PAD - (n - 1) + j:FIR_PAD - (n - 1) + j + T]
                    if j == 0:
                        ins = dve.tensor_scalar(fir[:, i, :, :], src, tap, None, ALU.mult)
                    else:
                        ins = dve.scalar_tensor_tensor(out=fir[:, i, :, :], in0=src, scalar=tap, in1=fir[:, i, :, :],
                                                       op0=ALU.mult, op1=ALU.add)
                    if j < n - 1:
                        dve.drain()
                ins.then_inc(fir_ready.sem, 1)

            def gate(p):
                return gates[:, :, :, p:p + 1].rearrange("p t h o -> p (t h) o").broadcast_to([P, NT * H, 32])

            dve.tensor_tensor(rows(total[:, :, :]), rows(delta[:, :, :]), gate(3), ALU.mult)
            for i, p in enumerate((4, 0, 1, 2)):
                dve.wait_ge(local_ready.sem, local_ready.nth(2 * i + 2))
                dve.tensor_tensor(rows(local[:, i % 2, :, :]), rows(local[:, i % 2, :, :]), gate(p), ALU.mult)
                dve.drain()
                dve.tensor_tensor(total[:, :, :], total[:, :, :], local[:, i % 2, :, :], ALU.add).then_inc(local_used.sem, 1)
            dve.drain()
            dve.tensor_tensor(local[:, 0, :, :], total[:, :, :], total[:, :, :], ALU.mult)
            dve.drain()
            dve.tensor_reduce(stat[:, :, :].rearrange("p t h -> p (t h)"), rows(local[:, 0, :, :]), AX.X, ALU.add)
            dve.drain()
            dve.tensor_scalar(stat[:, :, :], stat[:, :, :], 1.0 / 32, 1e-5, ALU.mult, ALU.add).then_inc(mean_ready.sem, 1)
            dve.wait_ge(root_ready.sem, root_ready.nth(1))
            dve.reciprocal(stat[:, :, :], stat[:, :, :])
            dve.drain()
            dve.tensor_tensor(rows(total[:, :, :]), rows(total[:, :, :]), over(stat[:, :, :], 32), ALU.mult)
            dve.drain()
            w32 = row[:, 28:60].rearrange("p (o c) -> p o c", o=1).broadcast_to([P, NT * H, 32])
            dve.tensor_tensor(rows(total[:, :, :]), rows(total[:, :, :]), w32, ALU.mult).then_inc(normed.sem, 1)
            dve.wait_ge(y_ready.sem, y_ready.nth(1))
            dve.tensor_copy(m.Y[:, :, :], ps_y[:, :, :].rearrange("p h (t d) -> p (h t) d", d=D))


def bidaf(m):
    nc = m.nc
    with ExitStack() as outer:
        keep = Place(nc, outer, "bidaf")
        c2qT = keep.sbuf("c2qT", [P, B * T])
        neg_max = keep.sbuf("neg_max", [P, NT])
        attention(m, Heads("L0_xattn", S, 1, P, D, biased=True, context=True, n_heads=1), m.XT, c2qT, neg_max_out=neg_max)

        with ExitStack() as ctx:
            place = Place(nc, ctx, "join")
            w_c = place.sbuf("w_c", [P, 1])
            b3 = place.sbuf("b3", [P, 3])
            bias = place.sbuf("bias", [P, 1])
            W_l = place.sbuf("W_l", [P, 4, D])
            b_l = place.sbuf("b_l", [1, D])
            best = place.sbuf("best", [P, NT])
            row = place.sbuf("row", [1, B, T])
            stat = place.sbuf("stat", [1, B])
            weighted = place.sbuf("weighted", [P, B, T])
            q2c = place.sbuf("q2c", [P, B])
            prodT = place.sbuf("prodT", [P, B * T])
            c_q2cT = place.sbuf("c_q2cT", [P, B * T])
            ps_c = place.psum("ps_c", [P, BANK])
            ps_row = place.psum("ps_row", [P, 2, BANK])
            ps_b = place.psum("ps_b", [P, 2, BANK])
            ps_y = place.psum("ps_y", [P, 2, BANK])
            small_in = place.counter("small_in")
            self_ready = place.counter("self_ready")
            best_ready = place.counter("best_ready")
            row_ready = place.counter("row_ready")
            shifted = place.counter("shifted")
            exp_ready = place.counter("exp_ready")
            att_ready = place.counter("att_ready")
            spread = place.counter("spread")
            features_ready = place.counter("features_ready")
            y_ready = place.counter("y_ready")
            block = ctx.enter_context(nc.Block())

            @block.sync
            def _(sp):
                for tile, source in [(w_c[:, :], m.dram["L0_xattn_w_c"].rearrange("(p o) -> p o", o=1)),
                                     (b3[:, :], m.dram["L0_xattn_b"].broadcast_to([P, 3])),
                                     (W_l[:, :, :], m.dram["L0_xattn_W_l"]),
                                     (b_l[:, :], m.dram["L0_xattn_b_l"].rearrange("(o d) -> o d", o=1))]:
                    sp.dma_start(tile, source).then_inc(small_in.sem, 16)

            @block.tensor
            def _(pe):
                pe.wait_ge(small_in.sem, small_in.nth(64))
                for t in range(NT):
                    mm = pe.matmul(ps_c[:, t:t + 1], m.XT[:, t * P:(t + 1) * P], w_c[:, :], start=True, stop=True)
                mm.then_inc(self_ready.sem, 1)
                pe.wait_ge(best_ready.sem, best_ready.nth(1))
                for t in range(NT):
                    mm = pe.transpose(ps_row[0:1, t // 4, (t % 4) * P:(t % 4 + 1) * P], best[:, t:t + 1], m.ident[:, :])
                mm.then_inc(row_ready.sem, 1)
                pe.wait_ge(att_ready.sem, att_ready.nth(1))
                for half in range(2):
                    mm = pe.matmul(ps_b[:, half, :], m.ones[0:1, :], row[:, 2 * half:2 * half + 2, :].rearrange("o b t -> o (b t)"),
                                   start=True, stop=True)
                mm.then_inc(spread.sem, 1)
                pe.wait_ge(features_ready.sem, features_ready.nth(1))
                for t in range(NT):
                    tok = slice(t * P, (t + 1) * P)
                    out = ps_y[:, t // 4, (t % 4) * P:(t % 4 + 1) * P]
                    for k, feature in enumerate((m.XT, c2qT, prodT, c_q2cT)):
                        pe.matmul(out, feature[:, tok], W_l[:, k, :], start=(k == 0), stop=False)
                    mm = pe.matmul(out, m.ones[0:1, :], b_l[:, :], start=False, stop=True)
                mm.then_inc(y_ready.sem, 1)

            @block.scalar
            def _(act):
                act.wait_ge(shifted.sem, shifted.nth(1))
                act.activation(row[:, :, :], row[:, :, :], ACT.Exp).then_inc(exp_ready.sem, 1)

            @block.vector
            def _(dve):
                dve.wait_ge(small_in.sem, small_in.nth(64))
                dve.tensor_reduce(bias[:, :], b3[:, :], AX.X, ALU.add)
                dve.drain()
                dve.wait_ge(self_ready.sem, self_ready.nth(1))
                dve.scalar_tensor_tensor(out=best[:, :], in0=ps_c[:, 0:NT], scalar=bias[:, 0:1], in1=neg_max[:, :],
                                         op0=ALU.add, op1=ALU.subtract).then_inc(best_ready.sem, 1)
                dve.tensor_tensor(prodT[:, :], m.XT[:, :], c2qT[:, :], ALU.mult)
                dve.wait_ge(row_ready.sem, row_ready.nth(1))
                dve.tensor_copy(row[:, :, :], ps_row[0:1, :, :].rearrange("o h (b t) -> o (h b) t", b=2))
                dve.drain()
                dve.tensor_reduce(stat[:, :], row[:, :, :], AX.X, ALU.max)
                dve.drain()
                for b in range(B):
                    ins = dve.tensor_scalar(row[:, b, :], row[:, b, :], stat[:, b:b + 1], None, ALU.subtract)
                ins.then_inc(shifted.sem, 1)
                dve.wait_ge(exp_ready.sem, exp_ready.nth(1))
                dve.tensor_reduce(stat[:, :], row[:, :, :], AX.X, ALU.add)
                dve.drain()
                dve.reciprocal(stat[:, :], stat[:, :])
                dve.drain()
                for b in range(B):
                    ins = dve.tensor_scalar(row[:, b, :], row[:, b, :], stat[:, b:b + 1], None, ALU.mult)
                ins.then_inc(att_ready.sem, 1)
                dve.wait_ge(spread.sem, spread.nth(1))
                for half in range(2):
                    dve.tensor_tensor(weighted[:, 2 * half:2 * half + 2, :].rearrange("p b t -> p (b t)"), ps_b[:, half, :],
                                      m.XT[:, half * BANK:(half + 1) * BANK], ALU.mult)
                dve.drain()
                dve.tensor_reduce(q2c[:, :], weighted[:, :, :], AX.X, ALU.add)
                dve.drain()
                for b in range(B):
                    tok = slice(b * T, (b + 1) * T)
                    ins = dve.tensor_scalar(c_q2cT[:, tok], m.XT[:, tok], q2c[:, b:b + 1], None, ALU.mult)
                ins.then_inc(features_ready.sem, 1)
                dve.wait_ge(y_ready.sem, y_ready.nth(1))
                dve.tensor_copy(m.Y[:, :, :], ps_y[:, :, :].rearrange("p h (t d) -> p (h t) d", d=D))


def moe(m, name, E, normed):
    nc = m.nc
    F = 512
    FC = F // P
    HALVES = B * T // BANK
    U = FC * HALVES
    EB = 2
    N = U * EB
    RING = 4
    gates_dram = nc.dram_tensor(f"gates_{name}", (E, B * T), F32, kind="Internal").ap()
    w1_dram, w2_dram, b1_dram = (m.dram[f"{name}_{w}"] for w in (("W1", "W2", "b1") if normed else ("w1", "w2", "b1")))

    with ExitStack() as ctx:
        place = Place(nc, ctx, "moe")
        xn = place.sbuf("xn", [P, NT, D]) if normed else None
        xnT = place.sbuf("xnT", [P, B * T]) if normed else m.XT
        affine = place.sbuf("affine", [P, 2])
        stats = place.sbuf("stats", [P, NT, 6])
        mv = place.sbuf("mv", [P, NT, 2])
        rstd = place.sbuf("rstd", [P, NT])
        wg = place.sbuf("wg", [P, E])
        bg = place.sbuf("bg", [1, E])
        b2 = place.sbuf("b2", [E, D])
        number = place.sbuf("number", [P, E])
        scores = place.sbuf("scores", [P, NT, E])
        z = place.sbuf("z", [P, NT])
        top = place.sbuf("top", [P, NT, 8])
        at = place.sbuf("at", [P, NT, 8], U32)
        atf = place.sbuf("atf", [P, NT, 8])
        gate = place.sbuf("gate", [P, NT, 2])
        first = place.sbuf("first", [P, NT, E])
        second = place.sbuf("second", [P, NT, E])
        gT = place.sbuf("gT", [E, B * T])
        w1 = place.sbuf("w1", [P, EB, F])
        w2 = place.sbuf("w2", [P, EB, FC, D])
        b1 = place.sbuf("b1", [P, EB, FC])
        G = place.sbuf("G", [P, EB, B * T])
        h = place.sbuf("h", [P, RING, BANK])
        hg = place.sbuf("hg", [P, RING, BANK])
        yT = place.sbuf("yT", [P, B * T])
        ps_h = place.psum("ps_h", [P, RING, BANK])
        ps_y = place.psum("ps_y", [P, HALVES, BANK])
        ps_t = place.psum("ps_t", [P, 2, BANK])

        small_in = place.counter("small_in")
        var_ready = place.counter("var_ready")
        root_ready = place.counter("root_ready")
        xn_ready = place.counter("xn_ready")
        xn_turned = place.counter("xn_turned")
        xnT_ready = place.counter("xnT_ready")
        scores_ready = place.counter("scores_ready")
        exp_in = place.counter("exp_in")
        exp_out = place.counter("exp_out")
        gates_ready = place.counter("gates_ready")
        gates_turned = place.counter("gates_turned")
        gT_ready = place.counter("gT_ready")
        gates_stored = place.counter("gates_stored")
        expert_in = [place.counter(f"expert_in_{k}", per=64) for k in range(EB)]
        h_ready = place.counter("h_ready", per=N)
        gelu_ready = place.counter("gelu_ready", per=N)
        gated = place.counter("gated", per=N, ahead=RING)
        y_added = place.counter("y_added", per=N, ahead=EB * U)
        y_ready = place.counter("y_ready")
        yT_ready = place.counter("yT_ready")
        y_turned = place.counter("y_turned")
        block = ctx.enter_context(nc.Block())

        @block.sync
        def _(sp):
            for tile, source in ([(affine[:, 0:1], m.dram[name + "_gamma"].rearrange("(p o) -> p o", o=1)),
                                  (affine[:, 1:2], m.dram[name + "_beta"].rearrange("(p o) -> p o", o=1))] if normed else []) + [
                    (wg[:, :], m.dram[name + ("_Wg" if normed else "_gate_w")]),
                    (bg[:, :], m.dram[name + ("_bg" if normed else "_gate_b")].rearrange("(o e) -> o e", o=1)),
                    (b2[:, :], m.dram[name + "_b2"]),
                    (number[:, :], m.dram["c_number"][:, 0:E])]:
                sp.dma_start(tile, source).then_inc(small_in.sem, 16)
            sp.wait_ge(gT_ready.sem, gT_ready.nth(1))
            sp.dma_start(gates_dram, gT[:, :]).then_inc(gates_stored.sem, 16)
            sp.wait_ge(gates_stored.sem, gates_stored.nth(16))
            with sp.Fori(0, E // EB) as it:
                for k in range(EB):
                    e = it * EB + k
                    sp.wait_ge(y_added.sem, y_added.nth((k + 1 - EB) * U, it))
                    sp.dma_start(w1[:, k, :], w1_dram[bass.ds(e, 1), :, :].rearrange("e d f -> (e d) f")).then_inc(expert_in[k].sem, 16)
                    sp.dma_start(w2[:, k, :, :], w2_dram[bass.ds(e, 1), :, :].rearrange("e (c p) d -> p (e c) d", p=P)).then_inc(expert_in[k].sem, 16)
                    sp.dma_start(b1[:, k, :], b1_dram[bass.ds(e, 1), :, :].rearrange("e p c -> (e p) c")).then_inc(expert_in[k].sem, 16)
                    sp.dma_start(G[:, k, :], gates_dram[bass.ds(e, 1), :].broadcast_to([P, B * T])).then_inc(expert_in[k].sem, 16)

        @block.vector
        def _(dve):
            dve.sem_inc(gated.sem, gated.ahead)
            if normed:
                for t in range(NT):
                    dve.bn_stats(stats[:, t, :], m.X[:, t, :])
                dve.drain()
                for t in range(NT):
                    dve.bn_aggr(mv[:, t, :], stats[:, t, :])
                dve.drain()
                dve.tensor_scalar(rstd[:, :], mv[:, :, 1], 1e-5, None, ALU.add).then_inc(var_ready.sem, 1)
                dve.wait_ge(root_ready.sem, root_ready.nth(1))
                dve.reciprocal(rstd[:, :], rstd[:, :])
                dve.drain()
                for t in range(NT):
                    dve.tensor_scalar(xn[:, t, :], m.X[:, t, :], mv[:, t, 0:1], rstd[:, t:t + 1],
                                      ALU.subtract, ALU.mult).then_inc(xn_ready.sem, 1)
                dve.wait_ge(small_in.sem, small_in.nth(16 * 6))
                for half in range(HALVES):
                    dve.wait_ge(xn_turned.sem, xn_turned.nth(half + 1))
                    dve.tensor_scalar(xnT[:, half * BANK:(half + 1) * BANK], ps_t[:, half, :], affine[:, 0:1], affine[:, 1:2],
                                      ALU.mult, ALU.add).then_inc(xnT_ready.sem, 1)
            dve.wait_ge(scores_ready.sem, scores_ready.nth(1))
            dve.tensor_copy(scores[:, :, :], ps_h[:, 0, 0:NT * E].rearrange("p (t e) -> p t e", e=E))
            dve.drain()
            if normed:
                dve.tensor_reduce(z[:, :], scores[:, :, :], AX.X, ALU.max)
                dve.drain()
                for t in range(NT):
                    dve.tensor_scalar(scores[:, t, :], scores[:, t, :], z[:, t:t + 1], None, ALU.subtract)
                dve.drain()
                dve.sem_inc(exp_in.sem, 1)
                dve.wait_ge(exp_out.sem, exp_out.nth(1))
                dve.tensor_reduce(z[:, :], scores[:, :, :], AX.X, ALU.add)
                dve.drain()
                dve.reciprocal(z[:, :], z[:, :])
                dve.drain()
                for t in range(NT):
                    dve.tensor_scalar(scores[:, t, :], scores[:, t, :], z[:, t:t + 1], None, ALU.mult)
                dve.drain()
            for t in range(NT):
                dve.max(top[:, t, :], scores[:, t, :])
            dve.drain()
            for t in range(NT):
                dve.max_index(at[:, t, :], top[:, t, :], scores[:, t, :])
            if normed:
                dve.tensor_tensor(z[:, :], top[:, :, 0], top[:, :, 1], ALU.add)
                dve.drain()
                dve.tensor_scalar(z[:, :], z[:, :], 1e-8, None, ALU.add)
                dve.drain()
                dve.reciprocal(z[:, :], z[:, :])
                dve.drain()
                dve.tensor_tensor(gate[:, :, 0], top[:, :, 0], z[:, :], ALU.mult)
                dve.tensor_tensor(gate[:, :, 1], top[:, :, 1], z[:, :], ALU.mult)
            else:
                dve.tensor_tensor(z[:, :], top[:, :, 1], top[:, :, 0], ALU.subtract).then_inc(exp_in.sem, 1)
                dve.wait_ge(exp_out.sem, exp_out.nth(1))
                dve.tensor_scalar(gate[:, :, 0], z[:, :], 1.0, None, ALU.add)
                dve.drain()
                dve.reciprocal(gate[:, :, 0], gate[:, :, 0])
                dve.drain()
                dve.tensor_tensor(gate[:, :, 1], gate[:, :, 0], z[:, :], ALU.mult)
            dve.tensor_copy(atf[:, :, :], at[:, :, :])
            dve.wait_ge(small_in.sem, small_in.nth(16 * (6 if normed else 4)))
            dve.drain()
            for t in range(NT):
                dve.tensor_scalar(first[:, t, :], number[:, :], atf[:, t, 0:1], gate[:, t, 0:1], ALU.is_equal, ALU.mult)
                dve.tensor_scalar(second[:, t, :], number[:, :], atf[:, t, 1:2], gate[:, t, 1:2], ALU.is_equal, ALU.mult)
            dve.drain()
            dve.tensor_tensor(first[:, :, :], first[:, :, :], second[:, :, :], ALU.add).then_inc(gates_ready.sem, 1)
            dve.wait_ge(gates_turned.sem, gates_turned.nth(1))
            for half in range(HALVES):
                copied = dve.tensor_copy(gT[:, half * BANK:(half + 1) * BANK], ps_t[0:E, half, :])
            copied.then_inc(gT_ready.sem, 1)
            with dve.Fori(0, E // EB) as it:
                for n in range(N):
                    k, half = n // U, n % U // FC
                    if n % U == 0:
                        dve.wait_ge(expert_in[k].sem, expert_in[k].nth(64, it))
                    dve.wait_ge(gelu_ready.sem, gelu_ready.nth(n + 1, it))
                    dve.wait_ge(y_added.sem, y_added.nth(n + 1 - RING, it))
                    dve.tensor_tensor(hg[:, n % RING, :], h[:, n % RING, :], G[:, k, half * BANK:(half + 1) * BANK],
                                      ALU.mult).then_inc(gated.sem, 1)
            for half in range(HALVES):
                dve.wait_ge(y_ready.sem, y_ready.nth(half + 1))
                dve.tensor_copy(yT[:, half * BANK:(half + 1) * BANK], ps_y[:, half, :]).then_inc(yT_ready.sem, 1)
            for half in range(HALVES):
                dve.wait_ge(y_turned.sem, y_turned.nth(half + 1))
                dve.tensor_copy(m.Y[:, half * 4:half * 4 + 4, :], ps_t[:, half, :].rearrange("p (t d) -> p t d", d=D))

        @block.scalar
        def _(act):
            if normed:
                act.wait_ge(var_ready.sem, var_ready.nth(1))
                act.activation(rstd[:, :], rstd[:, :], ACT.Sqrt).then_inc(root_ready.sem, 1)
            act.wait_ge(exp_in.sem, exp_in.nth(1))
            v = scores[:, :, :] if normed else z[:, :]
            act.activation(v, v, ACT.Exp).then_inc(exp_out.sem, 1)
            with act.Fori(0, E // EB) as it:
                for n in range(N):
                    k, f = n // U, n % FC
                    if n % U == 0:
                        act.wait_ge(expert_in[k].sem, expert_in[k].nth(64, it))
                    act.wait_ge(h_ready.sem, h_ready.nth(n + 1, it))
                    act.wait_ge(gated.sem, gated.nth(n + 1 - RING, it))
                    act.activation(h[:, n % RING, :], ps_h[:, n % RING, :], ACT.Gelu, bias=b1[:, k, f:f + 1])\
                       .then_inc(gelu_ready.sem, 1)

        @block.tensor
        def _(pe):
            pe.sem_inc(y_added.sem, y_added.ahead)
            if normed:
                for t in range(NT):
                    pe.wait_ge(xn_ready.sem, xn_ready.nth(t + 1))
                    mm = pe.transpose(ps_t[:, t // 4, (t % 4) * P:(t % 4 + 1) * P], xn[:, t, :], m.ident[:, :])
                    if t % 4 == 3:
                        mm.then_inc(xn_turned.sem, 1)
                pe.wait_ge(xnT_ready.sem, xnT_ready.nth(HALVES))
            pe.wait_ge(small_in.sem, small_in.nth(16 * (6 if normed else 4)))
            for t in range(NT):
                out = ps_h[:, 0, t * E:(t + 1) * E]
                pe.matmul(out, xnT[:, t * P:(t + 1) * P], wg[:, :], start=True, stop=False)
                mm = pe.matmul(out, m.ones[0:1, :], bg[:, :], start=False, stop=True)
            mm.then_inc(scores_ready.sem, 1)
            pe.wait_ge(gates_ready.sem, gates_ready.nth(1))
            for t in range(NT):
                mm = pe.transpose(ps_t[0:E, t // 4, (t % 4) * P:(t % 4 + 1) * P], first[:, t, :], m.ident[:, :])
            mm.then_inc(gates_turned.sem, 1)
            pe.wait_ge(gT_ready.sem, gT_ready.nth(1))
            for half in range(HALVES):
                pe.matmul(ps_y[:, half, :], b2[:, :], gT[:, half * BANK:(half + 1) * BANK], start=True, stop=False,
                          skip_group_check=True)

            def up(it, n):
                k, half, f = n // U, n % U // FC, n % FC
                if n % U == 0:
                    pe.wait_ge(expert_in[k].sem, expert_in[k].nth(64, it))
                pe.wait_ge(gated.sem, gated.nth(n + 1 - RING, it))
                pe.matmul(ps_h[:, n % RING, :], w1[:, k, f * P:(f + 1) * P], xnT[:, half * BANK:(half + 1) * BANK],
                          start=True, stop=True).then_inc(h_ready.sem, 1)

            def down(it, n):
                k, half, f = n // U, n % U // FC, n % FC
                pe.wait_ge(gated.sem, gated.nth(n + 1, it))
                pe.matmul(ps_y[:, half, :], w2[:, k, f, :], hg[:, n % RING, :], start=False, stop=False,
                          skip_group_check=True).then_inc(y_added.sem, 1)

            with pe.Fori(0, E // EB) as it:
                for n in range(N):
                    up(it, n)
                    if n >= 2:
                        down(it, n - 2)
                down(it, N - 2)
                down(it, N - 1)
            for half in range(HALVES):
                pe.matmul(ps_y[:, half, :], m.ident[:, :], m.XT[:, half * BANK:(half + 1) * BANK], start=False, stop=True,
                          skip_group_check=True).then_inc(y_ready.sem, 1)
            for t in range(NT):
                pe.wait_ge(yT_ready.sem, yT_ready.nth(t // 4 + 1))
                mm = pe.transpose(ps_t[:, t // 4, (t % 4) * P:(t % 4 + 1) * P], yT[:, t * P:(t + 1) * P], m.ident[:, :])
                if t % 4 == 3:
                    mm.then_inc(y_turned.sem, 1)


def moe_0(m):
    moe(m, "L0_ffn", 8, normed=True)


def moe_1(m):
    moe(m, "L1_ffn", 24, normed=False)


def sparse_attention(m):
    with ExitStack() as ctx:
        place = Place(m.nc, ctx, "sparse")
        accT = place.sbuf("accT", [P, B * T])
        attention(m, Heads("L1_attn", T, 4, 32, 8, scale=8 ** -0.5, biased=True, masked=True), m.XT, accT)
        add_column(m, accT, m.dram["L1_attn_b_out"])
        to_rows(m, accT)


def cosine_cross(m):
    nc = m.nc
    with ExitStack() as ctx:
        place = Place(nc, ctx, "cosine")
        xnT = place.sbuf("xnT", [P, B * T])
        accT = place.sbuf("accT", [P, B * T])
        normed_columns(m, xnT, m.dram["L1_xattn_g_norm"])
        attention(m, Heads("L1_xattn", S + 1, 2, 64, 64, scale=8.0, context=True, cosine=True, null=True), xnT, accT)
        to_rows(m, accT, norm=m.dram["L1_xattn_g_out"])


def normed_columns(m, xnT, gain_dram):
    nc = m.nc
    with ExitStack() as ctx:
        place = Place(nc, ctx, "normed")
        gain = place.sbuf("gain", [P, 1])
        xn = place.sbuf("xn", [P, NT, D])
        stats = place.sbuf("stats", [P, NT, 6])
        mv = place.sbuf("mv", [P, NT, 2])
        rstd = place.sbuf("rstd", [P, NT])
        ps = place.psum("ps", [P, NT * P])
        gain_in = place.counter("gain_in")
        var_ready = place.counter("var_ready")
        root_ready = place.counter("root_ready")
        xn_ready = place.counter("xn_ready")
        turned = place.counter("turned")
        block = ctx.enter_context(nc.Block())

        @block.sync
        def _(sp):
            sp.dma_start(gain[:, :], gain_dram.rearrange("(p o) -> p o", o=1)).then_inc(gain_in.sem, 16)

        @block.vector
        def _(dve):
            for t in range(NT):
                dve.bn_stats(stats[:, t, :], m.X[:, t, :])
            dve.drain()
            for t in range(NT):
                dve.bn_aggr(mv[:, t, :], stats[:, t, :])
            dve.drain()
            dve.tensor_scalar(rstd[:, :], mv[:, :, 1], 1e-5, None, ALU.add).then_inc(var_ready.sem, 1)
            dve.wait_ge(root_ready.sem, root_ready.nth(1))
            dve.reciprocal(rstd[:, :], rstd[:, :])
            dve.drain()
            for t in range(NT):
                dve.tensor_scalar(xn[:, t, :], m.X[:, t, :], mv[:, t, 0:1], rstd[:, t:t + 1],
                                  ALU.subtract, ALU.mult).then_inc(xn_ready.sem, 1)
            dve.wait_ge(gain_in.sem, gain_in.nth(16))
            for half in range(2):
                dve.wait_ge(turned.sem, turned.nth(half + 1))
                cols = slice(half * BANK, (half + 1) * BANK)
                dve.tensor_scalar(xnT[:, cols], ps[:, cols], gain[:, 0:1], None, ALU.mult)

        @block.scalar
        def _(act):
            act.wait_ge(var_ready.sem, var_ready.nth(1))
            act.activation(rstd[:, :], rstd[:, :], ACT.Sqrt).then_inc(root_ready.sem, 1)

        @block.tensor
        def _(pe):
            for t in range(NT):
                pe.wait_ge(xn_ready.sem, xn_ready.nth(t + 1))
                mm = pe.transpose(ps[:, t * P:(t + 1) * P], xn[:, t, :], m.ident[:, :])
                if t % 4 == 3:
                    mm.then_inc(turned.sem, 1)


def peridynamic(m):
    nc = m.nc
    J = 64
    H = 16
    E = 16
    G = 2
    PAD = J - 1
    WT = PAD + T
    JB = 8
    NB = J // JB
    with ExitStack() as outer:
        keep = Place(nc, outer, "peri")
        logits = keep.sbuf("logits", [P, NT, J, H])
        value = keep.sbuf("value", [P, B, WT])
        with ExitStack() as mid:
            keep2 = Place(nc, mid, "peri_in")
            damage = keep2.sbuf("damage", [P, NT, J, H])
            moved = keep2.sbuf("moved", [P, G, B, 2, WT])
            pos = keep2.sbuf("pos", [P, J])
            b_dmg = keep2.sbuf("b_dmg", [P, 1])
            out8 = keep2.sbuf("out8", [P, 2, 8])
            peridynamic_project(m, moved, value, pos, b_dmg, out8)
            peridynamic_bonds(m, moved, pos, b_dmg, out8, logits, damage)
            peridynamic_softmax(m, logits, damage)
        peridynamic_gather(m, logits, value)


def peridynamic_project(m, moved, value, pos, b_dmg, out8):
    nc = m.nc
    G, J, PAD = 2, 64, 63
    with ExitStack() as ctx:
        place = Place(nc, ctx, "project")
        W_disp = place.sbuf("W_disp", [P, 256])
        W_val = place.sbuf("W_val", [P, D])
        blocks = place.sbuf("blocks", [P, 2, P])
        pos8 = place.sbuf("pos8", [16, P])
        rel_T = place.sbuf("rel_T", [16, J])
        dispT = place.sbuf("dispT", [P, G, B * T])
        ps = place.psum("ps", [P, 2, BANK])
        w_in = place.counter("w_in")
        product_ready = place.counter("product_ready")
        product_taken = place.counter("product_taken")
        block = ctx.enter_context(nc.Block())

        @block.sync
        def _(sp):
            for tile, name in [(W_disp, "W_disp"), (W_val, "W_val"), (blocks, "blocks"), (pos8, "pos8"), (rel_T, "rel_T"),
                               (b_dmg, "b_dmg8"), (out8, "out8")]:
                at = tuple([slice(None)] * len(tile.shape))
                sp.dma_start(tile[at], m.dram["L2_attn_" + name]).then_inc(w_in.sem, 16)

        jobs = [("disp", g, half) for g in range(G) for half in range(2)] + [("val", 0, half) for half in range(2)] + \
            [("pos", 0, 0)] + [("moved", g * 2 + k, half) for g in range(G) for k in range(2) for half in range(2)]

        @block.tensor
        def _(pe):
            pe.wait_ge(w_in.sem, w_in.nth(16 * 7))
            for n, (what, i, half) in enumerate(jobs):
                cols = slice(half * BANK, (half + 1) * BANK)
                if what == "moved":
                    pe.wait_ge(product_taken.sem, product_taken.nth(max(n - 1, 4)))
                elif n >= 2:
                    pe.wait_ge(product_taken.sem, product_taken.nth(n - 1))
                if what == "disp":
                    mm = pe.matmul(ps[:, n % 2, :], W_disp[:, i * P:(i + 1) * P], m.XT[:, cols], start=True, stop=True)
                elif what == "val":
                    mm = pe.matmul(ps[:, n % 2, :], W_val[:, :], m.XT[:, cols], start=True, stop=True)
                elif what == "pos":
                    mm = pe.matmul(ps[:, n % 2, 0:J], pos8[:, :], rel_T[:, :], start=True, stop=True)
                else:
                    mm = pe.matmul(ps[:, n % 2, :], blocks[:, i % 2, :], dispT[:, i // 2, cols], start=True, stop=True)
                mm.then_inc(product_ready.sem, 1)

        @block.vector
        def _(dve):
            dve.memset(moved[:, :, :, :, 0:PAD], 0.0)
            dve.memset(value[:, :, 0:PAD], 0.0)
            for n, (what, i, half) in enumerate(jobs):
                dve.wait_ge(product_ready.sem, product_ready.nth(n + 1))
                cols = slice(half * BANK, (half + 1) * BANK)
                batches = slice(2 * half, 2 * half + 2)
                both = ps[:, n % 2, :].rearrange("p (b t) -> p b t", b=2)
                if what == "disp":
                    ins = dve.tensor_copy(dispT[:, i, cols], ps[:, n % 2, :])
                elif what == "val":
                    ins = dve.tensor_copy(value[:, batches, PAD:], both)
                elif what == "pos":
                    ins = dve.tensor_copy(pos[:, :], ps[:, n % 2, 0:J])
                else:
                    ins = dve.tensor_copy(moved[:, i // 2, batches, i % 2, PAD:], both)
                ins.then_inc(product_taken.sem, 1)


def peridynamic_bonds(m, moved, pos, b_dmg, out8, logits, damage):
    nc = m.nc
    G, J, PAD, JB = 2, 64, 63, 8
    NB = J // JB
    Q = 2
    NQ = JB // Q
    with ExitStack() as ctx:
        place = Place(nc, ctx, "bonds")
        here = place.sbuf("here", [P, 2, PAD + T])
        strain = place.sbuf("strain", [P, 2, 2, Q, T])
        act_of = place.sbuf("act_of", [P, 2, 2, Q, T])
        ps = place.psum("ps", [P, 2, 2, BANK])
        here_in = place.counter("here_in", per=1)
        strain_ready = place.counter("strain_ready", per=NQ, ahead=NQ)
        gelu_ready = place.counter("gelu_ready", per=NQ, ahead=NQ)
        summed = place.counter("summed", per=NQ, ahead=NQ)
        logits_taken = place.counter("logits_taken", per=1, ahead=1)
        block = ctx.enter_context(nc.Block())

        @block.vector
        def _(dve):
            dve.sem_inc(strain_ready.sem, strain_ready.ahead)
            dve.sem_inc(logits_taken.sem, logits_taken.ahead)
            with dve.Fori(0, B) as b, dve.Fori(0, G) as g, dve.Fori(0, NB) as jb:
                it = (b * G + g) * NB + jb
                window = moved[:, bass.ds(g, 1), bass.ds(b, 1), :, :].rearrange("p g b k t -> p (g b k) t")
                for q in range(NQ):
                    dve.wait_ge(gelu_ready.sem, gelu_ready.nth(q - 1, it))
                    for o in range(Q):
                        ins = dve.tensor_tensor(strain[:, q % 2, :, o, :], window[:, :, bass.ds(jb * JB + q * Q + o, T)],
                                                window[:, :, PAD:], ALU.subtract)
                    ins.then_inc(strain_ready.sem, 1)
                dve.wait_ge(summed.sem, summed.nth(NQ, it))
                col = jb * JB
                for t in range(2):
                    for k, where in enumerate((logits, damage)):
                        at = where[:, bass.ds(b * 2 + t, 1), bass.ds(col, JB), bass.ds(g * 8, 8)]
                        ins = dve.tensor_copy(at.rearrange("p o j h -> p (o j) h"),
                                              ps[:, k, t, 0:JB * 8].rearrange("p (j h) -> p j h", h=8))
                ins.then_inc(logits_taken.sem, 1)

        @block.scalar
        def _(act):
            act.sem_inc(gelu_ready.sem, gelu_ready.ahead)
            with act.Fori(0, B) as b, act.Fori(0, G) as g, act.Fori(0, NB) as jb:
                it = (b * G + g) * NB + jb
                for q in range(NQ):
                    act.wait_ge(strain_ready.sem, strain_ready.nth(q + 1, it))
                    act.wait_ge(summed.sem, summed.nth(q - 1, it))
                    for o in range(Q):
                        act.activation(act_of[:, q % 2, 0, o, :], strain[:, q % 2, 0, o, :], ACT.Gelu,
                                       bias=pos[:, bass.ds(jb * JB + q * Q + o, 1)])
                    act.activation(act_of[:, q % 2, 1, :, :], strain[:, q % 2, 1, :, :], ACT.Gelu, bias=b_dmg[:, :])\
                       .then_inc(gelu_ready.sem, 1)

        @block.tensor
        def _(pe):
            pe.sem_inc(summed.sem, summed.ahead)
            with pe.Fori(0, B * G * NB) as it:
                pe.wait_ge(logits_taken.sem, logits_taken.nth(0, it))
                for q in range(NQ):
                    pe.wait_ge(gelu_ready.sem, gelu_ready.nth(q + 1, it))
                    for k in range(2):
                        for t in range(2):
                            for o in range(Q):
                                j = q * Q + o
                                mm = pe.matmul(ps[:, k, t, j * 8:(j + 1) * 8], act_of[:, q % 2, k, o, t * P:(t + 1) * P],
                                               out8[:, k, :], start=True, stop=True)
                    mm.then_inc(summed.sem, 1)


def peridynamic_softmax(m, logits, damage):
    nc = m.nc
    J, H = 64, 16
    with ExitStack() as ctx:
        place = Place(nc, ctx, "weights")
        mask = place.sbuf("mask", [P, J])
        b_out = place.sbuf("b_out", [P, 1])
        stat = place.sbuf("stat", [P, NT, H])
        small_in = place.counter("small_in")
        damage_ready = place.counter("damage_ready")
        shifted = place.counter("shifted")
        exp_l = place.counter("exp_l")
        block = ctx.enter_context(nc.Block())

        @block.sync
        def _(sp):
            sp.dma_start(mask[:, :], m.dram["L2_attn_mask"]).then_inc(small_in.sem, 16)
            sp.dma_start(b_out[:, :], m.dram["L2_attn_b_dmg_out"].rearrange("(o d) -> o d", o=1).broadcast_to([P, 1]))\
              .then_inc(small_in.sem, 16)

        @block.scalar
        def _(act):
            act.wait_ge(small_in.sem, small_in.nth(32))
            for t in range(NT):
                act.activation(damage[:, t, :, :], damage[:, t, :, :], ACT.Sigmoid, bias=b_out[:, :])\
                   .then_inc(damage_ready.sem, 1)
            for t in range(NT):
                act.wait_ge(shifted.sem, shifted.nth(t + 1))
                act.activation(logits[:, t, :, :], logits[:, t, :, :], ACT.Exp).then_inc(exp_l.sem, 1)

        @block.vector
        def _(dve):
            dve.wait_ge(small_in.sem, small_in.nth(32))
            for t in range(NT):
                dve.wait_ge(damage_ready.sem, damage_ready.nth(t + 1))
                dve.scalar_tensor_tensor(out=logits[:, t, :, :], in0=damage[:, t, :, :], scalar=-10.0, in1=logits[:, t, :, :],
                                         op0=ALU.mult, op1=ALU.add)
                if t % TB == 0:
                    dve.drain()
                    spread = mask[:, :].rearrange("p (j o) -> p j o", o=1).broadcast_to([P, J, H])
                    dve.tensor_tensor(logits[:, t, :, :], logits[:, t, :, :], spread, ALU.add)
                dve.drain()
                dve.tensor_reduce(stat[:, t, :], logits[:, t, :, :].rearrange("p j h -> p h j"), AX.X, ALU.max)
                dve.drain()
                over = stat[:, t:t + 1, :].broadcast_to([P, J, H])
                dve.tensor_tensor(logits[:, t, :, :], logits[:, t, :, :], over, ALU.subtract).then_inc(shifted.sem, 1)
            for t in range(NT):
                dve.wait_ge(exp_l.sem, exp_l.nth(t + 1))
                dve.tensor_reduce(stat[:, t, :], logits[:, t, :, :].rearrange("p j h -> p h j"), AX.X, ALU.add)
                dve.drain()
                dve.reciprocal(stat[:, t, :], stat[:, t, :])
                dve.drain()
                over = stat[:, t:t + 1, :].broadcast_to([P, J, H])
                dve.tensor_tensor(logits[:, t, :, :], logits[:, t, :, :], over, ALU.mult)


def peridynamic_gather(m, weights, value):
    nc = m.nc
    J, H, JB = 64, 16, 8
    NB = J // JB
    with ExitStack() as ctx:
        place = Place(nc, ctx, "gather")
        spread = place.sbuf("spread", [P, JB, P])
        W_cproj = place.sbuf("W_cproj", [P, D])
        now = place.sbuf("now", [P, TB, P])
        wT = place.sbuf("wT", [P, T])
        prod = place.sbuf("prod", [P, 2, 2, T])
        oT = place.sbuf("oT", [P, B * T])
        ps_t = place.psum("ps_t", [P, T])
        ps_w = place.psum("ps_w", [P, 2, BANK])
        ps_o = place.psum("ps_o", [P, BANK])
        ps_y = place.psum("ps_y", [P, 2, BANK])
        NQ = JB // 2
        small_in = place.counter("small_in")
        staged = place.counter("staged")
        w_turned = place.counter("w_turned", ahead=1)
        wT_ready = place.counter("wT_ready")
        spread_ready = place.counter("spread_ready", per=NQ)
        prod_ready = place.counter("prod_ready", per=NQ, ahead=NQ)
        added = place.counter("added", per=NQ, ahead=NQ)
        sum_taken = place.counter("sum_taken", ahead=1)
        y_ready = place.counter("y_ready")
        block = ctx.enter_context(nc.Block())

        @block.sync
        def _(sp):
            sp.dma_start(spread[:, :, :], m.dram["L2_attn_spread"]).then_inc(small_in.sem, 16)
            sp.dma_start(W_cproj[:, :], m.dram["L2_attn_W_cproj"]).then_inc(small_in.sem, 16)

        @block.scalar
        def _(act):
            with act.Fori(0, B) as b, act.Fori(0, NB) as jb:
                it = b * NB + jb
                act.wait_ge(w_turned.sem, w_turned.nth(0, it))
                at = weights[:, bass.ds(b * TB, TB), bass.ds(jb * JB, JB), :].rearrange("p t j h -> p t (j h)")
                act.activation(now[:, :, :], at, ACT.Copy).then_inc(staged.sem, 1)
                act.wait_ge(w_turned.sem, w_turned.nth(1, it))
                act.activation(wT[:, :], ps_t[:, :], ACT.Copy).then_inc(wT_ready.sem, 1)

        @block.tensor
        def _(pe):
            pe.sem_inc(w_turned.sem, w_turned.ahead)
            pe.sem_inc(added.sem, added.ahead)
            pe.wait_ge(small_in.sem, small_in.nth(32))
            with pe.Fori(0, B) as b:
                pe.wait_ge(sum_taken.sem, sum_taken.nth(0, b))
                for jb in range(NB):
                    it = b * NB + jb
                    pe.wait_ge(staged.sem, staged.nth(1, it))
                    for t in range(TB):
                        mm = pe.transpose(ps_t[:, t * P:(t + 1) * P], now[:, t, :], m.ident[:, :])
                    mm.then_inc(w_turned.sem, 1)
                    pe.wait_ge(wT_ready.sem, wT_ready.nth(1, it))

                    def spread_out(q):
                        pe.wait_ge(prod_ready.sem, prod_ready.nth(q - 1, it))
                        for o in range(2):
                            mm = pe.matmul(ps_w[:, q % 2, o * T:(o + 1) * T], spread[:, 2 * q + o, :], wT[:, :], start=True, stop=True)
                        mm.then_inc(spread_ready.sem, 1)

                    def add(q):
                        pe.wait_ge(prod_ready.sem, prod_ready.nth(q + 1, it))
                        for o in range(2):
                            j = jb * JB + 2 * q + o
                            mm = pe.matmul(ps_o[:, 0:T], m.ident[:, :], prod[:, q % 2, o, :], start=(j == 0), stop=(j == J - 1),
                                           skip_group_check=True)
                        mm.then_inc(added.sem, 1)

                    spread_out(0)
                    for q in range(NQ):
                        if q + 1 < NQ:
                            spread_out(q + 1)
                        add(q)
            pe.wait_ge(sum_taken.sem, sum_taken.nth(B))
            for t in range(NT):
                mm = pe.matmul(ps_y[:, t // 4, (t % 4) * P:(t % 4 + 1) * P], oT[:, t * P:(t + 1) * P], W_cproj[:, :], start=True,
                               stop=True)
            mm.then_inc(y_ready.sem, 1)

        @block.vector
        def _(dve):
            dve.sem_inc(prod_ready.sem, prod_ready.ahead)
            dve.sem_inc(sum_taken.sem, sum_taken.ahead)
            with dve.Fori(0, B) as b:
                with dve.Fori(0, NB) as jb:
                    it = b * NB + jb
                    for q in range(NQ):
                        dve.wait_ge(spread_ready.sem, spread_ready.nth(q + 1, it))
                        dve.wait_ge(added.sem, added.nth(q - 1, it))
                        for o in range(2):
                            v = value[:, bass.ds(b, 1), bass.ds(jb * JB + 2 * q + o, T)].rearrange("p b t -> p (b t)")
                            ins = dve.tensor_tensor(prod[:, q % 2, o, :], ps_w[:, q % 2, o * T:(o + 1) * T], v, ALU.mult)
                        ins.then_inc(prod_ready.sem, 1)
                dve.wait_ge(added.sem, added.nth(NQ, b * NB + (NB - 1)))
                dve.tensor_copy(oT[:, bass.ds(b * T, T)], ps_o[:, 0:T]).then_inc(sum_taken.sem, 1)
            dve.wait_ge(y_ready.sem, y_ready.nth(1))
            dve.tensor_copy(m.Y[:, :, :], ps_y[:, :, :].rearrange("p h (t d) -> p (h t) d", d=D))


def top_k_cross(m):
    with ExitStack() as ctx:
        place = Place(m.nc, ctx, "topk")
        accT = place.sbuf("accT", [P, B * T])
        attention(m, Heads("L2_xattn", S, 1, P, D, scale=D ** -0.5, biased=True, context=True, n_heads=1, choose=32),
                  m.XT, accT)
        add_column(m, accT, m.dram["L2_xattn_bo"])
        to_rows(m, accT)


def local_transformer(m):
    nc = m.nc
    with ExitStack() as ctx:
        place = Place(nc, ctx, "local")
        Z = place.sbuf("Z", [P, B * T])
        shifted = place.sbuf("shifted", [P, B * T])
        copy_columns(m, m.XT, Z)
        with nc.Fori(0, 6) as layer:
            shift_tokens(m, Z, shifted)
            attention(m, Heads("L2_ffn", T, 2, 64, 64, scale=8.0, cosine=True, masked=True, rotary=True), shifted, Z,
                      layer=layer, add=True)
            gated_ffn(m, Z, shifted, layer)
        to_rows(m, Z)


def copy_columns(m, source, target):
    with ExitStack() as ctx:
        block = ctx.enter_context(m.nc.Block())

        @block.vector
        def _(dve):
            dve.tensor_copy(target[:, :], source[:, :])


def shift_tokens(m, Z, shifted):
    with ExitStack() as ctx:
        block = ctx.enter_context(m.nc.Block())
        lower, upper = slice(0, D // 2), slice(D // 2, D)

        @block.vector
        def _(dve):
            by_batch = shifted[upper, :].rearrange("p (b t) -> p b t", t=T)
            dve.tensor_copy(by_batch[:, :, 1:], Z[upper, :].rearrange("p (b t) -> p b t", t=T)[:, :, 0:T - 1])
            dve.memset(by_batch[:, :, 0:1], 0.0)

        @block.scalar
        def _(act):
            act.activation(shifted[lower, :], Z[lower, :], ACT.Copy)


def gated_ffn(m, Z, xs, layer):
    nc = m.nc
    FC = 3
    FP = FC * P
    N = 2 * FC
    BIAS = 2 * FP
    with ExitStack() as ctx:
        place = Place(nc, ctx, "gated")
        up = place.sbuf("up", [P, 2 * FP + 2 * FC + 3])
        down = place.sbuf("down", [P, FC, D])
        centred = place.sbuf("centred", [P, B * T])
        work = place.sbuf("work", [P, B * T])
        gate = place.sbuf("gate", [P, 2, BANK])
        h = place.sbuf("h", [P, 2, BANK])
        ps_m = place.psum("ps_m", [P, 2, BANK])
        ps_a = place.psum("ps_a", [P, 2, BANK])
        ps_g = place.psum("ps_g", [P, 2, BANK])
        ps_y = place.psum("ps_y", [P, 2, BANK])
        w_in = place.counter("w_in")
        xs_ready = place.counter("xs_ready")
        mean_ready = place.counter("mean_ready")
        squares_ready = place.counter("squares_ready")
        var_ready = place.counter("var_ready")
        var_taken = place.counter("var_taken")
        root_ready = place.counter("root_ready")
        xn_ready = place.counter("xn_ready")
        up_ready = place.counter("up_ready")
        gelu_ready = place.counter("gelu_ready")
        h_ready = place.counter("h_ready")
        down_done = place.counter("down_done")
        block = ctx.enter_context(nc.Block())
        halves = [slice(half * BANK, (half + 1) * BANK) for half in range(2)]

        @block.sync
        def _(sp):
            sp.dma_start(up[:, :], m.dram["L2_ffn_up"][bass.ds(layer, 1), :, :].rearrange("l p c -> (l p) c")).then_inc(w_in.sem, 16)
            sp.dma_start(down[:, :, :], m.dram["L2_ffn_down"][bass.ds(layer, 1), :, :, :].rearrange("l p c d -> (l p) c d"))\
              .then_inc(w_in.sem, 16)

        @block.vector
        def _(dve):
            by_batch = xs[D // 2:, :].rearrange("p (b t) -> p b t", t=T)
            dve.tensor_copy(by_batch[:, :, 1:], Z[D // 2:, :].rearrange("p (b t) -> p b t", t=T)[:, :, 0:T - 1])\
               .then_inc(xs_ready.sem, 1)
            for half in range(2):
                dve.wait_ge(mean_ready.sem, mean_ready.nth(half + 1))
                dve.scalar_tensor_tensor(out=centred[:, halves[half]], in0=ps_m[:, half, :], scalar=-1.0 / D, in1=xs[:, halves[half]],
                                         op0=ALU.mult, op1=ALU.add)
                dve.drain()
                dve.tensor_tensor(work[:, halves[half]], centred[:, halves[half]], centred[:, halves[half]], ALU.mult)\
                   .then_inc(squares_ready.sem, 1)
            for half in range(2):
                dve.wait_ge(var_ready.sem, var_ready.nth(half + 1))
                dve.tensor_scalar(work[:, halves[half]], ps_m[:, half, :], 1.0 / D, 1e-5, ALU.mult, ALU.add).then_inc(var_taken.sem, 1)
            dve.wait_ge(w_in.sem, w_in.nth(32))
            for half in range(2):
                dve.wait_ge(root_ready.sem, root_ready.nth(half + 1))
                dve.reciprocal(work[:, halves[half]], work[:, halves[half]])
                dve.drain()
                dve.tensor_tensor(centred[:, halves[half]], centred[:, halves[half]], work[:, halves[half]], ALU.mult)
                dve.drain()
                c = BIAS + 2 * FC
                dve.tensor_scalar(centred[:, halves[half]], centred[:, halves[half]], up[:, c:c + 1], up[:, c + 1:c + 2],
                                  ALU.mult, ALU.add).then_inc(xn_ready.sem, 1)
            for n in range(N):
                half, f = n // FC, n % FC
                dve.wait_ge(gelu_ready.sem, gelu_ready.nth(n + 1))
                if n >= 2:
                    dve.wait_ge(down_done.sem, down_done.nth(n - 1))
                dve.scalar_tensor_tensor(out=h[:, n % 2, :], in0=ps_a[:, n % 2, :], scalar=up[:, BIAS + f:BIAS + f + 1],
                                         in1=gate[:, n % 2, :], op0=ALU.add, op1=ALU.mult).then_inc(h_ready.sem, 1)
            for half in range(2):
                dve.wait_ge(down_done.sem, down_done.nth((half + 1) * FC))
                c = BIAS + 2 * FC + 2
                dve.scalar_tensor_tensor(out=Z[:, halves[half]], in0=ps_y[:, half, :], scalar=up[:, c:c + 1], in1=Z[:, halves[half]],
                                         op0=ALU.add, op1=ALU.add)

        @block.scalar
        def _(act):
            act.activation(xs[0:D // 2, :], Z[0:D // 2, :], ACT.Copy).then_inc(xs_ready.sem, 1)
            for half in range(2):
                act.wait_ge(var_taken.sem, var_taken.nth(half + 1))
                act.activation(work[:, halves[half]], work[:, halves[half]], ACT.Sqrt).then_inc(root_ready.sem, 1)
            act.wait_ge(w_in.sem, w_in.nth(32))
            for n in range(N):
                f = n % FC
                act.wait_ge(up_ready.sem, up_ready.nth(n + 1))
                if n >= 2:
                    act.wait_ge(h_ready.sem, h_ready.nth(n - 1))
                act.activation(gate[:, n % 2, :], ps_g[:, n % 2, :], ACT.Gelu, bias=up[:, BIAS + FC + f:BIAS + FC + f + 1])\
                   .then_inc(gelu_ready.sem, 1)

        @block.tensor
        def _(pe):
            pe.wait_ge(xs_ready.sem, xs_ready.nth(2))
            for half in range(2):
                pe.matmul(ps_m[:, half, :], m.ones[:, :], xs[:, halves[half]], start=True, stop=True).then_inc(mean_ready.sem, 1)
            for half in range(2):
                pe.wait_ge(squares_ready.sem, squares_ready.nth(half + 1))
                pe.matmul(ps_m[:, half, :], m.ones[:, :], work[:, halves[half]], start=True, stop=True).then_inc(var_ready.sem, 1)
            pe.wait_ge(w_in.sem, w_in.nth(32))

            def rise(n):
                half, f = n // FC, n % FC
                pe.wait_ge(xn_ready.sem, xn_ready.nth(half + 1))
                if n >= 2:
                    pe.wait_ge(h_ready.sem, h_ready.nth(n - 1))
                pe.matmul(ps_a[:, n % 2, :], up[:, f * P:(f + 1) * P], centred[:, halves[half]], start=True, stop=True)
                pe.matmul(ps_g[:, n % 2, :], up[:, FP + f * P:FP + (f + 1) * P], centred[:, halves[half]], start=True, stop=True)\
                  .then_inc(up_ready.sem, 1)

            rise(0)
            for n in range(N):
                if n + 1 < N:
                    rise(n + 1)
                half, f = n // FC, n % FC
                pe.wait_ge(h_ready.sem, h_ready.nth(n + 1))
                pe.matmul(ps_y[:, half, :], down[:, f, :], h[:, n % 2, :], start=(f == 0), stop=(f == FC - 1))\
                  .then_inc(down_done.sem, 1)


def linear_recurrence(m):
    nc = m.nc
    HALVES = B * T // BANK
    with ExitStack() as ctx:
        place = Place(nc, ctx, "recur")
        names = ["Wk", "Wv", "Ww", "Wr", "Wo"]
        w = place.sbuf("w", [P, len(names), D])
        same_head = place.sbuf("same_head", [P, P])
        kT = place.sbuf("kT", [P, B * T])
        vT = place.sbuf("vT", [P, B * T])
        dT = place.sbuf("dT", [P, B * T])
        rT = place.sbuf("rT", [P, B * T])
        oT = place.sbuf("oT", [P, B * T])
        o2T = place.sbuf("o2T", [P, B * T])
        ms = place.sbuf("ms", [P, NT])
        ps = place.psum("ps", [P, 2, BANK])
        ps_k = place.psum("ps_k", [P, 2, BANK])
        ps_y = place.psum("ps_y", [P, 2, BANK])
        ps_s = place.psum("ps_s", [P, BANK])
        w_in = place.counter("w_in")
        product_ready = place.counter("product_ready")
        product_taken = place.counter("product_taken")
        k_sum_ready = place.counter("k_sum_ready")
        o_ready = place.counter("o_ready")
        y_ready = place.counter("y_ready")
        mean_ready = place.counter("mean_ready")
        root_ready = place.counter("root_ready")
        block = ctx.enter_context(nc.Block())

        @block.sync
        def _(sp):
            for i, name in enumerate(names):
                sp.dma_start(w[:, i, :], m.dram["L3_attn_" + name]).then_inc(w_in.sem, 16)
            sp.dma_start(same_head[:, :], m.dram["c_same_head8"]).then_inc(w_in.sem, 16)

        @block.tensor
        def _(pe):
            pe.wait_ge(w_in.sem, w_in.nth(16 * (len(names) + 1)))
            for n in range(4 * HALVES):
                i, half = n // HALVES, n % HALVES
                cols = slice(half * BANK, (half + 1) * BANK)
                if n >= 2:
                    pe.wait_ge(product_taken.sem, product_taken.nth(n - 1))
                pe.matmul(ps[:, n % 2, :], w[:, i, :], m.XT[:, cols], start=True, stop=True)\
                  .then_inc(product_ready.sem, 1)
            for half in range(HALVES):
                cols = slice(half * BANK, (half + 1) * BANK)
                pe.wait_ge(product_taken.sem, product_taken.nth(HALVES))
                pe.matmul(ps_k[:, half, :], same_head[:, :], kT[:, cols], start=True, stop=True)\
                  .then_inc(k_sum_ready.sem, 1)
            pe.wait_ge(o_ready.sem, o_ready.nth(1))
            for t in range(NT):
                tok = slice(t * P, (t + 1) * P)
                pe.matmul(ps_y[:, t // 4, (t % 4) * P:(t % 4 + 1) * P], oT[:, tok], w[:, 4, :], start=True, stop=True)
                mm = pe.matmul(ps_s[:, t:t + 1], o2T[:, tok], m.ones[:, 0:1], start=True, stop=True)
            mm.then_inc(y_ready.sem, 1)

        @block.scalar
        def _(act):
            for n in range(4 * HALVES):
                i, half = n // HALVES, n % HALVES
                cols = slice(half * BANK, (half + 1) * BANK)
                act.wait_ge(product_ready.sem, product_ready.nth(n + 1))
                act.activation([kT, vT, dT, rT][i][:, cols], ps[:, n % 2, :], ACT.Sigmoid if i >= 2 else ACT.Copy)\
                   .then_inc(product_taken.sem, 1)
            act.wait_ge(mean_ready.sem, mean_ready.nth(1))
            act.activation(ms[:, :], ms[:, :], ACT.Sqrt).then_inc(root_ready.sem, 1)

        @block.vector
        def _(dve):
            dve.wait_ge(product_taken.sem, product_taken.nth(4 * HALVES))
            dve.tensor_scalar(dT[:, :], dT[:, :], 0.99, None, ALU.mult)
            for half in range(HALVES):
                cols = slice(half * BANK, (half + 1) * BANK)
                dve.wait_ge(k_sum_ready.sem, k_sum_ready.nth(half + 1))
                dve.tensor_tensor(vT[:, cols], ps_k[:, half, :], vT[:, cols], ALU.mult)
            dve.drain()
            for b in range(B):
                tok = slice(b * T, (b + 1) * T)
                dve.tensor_tensor_scan(oT[:, tok], dT[:, tok], vT[:, tok], 0.0, ALU.mult, ALU.add)
            dve.drain()
            dve.tensor_tensor(oT[:, :], oT[:, :], rT[:, :], ALU.mult)
            dve.drain()
            dve.tensor_tensor(o2T[:, :], oT[:, :], oT[:, :], ALU.mult).then_inc(o_ready.sem, 1)
            dve.wait_ge(y_ready.sem, y_ready.nth(1))
            eps = float(np.finfo(np.float32).eps)
            dve.tensor_scalar(ms[:, :], ps_s[:, 0:NT], 1.0 / D, eps, ALU.mult, ALU.add).then_inc(mean_ready.sem, 1)
            dve.wait_ge(root_ready.sem, root_ready.nth(1))
            dve.reciprocal(ms[:, :], ms[:, :])
            dve.drain()
            for t in range(NT):
                dve.tensor_scalar(m.Y[:, t, :], ps_y[:, t // 4, (t % 4) * P:(t % 4 + 1) * P], ms[:, t:t + 1], None,
                                  ALU.mult)


def double_mha(m):
    with ExitStack() as ctx:
        place = Place(m.nc, ctx, "double")
        hT = place.sbuf("hT", [P, B * T])
        accT = place.sbuf("accT", [P, B * T])
        attention(m, Heads("L3_xattn1", T, 4, 32, 8, scale=8 ** -0.5, biased=True, masked=True), m.XT, hT)
        add_column(m, hT, m.dram["L3_xattn_bo1"])
        attention(m, Heads("L3_xattn2", S, 4, 32, 8, scale=8 ** -0.5, biased=True, context=True), hT, accT)
        add_column(m, accT, m.dram["L3_xattn_bo2"])
        to_rows(m, accT)


def ternary_ffn(m):
    nc = m.nc
    F = 512
    FC = F // P
    with ExitStack() as ctx:
        place = Place(nc, ctx, "ternary")
        w = place.sbuf("w", [P, 2, FC * P])
        wq = place.sbuf("wq", [P, 2, FC * P])
        small = place.sbuf("small", [P, FC * P])
        sums = place.sbuf("sums", [P, 2])
        level = place.sbuf("level", [P, 2, 2])
        sq = place.sbuf("sq", [P, NT, D])
        rms = place.sbuf("rms", [P, NT])
        xnT = place.sbuf("xnT", [P, B * T])
        hT = place.sbuf("hT", [P, FC, B * T])
        hsq = place.sbuf("hsq", [P, FC, B * T])
        rms_h = place.sbuf("rms_h", [P, NT])
        ps_level = place.psum("ps_level", [P, BANK])
        ps_x = place.psum("ps_x", [P, 2, BANK])
        ps_h = place.psum("ps_h", [P, 2, BANK])
        ps_y = place.psum("ps_y", [P, 2, BANK])
        ps_s = place.psum("ps_s", [P, BANK])
        w_in = place.counter("w_in")
        sums_ready = place.counter("sums_ready")
        level_ready = place.counter("level_ready")
        w_ready = place.counter("w_ready")
        square_ready = place.counter("square_ready")
        root_ready = place.counter("root_ready")
        xn_ready = place.counter("xn_ready")
        xn_turned = place.counter("xn_turned")
        xnT_ready = place.counter("xnT_ready")
        h_ready = place.counter("h_ready")
        gelu_ready = place.counter("gelu_ready")
        hsq_ready = place.counter("hsq_ready")
        y_ready = place.counter("y_ready")
        s_ready = place.counter("s_ready")
        mean_ready = place.counter("mean_ready")
        root_h_ready = place.counter("root_h_ready")
        block = ctx.enter_context(nc.Block())

        @block.sync
        def _(sp):
            sp.dma_start(w[:, 0, :], m.dram["L3_ffn_w_up"]).then_inc(w_in.sem, 16)
            sp.dma_start(w[:, 1, :].rearrange("p (c d) -> p c d", c=FC), m.dram["L3_ffn_w_down"].rearrange("(c p) d -> p c d", p=P))\
              .then_inc(w_in.sem, 16)

        @block.vector
        def _(dve):
            dve.tensor_tensor(sq[:, :, :], m.X[:, :, :], m.X[:, :, :], ALU.mult)
            dve.drain()
            dve.tensor_reduce(rms[:, :], sq[:, :, :], AX.X, ALU.add).then_inc(square_ready.sem, 1)
            dve.wait_ge(w_in.sem, w_in.nth(32))
            for i in range(2):
                dve.tensor_reduce(sums[:, i:i + 1], w[:, i, :], AX.X, ALU.add, apply_absolute_value=True)\
                   .then_inc(sums_ready.sem, 1)
            dve.wait_ge(level_ready.sem, level_ready.nth(1))
            dve.tensor_scalar(level[:, 0, :], ps_level[:, 0:2], 0.5 / (F * D), None, ALU.mult)
            dve.tensor_scalar(level[:, 1, :], ps_level[:, 0:2], -0.5 / (F * D), None, ALU.mult)
            dve.drain()
            for i in range(2):
                dve.tensor_scalar(wq[:, i, :], w[:, i, :], level[:, 0, i:i + 1], None, ALU.is_gt)
                dve.tensor_scalar(small[:, :], w[:, i, :], level[:, 1, i:i + 1], None, ALU.is_lt)
                dve.drain()
                dve.tensor_tensor(wq[:, i, :], wq[:, i, :], small[:, :], ALU.subtract)
                dve.drain()
                dve.tensor_tensor(wq[:, i, :], wq[:, i, :], w[:, i, :], ALU.subtract)
                dve.drain()
                dve.tensor_tensor(wq[:, i, :], wq[:, i, :], w[:, i, :], ALU.add).then_inc(w_ready.sem, 1)
            dve.wait_ge(root_ready.sem, root_ready.nth(1))
            dve.tensor_scalar(rms[:, :], rms[:, :], 1e-8, None, ALU.add)
            dve.drain()
            dve.reciprocal(rms[:, :], rms[:, :])
            dve.drain()
            for t in range(NT):
                dve.tensor_scalar(sq[:, t, :], m.X[:, t, :], rms[:, t:t + 1], None, ALU.mult).then_inc(xn_ready.sem, 1)
            for half in range(2):
                dve.wait_ge(xn_turned.sem, xn_turned.nth(half + 1))
                dve.tensor_copy(xnT[:, half * BANK:(half + 1) * BANK], ps_x[:, half, :]).then_inc(xnT_ready.sem, 1)
            for n in range(2 * FC):
                half, f = n // FC, n % FC
                cols = slice(half * BANK, (half + 1) * BANK)
                dve.wait_ge(gelu_ready.sem, gelu_ready.nth(n + 1))
                dve.tensor_tensor(hsq[:, f, cols], hT[:, f, cols], hT[:, f, cols], ALU.mult).then_inc(hsq_ready.sem, 1)
            dve.wait_ge(s_ready.sem, s_ready.nth(1))
            dve.tensor_scalar(rms_h[:, :], ps_s[:, 0:NT], 1.0 / F, None, ALU.mult).then_inc(mean_ready.sem, 1)
            dve.wait_ge(root_h_ready.sem, root_h_ready.nth(1))
            dve.tensor_scalar(rms_h[:, :], rms_h[:, :], 1e-8, None, ALU.add)
            dve.drain()
            dve.reciprocal(rms_h[:, :], rms_h[:, :])
            dve.drain()
            for t in range(NT):
                dve.tensor_scalar(m.Y[:, t, :], ps_y[:, t // 4, (t % 4) * P:(t % 4 + 1) * P], rms_h[:, t:t + 1], None,
                                  ALU.mult)

        @block.scalar
        def _(act):
            act.wait_ge(square_ready.sem, square_ready.nth(1))
            act.activation(rms[:, :], rms[:, :], ACT.Sqrt, scale=1.0 / D).then_inc(root_ready.sem, 1)
            for n in range(2 * FC):
                half, f = n // FC, n % FC
                act.wait_ge(h_ready.sem, h_ready.nth(n + 1))
                act.activation(hT[:, f, half * BANK:(half + 1) * BANK], ps_h[:, n % 2, :], ACT.Gelu).then_inc(gelu_ready.sem, 1)
            act.wait_ge(mean_ready.sem, mean_ready.nth(1))
            act.activation(rms_h[:, :], rms_h[:, :], ACT.Sqrt).then_inc(root_h_ready.sem, 1)

        @block.tensor
        def _(pe):
            pe.wait_ge(sums_ready.sem, sums_ready.nth(2))
            pe.matmul(ps_level[:, 0:2], m.ones[:, :], sums[:, :], start=True, stop=True).then_inc(level_ready.sem, 1)
            for t in range(NT):
                pe.wait_ge(xn_ready.sem, xn_ready.nth(t + 1))
                mm = pe.transpose(ps_x[:, t // 4, (t % 4) * P:(t % 4 + 1) * P], sq[:, t, :], m.ident[:, :])
                if t % 4 == 3:
                    mm.then_inc(xn_turned.sem, 1)
            pe.wait_ge(w_ready.sem, w_ready.nth(2))
            for n in range(2 * FC):
                half, f = n // FC, n % FC
                pe.wait_ge(xnT_ready.sem, xnT_ready.nth(half + 1))
                if n >= 2:
                    pe.wait_ge(gelu_ready.sem, gelu_ready.nth(n - 1))
                pe.matmul(ps_h[:, n % 2, :], wq[:, 0, f * P:(f + 1) * P], xnT[:, half * BANK:(half + 1) * BANK],
                          start=True, stop=True).then_inc(h_ready.sem, 1)
            pe.wait_ge(hsq_ready.sem, hsq_ready.nth(2 * FC))
            for t in range(NT):
                tok = slice(t * P, (t + 1) * P)
                for f in range(FC):
                    pe.matmul(ps_y[:, t // 4, (t % 4) * P:(t % 4 + 1) * P], hT[:, f, tok], wq[:, 1, f * P:(f + 1) * P],
                              start=(f == 0), stop=(f == FC - 1))
                for f in range(FC):
                    mm = pe.matmul(ps_s[:, t:t + 1], hsq[:, f, tok], m.ones[:, 0:1], start=(f == 0), stop=(f == FC - 1))
            mm.then_inc(s_ready.sem, 1)


def transposed(a):
    return np.swapaxes(a, -1, -2)


def by_chunk(a):
    return transposed(a.reshape(*a.shape[:-1], -1, P))


LAYOUTS = {
    "L0_ffn_Wg": transposed, "L0_ffn_W1": transposed, "L0_ffn_W2": transposed, "L0_ffn_b1": by_chunk,
    "L1_ffn_b1": by_chunk,
    "L3_ffn_w_up": transposed, "L3_ffn_w_down": transposed,
    "L3_attn_Wr": transposed, "L3_attn_Wk": transposed, "L3_attn_Wv": transposed,
    "L3_attn_Ww": transposed, "L3_attn_Wo": transposed,
}


MASKED = np.float32(-2.0 ** 100)


def pad_heads(a, axis, to):
    pad = [(0, 0)] * a.ndim
    pad[axis] = (0, to - a.shape[axis])
    return np.pad(a, pad)


def attention_layout(wq, wk, wv, wo, heads, bq=None, bk=None, bv=None, q_scale=None, k_scale=None):
    n, d, dh = wq.shape
    groups, stride = n // heads, P // heads
    zero = np.zeros((n, dh), np.float32)

    def side(a):
        a = pad_heads(a, 2, stride)
        return a.reshape(groups, heads, D, stride).transpose(0, 2, 1, 3).reshape(groups, D, P)

    def column(a):
        return pad_heads(a, 1, stride).reshape(groups, P, 1)

    values = wv.reshape(groups, heads, D, dh).transpose(0, 2, 1, 3).reshape(groups, D, heads * dh)
    columns = [column(zero if a is None else np.broadcast_to(a.reshape(-1, dh), (n, dh))) for a in (bq, bk, q_scale, k_scale)]
    out = {"w": np.concatenate([side(wq), side(wk), values] + columns, axis=2), "wo": wo.reshape(groups, heads * dh, D)}
    if bv is not None:
        out["bv"] = bv.reshape(groups, heads * dh)
    return out


def per_head(w):
    return w.reshape(D, 16, -1).transpose(1, 0, 2)


def attention_inputs(x):
    made = {}

    def put(name, **arrays):
        made.update({f"{name}_{k}": v for k, v in arrays.items()})

    w = x["L1_attn_w_qkv"]
    bias = x["L1_attn_b_qkv"].reshape(3, 16, 8)
    put("L1_attn", **attention_layout(per_head(w[:, 0:D]), per_head(w[:, D:2 * D]), per_head(w[:, 2 * D:]),
                                      x["L1_attn_w_out"], 4, bias[0], bias[1], bias[2]))
    i, j = np.arange(T)[:, None], np.arange(T)[None, :]
    open_ = (j % 32 == 0) | (np.abs(i - j) <= 64)
    put("L1_attn", mask=by_tile(np.where(open_, np.float32(0), MASKED)))
    put("L3_xattn1", mask=by_tile(np.where(j <= i, np.float32(0), MASKED)))
    for n in "12":
        v = [x[f"L3_xattn_{k}{n}"] for k in ("Wq", "Wk", "Wv", "Wo", "bq", "bk", "bv")]
        put("L3_xattn" + n, **attention_layout(v[0], v[1], v[2], v[3], 4, v[4], v[5], v[6]))
    kv = x["L1_xattn_Wkv"]
    put("L1_xattn", **attention_layout(per_head(x["L1_xattn_Wq"]), per_head(kv[:, 0:1024]), per_head(kv[:, 1024:]),
                                       x["L1_xattn_Wout"], 2, q_scale=x["L1_xattn_q_scale"], k_scale=x["L1_xattn_k_scale"]))
    null = x["L1_xattn_null_kv"]
    put("L1_xattn", null_k=np.tile(null[0], 2).reshape(P, 1), null_v=np.tile(null[1], 2).reshape(1, P))
    v = [x[f"L2_xattn_{k}"] for k in ("Wq", "Wk", "Wv", "Wo", "bq", "bk", "bv")]
    put("L2_xattn", **attention_layout(v[0].T[None], v[1].T[None], v[2].T[None], v[3].T[None], 1, v[4], v[5], v[6]))
    one = np.eye(D, dtype=np.float32)
    diagonal = np.zeros((D, D), np.float32)
    diagonal[np.arange(D), np.arange(D)] = x["L0_xattn_w_cq"]
    put("L0_xattn", **attention_layout(diagonal[None], one[None], one[None], one[None], 1, x["L0_xattn_w_q"],
                                       None, np.zeros((1, D), np.float32)))
    made["L0_xattn_b"] = np.concatenate([x[f"L0_xattn_b_{k}"].reshape(1, 1) for k in ("cq", "c", "q")], axis=1)
    made["L0_xattn_W_l"] = x["L0_xattn_W_l"].T.reshape(4, D, D).transpose(1, 0, 2)
    made["L2_ffn_mask"] = by_tile(np.where((j <= i) & (i - j <= 32), np.float32(0), MASKED))
    layers = []
    for n in range(6):
        kqv = x["L2_ffn_Wqkv"][n]
        layers.append(attention_layout(per_head(kqv[:, 0:1024]), per_head(kqv[:, 1024:2048]), per_head(kqv[:, 2048:]),
                                       x["L2_ffn_Wo"][n], 2, q_scale=x["L2_ffn_q_scale"][n], k_scale=x["L2_ffn_k_scale"][n]))
    put("L2_ffn", **{k: np.concatenate([a[k] for a in layers]) for k in ("w", "wo")})
    F, FP = 341, 384

    def pad(a, axis):
        width = [(0, 0)] * a.ndim
        width[axis] = (0, FP - F)
        return np.pad(a, width)

    w1, b1 = x["L2_ffn_W1"], x["L2_ffn_b1"]
    sides = [pad(w1[..., :F], 2), pad(w1[..., F:], 2)]
    columns = [by_chunk(pad(b1[:, :F], 1)), by_chunk(pad(b1[:, F:], 1))] + [x[f"L2_ffn_{k}"][:, :, None] for k in ("ln_g", "ln_b", "b2")]
    made["L2_ffn_up"] = np.concatenate(sides + columns, axis=2)
    made["L2_ffn_down"] = pad(x["L2_ffn_W2"], 1).reshape(6, 3, P, D).transpose(0, 2, 1, 3)
    made["L0_attn_proj"] = np.stack([x["L0_attn_Wq"].T, x["L0_attn_Wk"].T, x["L0_attn_Wv"].T,
                                     np.repeat(x["L0_attn_Wb"], 32, axis=0).T], axis=1)
    made["L0_attn_taps"] = np.concatenate([x[f"L0_attn_conv_{k}"] for k in "qkv"] +
                                          [x[f"L0_attn_fir_{k}"].reshape(D, -1) for k in "sml"], axis=1)
    made["L0_attn_gate"] = x["L0_attn_gate_w"].reshape(20, D).T
    made["L0_attn_WoT"] = x["L0_attn_Wo"].T
    made["L0_attn_row"] = np.concatenate([x[f"L0_attn_{k}"].reshape(1, -1) for k in ("gate_b", "log_temp", "eps_param", "norm_w")],
                                         axis=1)
    def blocks(w, n):
        r, c = w.shape
        out = np.zeros((n, r, n, c), np.float32)
        out[np.arange(n), :, np.arange(n), :] = w
        return out.reshape(n * r, n * c)

    made["L2_attn_blocks"] = np.stack([blocks(x["L2_attn_W_strain"], 8), blocks(x["L2_attn_W_dmg"], 8)], axis=1)
    made["L2_attn_out8"] = np.stack([blocks(x["L2_attn_W_bond"], 8), blocks(x["L2_attn_W_dmg_out"], 8)], axis=1)
    made["L2_attn_pos8"] = np.tile(x["L2_attn_W_pos"], (1, 8))
    made["L2_attn_rel_T"] = x["L2_attn_rel_pos_emb"].T
    made["L2_attn_b_dmg8"] = np.tile(x["L2_attn_b_dmg"], 8).reshape(P, 1)
    t, j = np.arange(P)[:, None], np.arange(64)[None, :]
    made["L2_attn_mask"] = np.where(t - 63 + j >= 0, np.float32(0), MASKED)
    jj, p, q = np.arange(8)[None, :, None], np.arange(P)[:, None, None], np.arange(P)[None, None, :]
    made["L2_attn_spread"] = ((p // 16 == jj) & (p % 16 == q // 8)).astype(np.float32)
    return made


def by_tile(mask):
    return mask.reshape(TB, P, -1).transpose(1, 0, 2)


def constants():
    i = np.arange(P)
    half = np.arange(0, 64, 2, dtype=np.float32)
    inv_freq = (1.0 / 10000.0 ** (half / 64)).astype(np.float32)
    freqs = np.arange(T, dtype=np.float32)[:, None] * inv_freq[None, :]
    base = ((half + 0.4 * 64) / (1.4 * 64)).astype(np.float64)
    scale = base[None, :] ** ((np.arange(T) - T // 2) / 16)[:, None]
    freqs, scale = np.tile(freqs, (1, 4)).T, np.tile(scale, (1, 4)).T
    cos, sin = np.cos(freqs.astype(np.float64)), np.sin(freqs.astype(np.float64))
    rotation = np.zeros((P, P), np.float32)
    for h in range(2):
        k = np.arange(32)
        rotation[64 * h + 32 + k, 64 * h + k] = -1.0
        rotation[64 * h + k, 64 * h + 32 + k] = 1.0
    below = []
    r, c = i[:, None], i[None, :]
    for s in (1, 2, 4, 8, 16):
        low = (r // (2 * s) == c // (2 * s)) & (r // s % 2 == 1) & (c // s % 2 == 0)
        below += [-low.astype(np.float32), -low.T.astype(np.float32)]
    return {
        "c_below": np.stack(below, axis=1),
        "c_causal32": ((r // 32 == c // 32) & (r <= c)).astype(np.float32),
        "c_same_head32": (r // 32 == c // 32).astype(np.float32),
        "c_cos": np.concatenate([cos / scale, cos * scale], axis=1).astype(np.float32),
        "c_sin": np.concatenate([sin / scale, sin * scale], axis=1).astype(np.float32),
        "c_rotation": rotation,
        "c_ident": np.eye(P, dtype=np.float32),
        "c_same_head8": (i[:, None] // 8 == i[None, :] // 8).astype(np.float32),
        "c_same_head64": (i[:, None] // 64 == i[None, :] // 64).astype(np.float32),
        "c_number": np.broadcast_to(i, (P, P)).astype(np.float32),
    }


SUBLAYERS = [gated_delta, bidaf, moe_0, sparse_attention, cosine_cross, moe_1, peridynamic, top_k_cross,
             local_transformer, linear_recurrence, double_mha, ternary_ffn]


def program(nc, dram):
    with ExitStack() as ctx:
        m = Model(nc, ctx, dram)
        load_model(m)
        for i, sublayer in enumerate(SUBLAYERS):
            sublayer(m)
            post_norm(m, last=(i == len(SUBLAYERS) - 1))


def kernel(**inputs):
    import concourse.bacc as bacc
    from concourse.bass_utils import run_bass_kernel_spmd

    nc = bacc.Bacc("TRN2", target_bir_lowering=False, num_devices=1)
    laid_out = {name: np.asarray(a) for name, a in inputs.items()}
    for name, layout in LAYOUTS.items():
        laid_out[name] = layout(laid_out[name])
    laid_out.update(attention_inputs(laid_out))
    laid_out["ctx_T"] = transposed(laid_out["ctx_1024"])
    laid_out.update(constants())
    arrays, dram = {}, {}
    for name, a in laid_out.items():
        a = np.ascontiguousarray(a)
        arrays[f"in_{name}"] = a
        dram[name] = nc.dram_tensor(f"in_{name}", a.shape, mybir.dt.from_np(a.dtype), kind="ExternalInput").ap()
    dram["out"] = nc.dram_tensor("out", (B, T, D), F32, kind="ExternalOutput").ap()
    program(nc, dram)
    r = run_bass_kernel_spmd(nc, [arrays], core_ids=[0])
    return r.results[0]["out"]
```

```python
from contextlib import ExitStack

import numpy as np

import concourse.bass as bass
from concourse import mybir

F32 = mybir.dt.float32
U32 = mybir.dt.uint32
ALU = mybir.AluOpType
ACT = mybir.ActivationFunctionType
AX = mybir.AxisListType

P = 128
B = 4
T = 256
D = 128
NT = B * T // P
TB = T // P
S = 1601
BANK = 512


class Counter:

    def __init__(self, place, name, per=1, ahead=0):
        self.sem = place.semaphore(name)
        self.per, self.ahead = per, ahead

    def nth(self, n, it=0):
        return it * self.per + (n + self.ahead)


class Place:

    count = 0

    def __init__(self, nc, ctx, name):
        Place.count += 1
        self.nc, self.ctx, self.name = nc, ctx, f"{name}{Place.count}"
        self.semaphores = []
        ctx.callback(self.close)

    def close(self):
        if self.semaphores:
            self.nc.clear_and_free_semaphores(self.semaphores)
            self.nc.all_engine_barrier()

    def sbuf(self, name, shape, dt=F32):
        return self.ctx.enter_context(self.nc.sbuf_tensor(f"{self.name}_{name}", shape, dt))

    def psum(self, name, shape, dt=F32):
        return self.ctx.enter_context(self.nc.psum_tensor(f"{self.name}_{name}", shape, dt))

    def semaphore(self, name):
        self.semaphores.append(self.nc.alloc_semaphore(f"{self.name}_{name}"))
        return self.semaphores[-1]

    def counter(self, name, per=1, ahead=0):
        return Counter(self, name, per, ahead)


class Model:

    def __init__(self, nc, ctx, dram):
        place = Place(nc, ctx, "model")
        self.nc, self.dram = nc, dram
        self.X = place.sbuf("X", [P, NT, D])
        self.XT = place.sbuf("XT", [P, B * T])
        self.Y = place.sbuf("Y", [P, NT, D])
        self.ident = place.sbuf("ident", [P, P])
        self.ones = place.sbuf("ones", [P, P])


def load_model(m):
    nc = m.nc
    with ExitStack() as ctx:
        place = Place(nc, ctx, "load")
        loaded = place.counter("loaded")
        turned = place.counter("turned")
        ps = place.psum("ps", [P, NT * P])
        block = ctx.enter_context(nc.Block())

        @block.sync
        def _(sp):
            sp.dma_start(m.X[:, :, :], m.dram["x"].rearrange("b (u p) d -> p (b u) d", p=P)).then_inc(loaded.sem, 16)
            sp.dma_start(m.ident[:, :], m.dram["c_ident"]).then_inc(loaded.sem, 16)

        @block.gpsimd
        def _(pool):
            pool.memset(m.ones[:, :], 1.0)

        @block.tensor
        def _(pe):
            pe.wait_ge(loaded.sem, loaded.nth(32))
            for t in range(NT):
                mm = pe.transpose(ps[:, t * P:(t + 1) * P], m.X[:, t, :], m.ident[:, :])
            mm.then_inc(turned.sem, 1)

        @block.vector
        def _(dve):
            dve.wait_ge(turned.sem, turned.nth(1))
            dve.tensor_copy(m.XT[:, :], ps[:, :])


def post_norm(m, last=False):
    nc = m.nc
    with ExitStack() as ctx:
        place = Place(nc, ctx, "norm")
        stats = place.sbuf("stats", [P, NT, 6])
        mv = place.sbuf("mv", [P, NT, 2])
        rstd = place.sbuf("rstd", [P, NT])
        ps = place.psum("ps", [P, NT * P])
        var_ready = place.counter("var_ready")
        root_ready = place.counter("root_ready")
        x_ready = place.counter("x_ready")
        turned = place.counter("turned")
        stored = place.counter("stored")
        block = ctx.enter_context(nc.Block())

        @block.vector
        def _(dve):
            dve.tensor_tensor(m.Y[:, :, :], m.Y[:, :, :], m.X[:, :, :], ALU.add)
            dve.drain()
            for t in range(NT):
                dve.bn_stats(stats[:, t, :], m.Y[:, t, :])
            dve.drain()
            for t in range(NT):
                dve.bn_aggr(mv[:, t, :], stats[:, t, :])
            dve.drain()
            dve.tensor_scalar(rstd[:, :], mv[:, :, 1], 1e-5, None, ALU.add).then_inc(var_ready.sem, 1)
            dve.wait_ge(root_ready.sem, root_ready.nth(1))
            dve.reciprocal(rstd[:, :], rstd[:, :])
            dve.drain()
            for t in range(NT):
                dve.tensor_scalar(m.X[:, t, :], m.Y[:, t, :], mv[:, t, 0:1], rstd[:, t:t + 1],
                                  ALU.subtract, ALU.mult).then_inc(x_ready.sem, 1)
            if not last:
                for half in range(2):
                    dve.wait_ge(turned.sem, turned.nth(half + 1))
                    dve.tensor_copy(m.XT[:, half * BANK:(half + 1) * BANK], ps[:, half * BANK:(half + 1) * BANK])

        @block.scalar
        def _(act):
            act.wait_ge(var_ready.sem, var_ready.nth(1))
            act.activation(rstd[:, :], rstd[:, :], ACT.Sqrt).then_inc(root_ready.sem, 1)

        if last:
            @block.sync
            def _(sp):
                sp.wait_ge(x_ready.sem, x_ready.nth(NT))
                sp.dma_start(m.dram["out"].rearrange("b (u p) d -> p (b u) d", p=P), m.X[:, :, :])\
                  .then_inc(stored.sem, 16)
                sp.wait_ge(stored.sem, stored.nth(16))
        else:
            @block.tensor
            def _(pe):
                for t in range(NT):
                    pe.wait_ge(x_ready.sem, x_ready.nth(t + 1))
                    mm = pe.transpose(ps[:, t * P:(t + 1) * P], m.X[:, t, :], m.ident[:, :])
                    if t % 4 == 3:
                        mm.then_inc(turned.sem, 1)


class Heads:

    def __init__(self, name, keys, heads, stride, dv, scale=1.0, context=False, biased=False, cosine=False, masked=False,
                 n_heads=16, choose=0, rotary=False, null=False, reach=None):
        self.name, self.keys, self.heads, self.stride, self.dv = name, keys, heads, stride, dv
        self.scale, self.context, self.biased, self.cosine, self.masked = scale, context, biased, cosine, masked
        self.groups = n_heads // heads
        self.rotary, self.null = rotary, null
        self.choose = choose
        self.reach = reach or [(0, keys)] * TB


def attention(m, a, xT, accT, neg_max_out=None, layer=0, add=False):
    nc = m.nc
    K = a.keys
    real = S if a.context else T
    KC = -(-K // P)
    W = K + T
    pieces = [(c, min(c + BANK, W)) for c in range(0, W, BANK)]
    NP = len(pieces)
    GC = a.heads * a.dv
    v_turn = BANK // GC
    v_turns = [(c, min(c + v_turn, KC)) for c in range(0, KC, v_turn)]
    per_turn = 4 if K > BANK else 2

    def turns(t):
        last = -(-a.reach[t][1] // P)
        return [(c, min(c + per_turn, last)) for c in range(0, last, per_turn)]

    U = a.heads * TB
    G = len(turns(0))
    assert G == len(turns(TB - 1))
    ring = [("turn", u, j) for u in range(U) for j in range(G)]
    ring.insert(2, ("turn_inverse", 0, None))
    ring.insert(4, ("final", 0, None))
    R = len(ring)
    WC = 2 * P + GC + 4
    BQ, BK, QS, KS = (slice(2 * P + GC + i, 2 * P + GC + i + 1) for i in range(4))
    score_bufs = 1 if K > BANK else 2
    AHEAD = score_bufs
    sign = -1.0 if a.masked else 1.0

    ACT_TAKES, DVE_TAKES = 0, 1
    projects = [("project", n, DVE_TAKES if c1 > K and not (a.cosine and real == K) else ACT_TAKES) for n, (c0, c1) in enumerate(pieces)]
    values = [("value", i, ACT_TAKES) for i in range(len(v_turns))]
    early = 1 if a.cosine else 0
    if a.cosine:
        prepare = [("scale", n, None) for n in range(NP)]
        if a.rotary:
            prepare.append(("rotate", 0, DVE_TAKES))
        for n in range(max(NP + 2, len(values))):
            prepare += projects[n:n + 1] + values[n:n + 1]
            if 1 <= n <= NP:
                prepare.append(("sum", n - 1, DVE_TAKES))
            if 2 <= n <= NP + 1:
                prepare.append(("root", n - 2, None))
    else:
        prepare = projects + values
    starts = ("project", "sum", "root") if a.cosine else ()
    uses = [e for e in prepare if e[2] is not None]
    NU = len(uses)
    place_of = {e[:2]: i for i, e in enumerate(uses)}
    rank = [sum(e[2] == uses[i][2] for e in uses[:i + 1]) for i in range(NU)]
    n_taken = [sum(e[2] == k for e in uses) for k in (ACT_TAKES, DVE_TAKES)]
    last_read = uses.index(values[-1])

    taker = [ACT_TAKES if e[2] == 0 else DVE_TAKES for e in ring]
    ring_rank = [taker[:i + 1].count(taker[i]) for i in range(R)]
    n_out = [taker.count(k) for k in (ACT_TAKES, DVE_TAKES)]

    def attend_plan():
        plan = [("invert", 0, None)]
        for u in range(U):
            if AHEAD == 1:
                plan.append(("scores", u + 1, None))
            for j in range(G):
                plan.append(("turn", u, j))
                if (u, j) == ring[1][1:]:
                    plan.append(("turn_inverse", 0, None))
                if (u, j) == ring[3][1:]:
                    plan.append(("final", 0, None))
                if j == 0 and AHEAD == 2:
                    plan.append(("scores", u + 2, None))
                if j == min(1, G - 1):
                    plan.append(("exp", u + 1, None))
                if j >= 1:
                    plan.append(("times", u, j - 1))
            plan.append(("times", u, G - 1))
            plan.append(("out", u, None))
        needed = plan.index(("scores", U, None))
        room = (len(plan) if a.cosine else needed) - 2
        spread = [[] for _ in plan]
        for k, e in enumerate(prepare):
            spread[2 + k * room // len(prepare)].append(e)
            assert e[0] not in ("scale", "rotate") or 2 + k * room // len(prepare) < needed
        return [e for p, more in zip(plan, spread) for e in more + [p]]

    plan = attend_plan()
    before = list(prepare) + [("scores", U + i, None) for i in range(AHEAD)] + [("exp", U, None)]
    rounds = [(e, s) for s in range(-1 - early, 0) for e in (before if s == -1 else prepare)]
    after = [("invert", 0, None), ("turn_inverse", 0, None), ("skip", 0, None), ("final", 0, None)]

    with ExitStack() as ctx:
        place = Place(nc, ctx, "heads")
        source = place.sbuf("source", [P, 2, real]) if a.context else None
        w = place.sbuf("w", [P, 2, WC])
        wo = place.sbuf("wo", [P, D])
        bv = place.sbuf("bv", [1, 2, GC]) if a.biased else None
        KQ = place.sbuf("KQ", [P, 2, W])
        raw = place.sbuf("raw", [P, W]) if a.cosine else None
        squares = place.sbuf("squares", [P, W]) if a.cosine else None
        together = place.sbuf("together", [P, P]) if a.cosine else None
        mask = place.sbuf("mask", [P, TB, K]) if a.masked else None
        masked = place.sbuf("masked", [P, 2, K]) if a.masked else None
        rotation = place.sbuf("rotation", [P, P]) if a.rotary else None
        cos = place.sbuf("cos", [P, W]) if a.rotary else None
        sin = place.sbuf("sin", [P, W]) if a.rotary else None
        cos_part = place.sbuf("cos_part", [P, W]) if a.rotary else None
        V = place.sbuf("V", [P, 2, KC, GC])
        probs = place.sbuf("probs", [P, 2, KC * P])
        probsT = place.sbuf("probsT", [P, 2, KC * P])
        neg_max = place.sbuf("neg_max", [P, 2])
        total = place.sbuf("total", [P, 2, U])
        inv = place.sbuf("inv", [P, U])
        rest = place.sbuf("rest", [P, K]) if a.choose else None
        top = place.sbuf("top", [P, 2, 8]) if a.choose else None
        inverse = place.sbuf("inverse", [P, TB, P])
        OT = place.sbuf("OT", [P, 2, T])
        divided = place.sbuf("divided", [P, T])
        ps_s = place.psum("ps_s", [P, 4 * BANK])
        ps_r = place.psum("ps_r", [P, 2, BANK])
        ps_p = place.psum("ps_p", [P, BANK])
        ps_o = place.psum("ps_o", [P, BANK])

        ONCE = 16 * (a.cosine + 3 * a.rotary + 3 * a.null + a.masked)
        once_in = place.counter("once_in")
        cleared = place.counter("cleared")
        LOADS = 16 * (1 + a.context + a.biased)
        loaded = [place.counter(f"loaded_{k}", per=LOADS) for k in range(2)]
        wo_in = place.counter("wo_in", per=16)
        source_read = place.counter("source_read", ahead=early)
        spent = place.counter("spent")
        prepared = place.counter("prepared", per=NU, ahead=early * NU)
        taken = [place.counter(f"taken_{k}", per=n_taken[k], ahead=(1 + early) * n_taken[k]) for k in (ACT_TAKES, DVE_TAKES)]
        squared = place.counter("squared", per=NP, ahead=NP)
        rooted = place.counter("rooted", per=NP, ahead=NP)
        scaled = place.counter("scaled", per=NP, ahead=NP)
        roped = place.counter("roped", ahead=1)
        cos_ready = place.counter("cos_ready")
        scores_ready = place.counter("scores_ready", per=U, ahead=U)
        max_ready = place.counter("max_ready", per=U, ahead=U)
        probs_ready = place.counter("probs_ready", per=U, ahead=U)
        chosen = place.counter("chosen", per=U, ahead=U) if a.choose else probs_ready
        turned = place.counter("turned", per=R, ahead=R)
        taken_out = [place.counter(f"taken_out_{k}", per=n_out[k], ahead=n_out[k]) for k in (ACT_TAKES, DVE_TAKES)]
        out_ready = place.counter("out_ready", per=U, ahead=U)
        out_taken = place.counter("out_taken", per=U, ahead=U)
        inverted = place.counter("inverted", ahead=1)
        block = ctx.enter_context(nc.Block())
        scores_read = max_ready if a.masked else probs_ready
        first_col = [0, 0] if score_bufs == 1 else [0, BANK]

        def ring_of(u, j, kind="turn"):
            return ring.index((kind, u, j))

        def emptied(i):
            k = taker[i]
            return taken_out[k], ring_rank[i] - (n_out[k] if i < 0 else 0)

        last_turned = [ring_of(u, G - 1) + 1 for u in range(U)]
        turned_inverse, finished = ring_of(0, None, "turn_inverse"), ring_of(0, None, "final")

        def total_of(u, b):
            return total[:, (b + u // U) % 2, u % U:u % U + 1]

        def rows_of(h):
            return slice(h * a.stride, h * a.stride + a.dv)

        def use_taken(i):
            k = uses[i][2]
            return taken[k], rank[i] - (n_taken[k] if i < 0 else 0)

        @block.sync
        def _(sp):
            if a.cosine:
                sp.dma_start(together[:, :], m.dram["c_same_head64"]).then_inc(once_in.sem, 16)
            if a.rotary:
                sp.dma_start(rotation[:, :], m.dram["c_rotation"]).then_inc(once_in.sem, 16)
                sp.dma_start(cos[:, :], m.dram["c_cos"]).then_inc(once_in.sem, 16)
                sp.dma_start(sin[:, :], m.dram["c_sin"]).then_inc(once_in.sem, 16)
            if a.masked:
                sp.dma_start(mask[:, :, :], m.dram[a.name + "_mask"]).then_inc(once_in.sem, 16)

            def load(row, batch, k):
                sp.dma_start(w[:, k, :], m.dram[a.name + "_w"][bass.ds(row, 1), :, :].rearrange("g p c -> (g p) c"))\
                  .then_inc(loaded[k].sem, 16)
                if a.context:
                    sp.dma_start(source[:, k, :], m.dram["ctx_T"][batch]).then_inc(loaded[k].sem, 16)
                if a.biased:
                    sp.dma_start(bv[:, k, :], m.dram[a.name + "_bv"][bass.ds(row, 1), :]).then_inc(loaded[k].sem, 16)

            rows = layer * (a.groups + 1)
            sp.dma_start(wo[:, :], m.dram[a.name + "_wo"][bass.ds(rows, 1), :, :].rearrange("g c d -> (g c) d"))\
              .then_inc(wo_in.sem, 16)
            load(rows, 0, 0)
            load(rows, 1, 1)
            if a.null:
                sp.dma_start(raw[:, real:K], m.dram[a.name + "_null_k"]).then_inc(once_in.sem, 16)
                sp.wait_ge(cleared.sem, cleared.nth(1))
                for k in range(2):
                    sp.dma_start(V[real % P:real % P + 1, k, KC - 1, :], m.dram[a.name + "_null_v"]).then_inc(once_in.sem, 16)
            with sp.Fori(0, a.groups) as g:
                for b in range(B):
                    step = g * B + b
                    sp.wait_ge(source_read.sem, source_read.nth(1, step))
                    sp.sem_inc(spent.sem, 1)
                    sp.wait_ge(taken[0].sem, taken[0].nth(n_taken[0], step))
                    sp.sem_inc(spent.sem, 1)
                    sp.wait_ge(taken[1].sem, taken[1].nth(n_taken[1], step))
                    sp.sem_inc(spent.sem, 1)
                    if a.cosine:
                        sp.wait_ge(scaled.sem, scaled.nth(NP, step))
                        sp.sem_inc(spent.sem, 1)
                    load(rows + g + (b + 2) // B, (b + 2) % B, b % 2)
                    if b == 0:
                        sp.wait_ge(turned.sem, turned.nth(finished + 1, g * B))
                        sp.dma_start(wo[:, :], m.dram[a.name + "_wo"][bass.ds(rows + g, 1), :, :].rearrange("g c d -> (g c) d"))\
                          .then_inc(wo_in.sem, 16)
            for k in range(2):
                sp.wait_ge(loaded[k].sem, loaded[k].nth(LOADS, a.groups * B // 2))

        if a.cosine:
            @block.gpsimd
            def _(pool):
                def prepare_step(q, k):
                    if a.rotary and k is not None:
                        pool.wait_ge(scaled.sem, scaled.nth(NP, q))
                        pool.wait_ge(roped.sem, roped.nth(0, q))
                        pool.tensor_tensor(cos_part[:, :], KQ[:, k, :], cos[:, :], ALU.mult).then_inc(cos_ready.sem, 1)
                    if a.rotary:
                        pool.wait_ge(roped.sem, roped.nth(1, q))
                    for n, (c0, c1) in enumerate(pieces):
                        side, nth = use_taken(place_of["project", n])
                        pool.wait_ge(side.sem, side.nth(nth, q))
                        pool.tensor_tensor(squares[:, c0:c1], raw[:, c0:c1], raw[:, c0:c1], ALU.mult)\
                            .then_inc(squared.sem, 1)

                pool.wait_ge(once_in.sem, ONCE)
                prepare_step(-1, None)
                prepare_step(0, 0)
                with pool.Fori(0, a.groups) as g:
                    for b in range(B):
                        prepare_step(g * B + b + 1, (b + 1) % 2)

        @block.tensor
        def _(pe):
            pe.sem_inc(turned.sem, turned.ahead)
            pe.sem_inc(out_ready.sem, out_ready.ahead)
            pe.sem_inc(scores_ready.sem, scores_ready.ahead)
            if ONCE:
                pe.wait_ge(once_in.sem, ONCE)

            def event(kind, u, j, s, b, g):
                lead = 2 if kind in starts else 1
                k = (b + lead) % 2
                nb = (b + lead) % B
                if (kind, u) in place_of:
                    i = place_of[kind, u]
                    src = source[:, k, :] if a.context else xT[:, nb * T:(nb + 1) * T]
                    if (kind, u) == ("project", 0):
                        n_loads = (s + lead - k) // 2 if isinstance(s, int) else g * (B // 2) + (b + lead - k) // 2
                        pe.wait_ge(loaded[k].sem, loaded[k].nth(LOADS, n_loads))
                    side, nth = use_taken(i - 1)
                    pe.wait_ge(side.sem, side.nth(nth, s + 1))
                if isinstance(s, int) and s == -2 and kind not in starts:
                    if kind in ("value", "rotate"):
                        pe.drain().then_inc(prepared.sem, 1)
                        if i == last_read:
                            pe.drain().then_inc(source_read.sem, 1)
                    return
                if kind == "project":
                    c0, c1 = pieces[u]
                    if c0 < real:
                        c = min(c1, real)
                        mm = pe.matmul(ps_p[:, 0:c - c0], w[:, k, P:2 * P], src[:, c0:c], start=True, stop=True)
                    if c1 > K:
                        mm = pe.matmul(ps_p[:, K - c0:W - c0], w[:, k, 0:P], xT[:, nb * T:(nb + 1) * T], start=True, stop=True)
                    mm.then_inc(prepared.sem, 1)
                elif kind == "value":
                    c0, c1 = v_turns[u]
                    for c in range(c0, c1):
                        n = min(P, real - c * P)
                        out = ps_p[0:n, (c - c0) * GC:(c - c0 + 1) * GC]
                        mm = pe.matmul(out, src[:, c * P:c * P + n], w[:, k, 2 * P:2 * P + GC], start=True, stop=not a.biased)
                        if a.biased:
                            mm = pe.matmul(out, m.ones[0:1, 0:n], bv[:, k, :], start=False, stop=True)
                    mm.then_inc(prepared.sem, 1)
                    if i == last_read:
                        pe.drain().then_inc(source_read.sem, 1)
                elif kind == "sum":
                    c0, c1 = pieces[u]
                    pe.wait_ge(squared.sem, squared.nth(u + 1, s + 1))
                    pe.matmul(ps_p[:, 0:c1 - c0], together[:, :], squares[:, c0:c1], start=True, stop=True).then_inc(prepared.sem, 1)
                elif kind == "rotate":
                    pe.wait_ge(scaled.sem, scaled.nth(NP, s + 1))
                    pe.matmul(ps_p[:, 0:W], rotation[:, :], KQ[:, k, :], start=True, stop=True).then_inc(prepared.sem, 1)
                elif kind == "scores":
                    h, t = u % U // TB, u % TB
                    at = b % 2 if u < U else k
                    if u == U:
                        if not a.cosine:
                            for n in range(NP):
                                if n == NP - 1 or projects[n + 1][2] != projects[n][2]:
                                    side, nth = use_taken(place_of["project", n])
                                    pe.wait_ge(side.sem, side.nth(nth, s + 1))
                        if a.cosine:
                            pe.wait_ge(scaled.sem, scaled.nth(NP, s + 1))
                        if a.rotary:
                            pe.wait_ge(roped.sem, roped.nth(1, s + 1))
                    part = slice(h * a.stride, (h + 1) * a.stride)
                    pe.wait_ge(scores_read.sem, scores_read.nth(u + 1 - score_bufs, s))
                    lo, hi = a.reach[t]
                    for c0 in range(lo, hi, BANK):
                        c1 = min(c0 + BANK, hi)
                        mm = pe.matmul(ps_s[:, first_col[u % 2] + c0:first_col[u % 2] + c1],
                                       KQ[part, at, K + t * P:K + (t + 1) * P], KQ[part, at, c0:c1], start=True, stop=True)
                    mm.then_inc(scores_ready.sem, 1)
                elif kind == "turn":
                    i = ring_of(u, j)
                    if j == 0:
                        pe.wait_ge(chosen.sem, chosen.nth(u + 1, s))
                    side, nth = emptied(i - 2)
                    pe.wait_ge(side.sem, side.nth(nth, s))
                    c0, c1 = turns(u % TB)[j]
                    for c in range(c0, c1):
                        mm = pe.transpose(ps_r[:, i % 2, (c - c0) * P:(c - c0 + 1) * P], probs[:, u % 2, c * P:(c + 1) * P],
                                          m.ident[:, :])
                    mm.then_inc(turned.sem, 1)
                elif kind == "times":
                    i, h = ring_of(u, j), u // TB
                    if (u, j) == (0, 0):
                        side, nth = use_taken(place_of["value", len(v_turns) - 1])
                        pe.wait_ge(side.sem, side.nth(nth, s))
                    if j == 0:
                        pe.wait_ge(out_taken.sem, out_taken.nth(u, s))
                    side, nth = emptied(i)
                    pe.wait_ge(side.sem, side.nth(nth, s))
                    c0, c1 = turns(u % TB)[j]
                    last = turns(u % TB)[-1][1]
                    for c in range(c0, c1):
                        mm = pe.matmul(ps_o[rows_of(h), 0:P], V[:, b % 2, c, h * a.dv:(h + 1) * a.dv],
                                       probsT[:, u % 2, c * P:(c + 1) * P], start=(c == 0), stop=(c == last - 1))
                    if j == G - 1:
                        mm.then_inc(out_ready.sem, 1)
                elif kind == "turn_inverse":
                    i = turned_inverse
                    pe.wait_ge(inverted.sem, inverted.nth(1, s))
                    side, nth = emptied(i - 2)
                    pe.wait_ge(side.sem, side.nth(nth, s))
                    for t in range(TB):
                        mm = pe.transpose(ps_r[:, i % 2, t * P:(t + 1) * P], inverse[:, t, :], m.ident[:, :])
                    mm.then_inc(turned.sem, 1)
                elif kind == "final":
                    i = finished
                    if b == 1:
                        pe.wait_ge(wo_in.sem, wo_in.nth(32, g))
                    side, nth = emptied(turned_inverse)
                    pe.wait_ge(side.sem, side.nth(nth, s))
                    pe.matmul(ps_r[:, i % 2, 0:T], wo[:, :], divided[:, :], start=True, stop=True).then_inc(turned.sem, 1)

            pe.wait_ge(cleared.sem, cleared.nth(1))
            pe.wait_ge(wo_in.sem, wo_in.nth(16))
            for (kind, u, j), s in rounds:
                event(kind, u, j, s, s, 0)
            with pe.Fori(0, a.groups) as g:
                for b in range(B):
                    for kind, u, j in plan:
                        event(kind, u, j, g * B + b, b, g)
            pe.drain().then_inc(turned.sem, turned_inverse)
            for kind, u, j in after:
                if kind == "skip":
                    pe.drain().then_inc(turned.sem, 1)
                event(kind, u, j, a.groups * B, 0, 0)

        @block.scalar
        def _(act):
            act.sem_inc(probs_ready.sem, probs_ready.ahead)
            act.sem_inc(out_taken.sem, out_taken.ahead)
            act.sem_inc(taken_out[0].sem, taken_out[0].ahead)
            act.sem_inc(taken[0].sem, n_taken[0])
            if a.cosine:
                act.preload_act_table_set("natural_log_exp_and_others")
            else:
                act.preload_act_table(ACT.Exp)
            act.wait_ge(cleared.sem, cleared.nth(1))
            if ONCE:
                act.wait_ge(once_in.sem, ONCE)

            def event(kind, u, j, s, b):
                k = (b + 1) % 2
                if (kind, u) in place_of and uses[place_of[kind, u]][2] == ACT_TAKES:
                    act.wait_ge(prepared.sem, prepared.nth(place_of[kind, u] + 1, s + 1))
                    if isinstance(s, int) and s == -2 and kind not in starts:
                        act.drain().then_inc(taken[0].sem, 1)
                    elif kind == "project":
                        c0, c1 = pieces[u]
                        c = c1 if a.cosine and real == K else min(c1, real)
                        if a.cosine:
                            if u == 0:
                                act.wait_ge(scaled.sem, scaled.nth(NP, s + 1))
                            act.activation(raw[:, c0:c], ps_p[:, 0:c - c0], ACT.Copy).then_inc(taken[0].sem, 1)
                        else:
                            act.activation(KQ[:, k, c0:c], ps_p[:, 0:c - c0], ACT.Identity, bias=w[:, k, BK]).then_inc(taken[0].sem, 1)
                    else:
                        c0, c1 = v_turns[u]
                        full = min(c1, real // P)
                        if full > c0:
                            ins = act.activation(V[:, k, c0:full, :],
                                                 ps_p[:, 0:(full - c0) * GC].rearrange("p (c v) -> p c v", v=GC), ACT.Copy)
                        if full < c1:
                            n = real - full * P
                            ins = act.activation(V[0:n, k, full, :], ps_p[0:n, (full - c0) * GC:(full - c0 + 1) * GC], ACT.Copy)
                        ins.then_inc(taken[0].sem, 1)
                elif kind == "root":
                    c0, c1 = pieces[u]
                    side, nth = use_taken(place_of["sum", u])
                    act.wait_ge(side.sem, side.nth(nth, s + 1))
                    act.activation(squares[:, c0:c1], squares[:, c0:c1], ACT.Ln, scale=NORM_RANGE)
                    act.drain()
                    act.activation(squares[:, c0:c1], squares[:, c0:c1], ACT.Exp, scale=-0.5).then_inc(rooted.sem, 1)
                elif kind == "exp":
                    act.wait_ge(max_ready.sem, max_ready.nth(u + 1, s))
                    act.wait_ge(turned.sem, turned.nth(last_turned[u - 2] - (R if u < 2 else 0), s))
                    act.wait_ge(inverted.sem, inverted.nth(u // U, s))
                    lo, hi = a.reach[u % TB]
                    first = first_col[u % 2]
                    v = masked[:, u % 2, lo:hi] if a.masked else ps_s[:, first + lo:first + hi]
                    act.activation(probs[:, u % 2, lo:hi], v, ACT.Exp, bias=neg_max[:, u % 2:u % 2 + 1], scale=sign,
                                   accum_out=None if a.choose else total_of(u, b)).then_inc(probs_ready.sem, 1)
                elif kind == "turn" and taker[ring_of(u, j)] == ACT_TAKES:
                    i = ring_of(u, j)
                    c0, c1 = turns(u % TB)[j]
                    act.wait_ge(turned.sem, turned.nth(i + 1, s))
                    act.wait_ge(out_ready.sem, out_ready.nth(u - 1, s))
                    act.activation(probsT[:, u % 2, c0 * P:c1 * P], ps_r[:, i % 2, 0:(c1 - c0) * P], ACT.Copy)\
                       .then_inc(taken_out[0].sem, 1)
                elif kind == "out":
                    h, t = u // TB, u % TB
                    act.wait_ge(out_ready.sem, out_ready.nth(u + 1, s))
                    side, nth = emptied(turned_inverse - R)
                    act.wait_ge(side.sem, side.nth(nth, s))
                    act.activation(OT[rows_of(h), b % 2, t * P:(t + 1) * P], ps_o[rows_of(h), 0:P], ACT.Copy).then_inc(out_taken.sem, 1)

            for (kind, u, j), s in rounds:
                event(kind, u, j, s, s)
            with act.Fori(0, a.groups) as g:
                for b in range(B):
                    for kind, u, j in plan:
                        event(kind, u, j, g * B + b, b)
            act.drain().then_inc(taken_out[0].sem, taker[:turned_inverse].count(ACT_TAKES))
            for kind, u, j in after:
                if kind == "skip" and taker[3] == ACT_TAKES:
                    act.drain().then_inc(taken_out[0].sem, 1)
                event(kind, u, j, a.groups * B, 0)

        @block.vector
        def _(dve):
            dve.sem_inc(taken_out[1].sem, taken_out[1].ahead)
            dve.sem_inc(taken[1].sem, n_taken[1])
            dve.sem_inc(inverted.sem, inverted.ahead)
            dve.sem_inc(max_ready.sem, max_ready.ahead)
            if a.choose:
                dve.sem_inc(chosen.sem, chosen.ahead)
            dve.memset(V[:, :, :, :], 0.0)
            dve.memset(probs[:, :, :], 0.0)
            dve.memset(OT[:, :, :], 0.0)
            dve.memset(total[:, :, :], 1.0)
            if not add:
                dve.memset(accT[:, :], 0.0)
            dve.drain()
            dve.sem_inc(cleared.sem, 1)
            if ONCE:
                dve.wait_ge(once_in.sem, ONCE)

            def event(kind, u, j, s, b, g):
                k = (b + 1) % 2
                if (kind, u) in place_of and uses[place_of[kind, u]][2] == DVE_TAKES:
                    dve.wait_ge(prepared.sem, prepared.nth(place_of[kind, u] + 1, s + 1))
                if isinstance(s, int) and s == -2 and kind not in starts:
                    if kind == "rotate":
                        dve.drain().then_inc(taken[1].sem, 1)
                        dve.drain().then_inc(roped.sem, 1)
                    elif kind == "scale":
                        dve.drain().then_inc(scaled.sem, 1)
                elif kind == "project" and uses[place_of[kind, u]][2] == DVE_TAKES:
                    c0, c1 = pieces[u]
                    if a.cosine:
                        if c0 < real:
                            dve.tensor_copy(raw[:, c0:min(c1, real)], ps_p[:, 0:min(c1, real) - c0])
                        dve.tensor_copy(raw[:, K:W], ps_p[:, K - c0:W - c0]).then_inc(taken[1].sem, 1)
                    else:
                        if c0 < real:
                            dve.tensor_scalar(KQ[:, k, c0:real], ps_p[:, 0:real - c0], w[:, k, BK], None, ALU.add)
                        dve.tensor_scalar(KQ[:, k, K:W], ps_p[:, K - c0:W - c0], w[:, k, BQ], sign * a.scale, ALU.add, ALU.mult)\
                           .then_inc(taken[1].sem, 1)
                elif kind == "sum":
                    c0, c1 = pieces[u]
                    dve.tensor_scalar(squares[:, c0:c1], ps_p[:, 0:c1 - c0], 1e-24, None, ALU.max).then_inc(taken[1].sem, 1)
                elif kind == "scale":
                    c0, c1 = pieces[u]
                    dve.wait_ge(rooted.sem, rooted.nth(u + 1, s))
                    for lo, hi, col in ((c0, min(c1, K), KS), (max(c0, K), c1, QS)):
                        if lo < hi:
                            ins = dve.scalar_tensor_tensor(out=KQ[:, k, lo:hi], in0=raw[:, lo:hi], scalar=w[:, k, col],
                                                           in1=squares[:, lo:hi], op0=ALU.mult, op1=ALU.mult)
                    if c1 == W:
                        dve.drain()
                        ins = dve.tensor_scalar(KQ[:, k, K:W], KQ[:, k, K:W], sign * a.scale * NORM_RANGE, None, ALU.mult)
                    ins.then_inc(scaled.sem, 1)
                elif kind == "rotate":
                    dve.tensor_tensor(squares[:, :], ps_p[:, 0:W], sin[:, :], ALU.mult).then_inc(taken[1].sem, 1)
                    dve.drain()
                    dve.wait_ge(cos_ready.sem, cos_ready.nth(1, s + 1))
                    dve.tensor_tensor(KQ[:, k, :], cos_part[:, :], squares[:, :], ALU.add).then_inc(roped.sem, 1)
                elif kind == "scores":
                    lo, hi = a.reach[u % TB]
                    here = ps_s[:, first_col[u % 2] + lo:first_col[u % 2] + hi]
                    least = neg_max[:, u % 2:u % 2 + 1]
                    dve.wait_ge(scores_ready.sem, scores_ready.nth(u + 1, s))
                    dve.wait_ge(probs_ready.sem, probs_ready.nth(u - 1, s))
                    if a.masked:
                        dve.memset(least, 0.0)
                        dve.drain()
                        dve.tensor_tensor_reduce(out=masked[:, u % 2, lo:hi], in0=here, in1=mask[:, u % TB, lo:hi], scale=1.0,
                                                 scalar=-MASKED, op0=ALU.add, op1=ALU.min, accum_out=least)\
                           .then_inc(max_ready.sem, 1)
                        return
                    if not a.choose:
                        dve.tensor_reduce(least, here, AX.X, ALU.max, negate=True).then_inc(max_ready.sem, 1)
                        if neg_max_out is not None and (u < U or s == -1):
                            dve.drain()
                            dve.tensor_copy(neg_max_out[:, b % B * TB + u:b % B * TB + u + 1] if u < U else neg_max_out[:, 0:1], least)
                        elif neg_max_out is not None and b + 1 < B:
                            dve.drain()
                            dve.tensor_copy(neg_max_out[:, (b + 1) * TB:(b + 1) * TB + 1], least)
                        return
                    dve.memset(top[:, 0, :], 0.0)
                    dve.drain()
                    dve.max(top[:, 0, :], here)
                    dve.drain()
                    dve.match_replace(rest[:, :], top[:, 0, :], here, TAKEN)
                    dve.tensor_scalar(least, top[:, 0, 0:1], -1.0, None, ALU.mult).then_inc(max_ready.sem, 1)
                    for r in range(1, a.choose // 8):
                        dve.drain()
                        dve.max(top[:, r % 2, :], rest[:, :])
                        dve.drain()
                        dve.match_replace(rest[:, :], top[:, r % 2, :], rest[:, :], TAKEN)
                    dve.drain()
                    dve.wait_ge(probs_ready.sem, probs_ready.nth(u + 1, s))
                    dve.scalar_tensor_tensor(out=probs[:, u % 2, 0:K], in0=rest[:, :], scalar=TAKEN, in1=probs[:, u % 2, 0:K],
                                             op0=ALU.is_equal, op1=ALU.mult, accum_out=total_of(u, b))\
                       .then_inc(chosen.sem, 1)
                elif kind == "turn" and taker[ring_of(u, j)] == DVE_TAKES:
                    i = ring_of(u, j)
                    c0, c1 = turns(u % TB)[j]
                    dve.wait_ge(turned.sem, turned.nth(i + 1, s))
                    dve.wait_ge(out_ready.sem, out_ready.nth(u - 1, s))
                    dve.tensor_copy(probsT[:, u % 2, c0 * P:c1 * P], ps_r[:, i % 2, 0:(c1 - c0) * P]).then_inc(taken_out[1].sem, 1)
                elif kind == "invert":
                    if not a.choose:
                        dve.wait_ge(probs_ready.sem, probs_ready.nth(0, s))
                    dve.reciprocal(inv[:, :], total[:, (b + 1) % 2, :])
                    dve.drain()
                    dve.wait_ge(turned.sem, turned.nth(turned_inverse + 1 - R, s))
                    dve.tensor_copy(inverse[:, :, :].rearrange("p t (h c) -> p h t c", c=a.stride),
                                    inv[:, :].rearrange("p (h t o) -> p h t o", t=TB, o=1).broadcast_to([P, a.heads, TB, a.stride]))\
                       .then_inc(inverted.sem, 1)
                elif kind == "turn_inverse":
                    dve.wait_ge(turned.sem, turned.nth(turned_inverse + 1, s))
                    dve.wait_ge(out_taken.sem, out_taken.nth(0, s))
                    dve.tensor_tensor(divided[:, :], ps_r[:, turned_inverse % 2, 0:T], OT[:, (b + 1) % 2, :], ALU.mult)\
                       .then_inc(taken_out[1].sem, 1)
                elif kind == "final":
                    dve.wait_ge(turned.sem, turned.nth(finished + 1, s))
                    last = slice((b + B - 1) % B * T, ((b + B - 1) % B + 1) * T)
                    dve.tensor_tensor(accT[:, last], accT[:, last], ps_r[:, finished % 2, 0:T], ALU.add).then_inc(taken_out[1].sem, 1)
                    dve.drain()

            for (kind, u, j), s in rounds:
                event(kind, u, j, s, s, 0)
            with dve.Fori(0, a.groups) as g:
                for b in range(B):
                    for kind, u, j in plan:
                        event(kind, u, j, g * B + b, b, g)
            if DVE_TAKES in taker[:turned_inverse]:
                dve.drain().then_inc(taken_out[1].sem, taker[:turned_inverse].count(DVE_TAKES))
            for kind, u, j in after:
                if kind == "skip" and taker[3] == DVE_TAKES:
                    dve.drain().then_inc(taken_out[1].sem, 1)
                event(kind, u, j, a.groups * B, 0, 0)


MASKED = -2.0 ** 100
TAKEN = -3.0e38
NORM_RANGE = float(2 ** 20)


def to_rows(m, accT, norm=None, bias=None):
    nc = m.nc
    with ExitStack() as ctx:
        place = Place(nc, ctx, "rows")
        ps = place.psum("ps", [P, NT * P])
        turned = place.counter("turned")
        stats = place.sbuf("stats", [P, NT, 6])
        mv = place.sbuf("mv", [P, NT, 2])
        rstd = place.sbuf("rstd", [P, NT])
        gain = place.sbuf("gain", [P, D])
        gain_in = place.counter("gain_in")
        var_ready = place.counter("var_ready")
        root_ready = place.counter("root_ready")
        block = ctx.enter_context(nc.Block())

        @block.tensor
        def _(pe):
            for t in range(NT):
                mm = pe.transpose(ps[:, t * P:(t + 1) * P], accT[:, t * P:(t + 1) * P], m.ident[:, :])
            mm.then_inc(turned.sem, 1)

        if norm is not None:
            @block.sync
            def _(sp):
                sp.dma_start(gain[:, :], norm.rearrange("(o d) -> o d", o=1).broadcast_to([P, D])).then_inc(gain_in.sem, 16)

            @block.scalar
            def _(act):
                act.wait_ge(var_ready.sem, var_ready.nth(1))
                act.activation(rstd[:, :], rstd[:, :], ACT.Sqrt).then_inc(root_ready.sem, 1)

        @block.vector
        def _(dve):
            dve.wait_ge(turned.sem, turned.nth(1))
            dve.tensor_copy(m.Y[:, :, :], ps[:, :].rearrange("p (t d) -> p t d", d=D))
            if norm is None:
                return
            dve.drain()
            for t in range(NT):
                dve.bn_stats(stats[:, t, :], m.Y[:, t, :])
            dve.drain()
            for t in range(NT):
                dve.bn_aggr(mv[:, t, :], stats[:, t, :])
            dve.drain()
            dve.tensor_scalar(rstd[:, :], mv[:, :, 1], 1e-5, None, ALU.add).then_inc(var_ready.sem, 1)
            dve.wait_ge(root_ready.sem, root_ready.nth(1))
            dve.reciprocal(rstd[:, :], rstd[:, :])
            dve.wait_ge(gain_in.sem, gain_in.nth(16))
            dve.drain()
            for t in range(NT):
                dve.tensor_scalar(m.Y[:, t, :], m.Y[:, t, :], mv[:, t, 0:1], rstd[:, t:t + 1], ALU.subtract, ALU.mult)
            dve.drain()
            for t in range(NT):
                dve.tensor_tensor(m.Y[:, t, :], m.Y[:, t, :], gain[:, :], ALU.mult)


def add_column(m, accT, column):
    nc = m.nc
    with ExitStack() as ctx:
        place = Place(nc, ctx, "bias")
        bias = place.sbuf("bias", [P, 1])
        bias_in = place.counter("bias_in")
        block = ctx.enter_context(nc.Block())

        @block.sync
        def _(sp):
            sp.dma_start(bias[:, :], column.rearrange("(p o) -> p o", o=1)).then_inc(bias_in.sem, 16)

        @block.vector
        def _(dve):
            dve.wait_ge(bias_in.sem, bias_in.nth(16))
            dve.tensor_scalar(accT[:, :], accT[:, :], bias[:, 0:1], None, ALU.add)


def gated_delta(m):
    nc = m.nc
    with ExitStack() as outer:
        keep = Place(nc, outer, "delta")
        vT = keep.sbuf("vT", [P, B, FIR_PAD + T])
        taps = keep.sbuf("taps", [P, 12 + 81])
        delta = keep.sbuf("delta", [P, NT, D])
        with ExitStack() as mid:
            inner = Place(nc, mid, "chunks")
            qT = inner.sbuf("qT", [P, B * T])
            kT = inner.sbuf("kT", [P, B * T])
            kbT = inner.sbuf("kbT", [P, B * T])
            vbT = inner.sbuf("vbT", [P, B * T])
            u = inner.sbuf("u", [P, NT, D])
            k = inner.sbuf("k", [P, NT, D])
            wT = inner.sbuf("wT", [P, B * T])
            attnT = inner.sbuf("attnT", [P, NT, 4, P])
            delta_project(m, taps, qT, kT, kbT, vT, vbT)
            delta_chunks(m, qT, kT, kbT, vbT, u, k, wT, attnT)
            delta_scan(m, qT, k, u, wT, attnT, delta)
        delta_mix(m, vT, taps, delta)


FIR_PAD = 62


def delta_project(m, taps, qT, kT, kbT, vT, vbT):
    nc = m.nc
    with ExitStack() as ctx:
        place = Place(nc, ctx, "proj")
        w = place.sbuf("w", [P, 4, D])
        same = place.sbuf("same", [P, P])
        raw = place.sbuf("raw", [P, 3, B, 3 + T])
        conv = place.sbuf("conv", [P, 3, B, T])
        beta = place.sbuf("beta", [P, B * T])
        sq = place.sbuf("sq", [P, 2, B * T])
        ps = place.psum("ps", [P, 2, BANK])
        ps_n = place.psum("ps_n", [P, 4, BANK])
        w_in = place.counter("w_in")
        product_ready = place.counter("product_ready")
        product_taken = place.counter("product_taken")
        conv_ready = place.counter("conv_ready")
        silu_ready = place.counter("silu_ready")
        beta_ready = place.counter("beta_ready")
        sq_ready = place.counter("sq_ready")
        sum_ready = place.counter("sum_ready")
        sum_taken = place.counter("sum_taken")
        root_ready = place.counter("root_ready")
        block = ctx.enter_context(nc.Block())

        def cols(half):
            return slice(half * BANK, (half + 1) * BANK)

        @block.sync
        def _(sp):
            sp.dma_start(w[:, :, :], m.dram["L0_attn_proj"]).then_inc(w_in.sem, 16)
            sp.dma_start(same[:, :], m.dram["c_same_head32"]).then_inc(w_in.sem, 16)
            sp.dma_start(taps[:, :], m.dram["L0_attn_taps"]).then_inc(w_in.sem, 16)

        @block.tensor
        def _(pe):
            pe.wait_ge(w_in.sem, w_in.nth(48))
            for n in range(8):
                i, half = n // 2, n % 2
                if n >= 2:
                    pe.wait_ge(product_taken.sem, product_taken.nth(n - 1))
                pe.matmul(ps[:, n % 2, :], w[:, i, :], m.XT[:, cols(half)], start=True, stop=True).then_inc(product_ready.sem, 1)
            for n in range(4):
                pe.wait_ge(sq_ready.sem, sq_ready.nth(n // 2 + 1))
                pe.matmul(ps_n[:, n, :], same[:, :], sq[:, n // 2, cols(n % 2)], start=True, stop=True).then_inc(sum_ready.sem, 1)

        @block.scalar
        def _(act):
            for n in range(8):
                i, half = n // 2, n % 2
                act.wait_ge(product_ready.sem, product_ready.nth(n + 1))
                if i < 3:
                    act.activation(raw[:, i, 2 * half:2 * half + 2, 3:], ps[:, n % 2, :].rearrange("p (b t) -> p b t", t=T),
                                   ACT.Copy).then_inc(product_taken.sem, 1)
                else:
                    act.activation(beta[:, cols(half)], ps[:, n % 2, :], ACT.Sigmoid).then_inc(product_taken.sem, 1)
            for i in range(3):
                act.wait_ge(conv_ready.sem, conv_ready.nth(i + 1))
                act.activation(raw[:, i, :, 3:], conv[:, i, :, :], ACT.Sigmoid).then_inc(silu_ready.sem, 1)
            for i in range(2):
                act.wait_ge(sum_taken.sem, sum_taken.nth(i + 1))
                act.activation(sq[:, i, :], sq[:, i, :], ACT.Sqrt).then_inc(root_ready.sem, 1)

        @block.vector
        def _(dve):
            dve.memset(raw[:, :, :, 0:3], 0.0)
            dve.memset(vT[:, :, 0:FIR_PAD], 0.0)
            dve.wait_ge(w_in.sem, w_in.nth(48))
            for i in range(3):
                dve.wait_ge(product_taken.sem, product_taken.nth(2 * i + 2))
                for j in range(4):
                    tap = taps[:, 4 * i + j:4 * i + j + 1]
                    if j == 0:
                        dve.drain()
                        dve.tensor_scalar(conv[:, i, :, :], raw[:, i, :, 0:T], tap, None, ALU.mult)
                    else:
                        dve.drain()
                        ins = dve.scalar_tensor_tensor(out=conv[:, i, :, :], in0=raw[:, i, :, j:j + T], scalar=tap,
                                                       in1=conv[:, i, :, :], op0=ALU.mult, op1=ALU.add)
                ins.then_inc(conv_ready.sem, 1)
            for i, v in enumerate((qT, kT)):
                dve.wait_ge(silu_ready.sem, silu_ready.nth(i + 1))
                dve.tensor_tensor(v[:, :].rearrange("p (b t) -> p b t", t=T), conv[:, i, :, :], raw[:, i, :, 3:], ALU.mult)
                dve.drain()
                dve.tensor_tensor(sq[:, i, :], v[:, :], v[:, :], ALU.mult).then_inc(sq_ready.sem, 1)
            dve.wait_ge(product_taken.sem, product_taken.nth(8))
            dve.wait_ge(silu_ready.sem, silu_ready.nth(3))
            dve.tensor_tensor(vT[:, :, FIR_PAD:], conv[:, 2, :, :], raw[:, 2, :, 3:], ALU.mult)
            dve.drain()
            dve.tensor_tensor(vbT[:, :].rearrange("p (b t) -> p b t", t=T), vT[:, :, FIR_PAD:],
                              beta[:, :].rearrange("p (b t) -> p b t", t=T), ALU.mult)
            for i in range(2):
                dve.wait_ge(sum_ready.sem, sum_ready.nth(2 * i + 2))
                dve.tensor_scalar(sq[:, i, :], ps_n[:, 2 * i:2 * i + 2, :].rearrange("p h c -> p (h c)"), 1e-6, None, ALU.add)\
                   .then_inc(sum_taken.sem, 1)
            for i, v in enumerate((qT, kT)):
                dve.wait_ge(root_ready.sem, root_ready.nth(i + 1))
                dve.reciprocal(sq[:, i, :], sq[:, i, :])
                dve.drain()
                dve.tensor_tensor(v[:, :], v[:, :], sq[:, i, :], ALU.mult)
            dve.drain()
            dve.tensor_tensor(kbT[:, :], kT[:, :], beta[:, :], ALU.mult)


def delta_chunks(m, qT, kT, kbT, vbT, u, k, wT, attnT):
    nc = m.nc
    H = 4
    LEVELS = 5
    STEPS = 3 * (LEVELS - 1) - 1
    with ExitStack() as ctx:
        place = Place(nc, ctx, "tiles")
        below = place.sbuf("below", [P, 2 * LEVELS, P])
        causal = place.sbuf("causal", [P, P])
        now = place.sbuf("now", [P, 4, P])
        rows = place.sbuf("rows", [P, 3, P])
        A_t = place.sbuf("A_t", [P, LEVELS, H, P])
        T_ = place.sbuf("T_", [P, H, P])
        Tt = place.sbuf("Tt", [P, H, P])
        AT = place.sbuf("AT", [P, H, P])
        ps_a = place.psum("ps_a", [P, H, BANK])
        ps_r = place.psum("ps_r", [P, BANK])
        ps_1 = place.psum("ps_1", [P, BANK])
        ps_2 = place.psum("ps_2", [P, BANK])
        ps_3 = place.psum("ps_3", [P, BANK])
        ps_u = ps_2[:, 0:2 * P].rearrange("p (i c) -> p i c", c=P)
        const_in = place.counter("const_in")
        now_ready = place.counter("now_ready", per=1)
        grams_ready = place.counter("grams_ready", per=3)
        rows_turned = place.counter("rows_turned", per=1)
        rows_ready = place.counter("rows_ready", per=1)
        first_ready = place.counter("first_ready", per=1)
        AT_made = place.counter("AT_made", per=LEVELS - 1)
        AT_ready = place.counter("AT_ready", per=LEVELS - 1)
        joined = place.counter("joined", per=LEVELS - 1)
        T_ready = place.counter("T_ready", per=LEVELS - 1)
        uw_made = place.counter("uw_made", per=1, ahead=1)
        uw_taken = place.counter("uw_taken", per=1, ahead=1)
        block = ctx.enter_context(nc.Block())

        def head(ps, h):
            return ps[:, h * P:(h + 1) * P]

        def heads(ps):
            return ps[:, :].rearrange("p (h c) -> p h c", c=P)

        def spread(mask):
            return mask.rearrange("p (o c) -> p o c", o=1).broadcast_to([P, H, P])

        @block.sync
        def _(sp):
            sp.dma_start(below[:, :, :], m.dram["c_below"]).then_inc(const_in.sem, 16)
            sp.dma_start(causal[:, :], m.dram["c_causal32"]).then_inc(const_in.sem, 16)

        @block.scalar
        def _(act):
            with act.Fori(0, NT) as t:
                act.wait_ge(uw_made.sem, uw_made.nth(0, t))
                for i, v in enumerate((qT, kT, kbT, vbT)):
                    ins = act.activation(now[:, i, :], v[:, bass.ds(t * P, P)], ACT.Copy)
                ins.then_inc(now_ready.sem, 1)
                act.wait_ge(rows_turned.sem, rows_turned.nth(1, t))
                act.activation(k[:, bass.ds(t, 1), :].rearrange("p o c -> p (o c)"), ps_r[:, 0:P], ACT.Copy)
                act.activation(rows[:, 1:3, :], ps_r[:, P:3 * P].rearrange("p (i c) -> p i c", c=P), ACT.Copy)\
                   .then_inc(rows_ready.sem, 1)

        @block.tensor
        def _(pe):
            with pe.Fori(0, NT) as t:
                pe.wait_ge(now_ready.sem, now_ready.nth(1, t))
                for i, (a, b) in enumerate(((1, 2), (2, 1), (1, 0))):
                    for h in range(H):
                        part = slice(32 * h, 32 * (h + 1))
                        mm = pe.matmul(ps_a[:, h, i * P:(i + 1) * P], now[part, a, :], now[part, b, :], start=True, stop=True)
                    mm.then_inc(grams_ready.sem, 1)
                for i in range(3):
                    mm = pe.transpose(ps_r[:, i * P:(i + 1) * P], now[:, i + 1, :], m.ident[:, :])
                mm.then_inc(rows_turned.sem, 1)
                for s in range(1, LEVELS):
                    if s == 1:
                        pe.wait_ge(first_ready.sem, first_ready.nth(1, t))
                    else:
                        pe.wait_ge(T_ready.sem, T_ready.nth(s - 1, t))
                    for h in range(H):
                        mm = pe.matmul(head(ps_1, h), A_t[:, s, h, :], T_[:, h, :], start=True, stop=True)
                    mm.then_inc(AT_made.sem, 1)
                    pe.wait_ge(AT_ready.sem, AT_ready.nth(s, t))
                    for h in range(H):
                        mm = pe.matmul(head(ps_3, h), AT[:, h, :], Tt[:, h, :], start=True, stop=True)
                    if s < LEVELS - 1:
                        for h in range(H):
                            mm = pe.matmul(head(ps_2, h), Tt[:, h, :], AT[:, h, :], start=True, stop=True)
                    mm.then_inc(joined.sem, 1)
                pe.wait_ge(T_ready.sem, T_ready.nth(LEVELS - 1, t))
                pe.wait_ge(rows_ready.sem, rows_ready.nth(1, t))
                pe.wait_ge(uw_taken.sem, uw_taken.nth(0, t))
                for h in range(H):
                    ch = slice(32 * h, 32 * (h + 1))
                    pe.matmul(ps_u[:, 0, ch], Tt[:, h, :], rows[:, 2, ch], start=True, stop=True)
                    mm = pe.matmul(ps_u[ch, 1, :], rows[:, 1, ch], Tt[:, h, :], start=True, stop=True)
                mm.then_inc(uw_made.sem, 1)

        @block.vector
        def _(dve):
            dve.sem_inc(uw_taken.sem, uw_taken.ahead)
            dve.sem_inc(uw_made.sem, uw_made.ahead)
            dve.wait_ge(const_in.sem, const_in.nth(32))
            with dve.Fori(0, NT) as t:
                dve.wait_ge(grams_ready.sem, grams_ready.nth(3, t))
                for i in range(3):
                    if i == 0:
                        for s in range(LEVELS):
                            ins = dve.tensor_tensor(A_t[:, s, :, :], ps_a[:, :, 0:P], spread(below[:, 2 * s + 1, :]), ALU.mult)
                        dve.drain()
                        dve.tensor_tensor(Tt[:, :, :], A_t[:, 0, :, :], spread(m.ident[:, :]), ALU.add)
                    elif i == 1:
                        dve.tensor_tensor(T_[:, :, :], ps_a[:, :, P:2 * P], spread(below[:, 0, :]), ALU.mult)
                        dve.drain()
                        dve.tensor_tensor(T_[:, :, :], T_[:, :, :], spread(m.ident[:, :]), ALU.add).then_inc(first_ready.sem, 1)
                    else:
                        dve.tensor_tensor(attnT[:, bass.ds(t, 1), :, :].rearrange("p o h c -> p (o h) c"), ps_a[:, :, 2 * P:3 * P],
                                          spread(causal[:, :]), ALU.mult)
                for s in range(1, LEVELS):
                    dve.wait_ge(AT_made.sem, AT_made.nth(s, t))
                    dve.tensor_copy(AT[:, :, :], heads(ps_1)).then_inc(AT_ready.sem, 1)
                    dve.wait_ge(joined.sem, joined.nth(s, t))
                    if s < LEVELS - 1:
                        dve.tensor_tensor(T_[:, :, :], T_[:, :, :], heads(ps_2), ALU.add)
                    dve.tensor_tensor(Tt[:, :, :], Tt[:, :, :], heads(ps_3), ALU.add).then_inc(T_ready.sem, 1)
                dve.wait_ge(uw_made.sem, uw_made.nth(1, t))
                dve.tensor_copy(u[:, bass.ds(t, 1), :].rearrange("p o c -> p (o c)"), ps_u[:, 0, :])
                dve.tensor_copy(wT[:, bass.ds(t * P, P)], ps_u[:, 1, :]).then_inc(uw_taken.sem, 1)


def delta_scan(m, qT, k, u, wT, attnT, delta):
    nc = m.nc
    C = T // 32
    with ExitStack() as ctx:
        place = Place(nc, ctx, "scan")
        same = place.sbuf("same", [P, P])
        state = place.sbuf("state", [P, B, P])
        grown = place.sbuf("grown", [P, B, P])
        ps_w = place.psum("ps_w", [P, BANK])
        ps_o = place.psum("ps_o", [P, BANK])
        ps_s = place.psum("ps_s", [P, BANK])
        same_in = place.counter("same_in")
        state_ready = place.counter("state_ready")
        w_made = place.counter("w_made")
        u_ready = place.counter("u_ready")
        o_made = place.counter("o_made")
        o_taken = place.counter("o_taken")
        s_made = place.counter("s_made")
        block = ctx.enter_context(nc.Block())

        @block.sync
        def _(sp):
            sp.dma_start(same[:, :], m.dram["c_same_head32"]).then_inc(same_in.sem, 16)

        @block.tensor
        def _(pe):
            for c in range(C):
                t, r = c // 4, slice(32 * (c % 4), 32 * (c % 4 + 1))
                pe.wait_ge(state_ready.sem, state_ready.nth(c + 1))
                for b in range(B):
                    tok = slice(b * T + 32 * c, b * T + 32 * (c + 1))
                    mm = pe.matmul(ps_w[r, b * P:(b + 1) * P], wT[:, tok], state[:, b, :], start=True, stop=True)
                mm.then_inc(w_made.sem, 1)
                pe.wait_ge(u_ready.sem, u_ready.nth(c + 1))
                for b in range(B):
                    mm = pe.matmul(ps_s[:, b * P:(b + 1) * P], k[r, b * TB + t, :], u[r, b * TB + t, :], start=True, stop=True,
                                   tile_position=(r.start, 0))
                mm.then_inc(s_made.sem, 1)
                if c >= 1:
                    pe.wait_ge(o_taken.sem, o_taken.nth(c))
                for b in range(B):
                    tok = slice(b * T + 32 * c, b * T + 32 * (c + 1))
                    pe.matmul(ps_o[r, b * P:(b + 1) * P], qT[:, tok], state[:, b, :], start=True, stop=False, skip_group_check=True)
                    for h in range(4):
                        ch = slice(32 * h, 32 * (h + 1))
                        mm = pe.matmul(ps_o[r, b * P + 32 * h:b * P + 32 * (h + 1)], attnT[r, b * TB + t, h, r],
                                       u[r, b * TB + t, ch], start=False, stop=(h == 3), skip_group_check=True,
                                       tile_position=(r.start, r.start))
                mm.then_inc(o_made.sem, 1)

        @block.vector
        def _(dve):
            dve.memset(state[:, :, :], 0.0).then_inc(state_ready.sem, 1)
            dve.wait_ge(same_in.sem, same_in.nth(16))
            for c in range(C):
                t, r = c // 4, slice(32 * (c % 4), 32 * (c % 4 + 1))
                dve.wait_ge(w_made.sem, w_made.nth(c + 1))
                here = u[:, :, :].rearrange("p (b u) d -> p b u d", u=TB)[r, :, t, :]
                dve.tensor_tensor(here, here, ps_w[r, :].rearrange("p (b d) -> p b d", d=P), ALU.subtract).then_inc(u_ready.sem, 1)
                dve.wait_ge(s_made.sem, s_made.nth(c + 1))
                dve.tensor_tensor(grown[:, :, :], ps_s[:, :].rearrange("p (b d) -> p b d", d=P),
                                  same[:, :].rearrange("p (o d) -> p o d", o=1).broadcast_to([P, B, P]), ALU.mult)
                dve.drain()
                dve.wait_ge(o_made.sem, o_made.nth(c + 1))
                dve.tensor_tensor(state[:, :, :], state[:, :, :], grown[:, :, :], ALU.add).then_inc(state_ready.sem, 1)

        @block.scalar
        def _(act):
            for c in range(C):
                t, r = c // 4, slice(32 * (c % 4), 32 * (c % 4 + 1))
                act.wait_ge(o_made.sem, o_made.nth(c + 1))
                act.activation(delta[:, :, :].rearrange("p (b u) d -> p b u d", u=TB)[r, :, t, :],
                               ps_o[r, :].rearrange("p (b d) -> p b d", d=P), ACT.Copy).then_inc(o_taken.sem, 1)


def delta_mix(m, vT, taps, delta):
    nc = m.nc
    H = 4
    FIRS = ((12, 3), (15, 15), (30, 63))
    with ExitStack() as ctx:
        place = Place(nc, ctx, "mix")
        gate_w = place.sbuf("gate_w", [P, 20])
        row = place.sbuf("row", [P, 20 + 4 + 4 + 32])
        Wo = place.sbuf("Wo", [P, D])
        fir = place.sbuf("fir", [P, 3, B, T])
        local = place.sbuf("local", [P, 2, NT, D])
        gates = place.sbuf("gates", [P, NT, H, 5])
        stat = place.sbuf("stat", [P, NT, H])
        keep = place.sbuf("keep", [P, H])
        total = place.sbuf("total", [P, NT, D])
        oT = place.sbuf("oT", [P, B * T])
        ps_g = place.psum("ps_g", [P, BANK])
        ps_t = place.psum("ps_t", [P, 2, BANK])
        ps_y = place.psum("ps_y", [P, 2, BANK])
        small_in = place.counter("small_in")
        gate_made = place.counter("gate_made")
        temp_ready = place.counter("temp_ready")
        shifted = place.counter("shifted")
        exp_ready = place.counter("exp_ready")
        fir_ready = place.counter("fir_ready")
        turned = place.counter("turned")
        local_ready = place.counter("local_ready")
        local_used = place.counter("local_used")
        mean_ready = place.counter("mean_ready")
        root_ready = place.counter("root_ready")
        normed = place.counter("normed")
        o_turned = place.counter("o_turned")
        oT_ready = place.counter("oT_ready")
        y_ready = place.counter("y_ready")
        block = ctx.enter_context(nc.Block())
        rows = lambda v: v.rearrange("p t (h c) -> p (t h) c", c=32)

        @block.sync
        def _(sp):
            sp.dma_start(gate_w[:, :], m.dram["L0_attn_gate"]).then_inc(small_in.sem, 16)
            sp.dma_start(row[:, :], m.dram["L0_attn_row"].broadcast_to([P, 60])).then_inc(small_in.sem, 16)
            sp.dma_start(Wo[:, :], m.dram["L0_attn_WoT"]).then_inc(small_in.sem, 16)

        @block.tensor
        def _(pe):
            pe.wait_ge(small_in.sem, small_in.nth(48))
            for t in range(NT):
                mm = pe.matmul(ps_g[:, t * 20:(t + 1) * 20], m.XT[:, t * P:(t + 1) * P], gate_w[:, :], start=True, stop=True)
            mm.then_inc(gate_made.sem, 1)
            for n in range(8):
                i, half = n // 2, n % 2
                if i >= 1:
                    pe.wait_ge(fir_ready.sem, fir_ready.nth(i))
                if n >= 2:
                    pe.wait_ge(local_ready.sem, local_ready.nth(n - 1))
                for t in range(4 * half, 4 * half + 4):
                    b, at = t // TB, t % TB * P
                    src = vT[:, b, FIR_PAD + at:FIR_PAD + at + P] if i == 0 else fir[:, i - 1, b, at:at + P]
                    mm = pe.transpose(ps_t[:, n % 2, (t % 4) * P:(t % 4 + 1) * P], src, m.ident[:, :])
                mm.then_inc(turned.sem, 1)
            for half in range(2):
                pe.wait_ge(normed.sem, normed.nth(1))
                if half == 0:
                    pe.wait_ge(local_ready.sem, local_ready.nth(8))
                for t in range(4 * half, 4 * half + 4):
                    mm = pe.transpose(ps_t[:, half, (t % 4) * P:(t % 4 + 1) * P], total[:, t, :], m.ident[:, :])
                mm.then_inc(o_turned.sem, 1)
            for t in range(NT):
                pe.wait_ge(oT_ready.sem, oT_ready.nth(t // 4 + 1))
                mm = pe.matmul(ps_y[:, t // 4, (t % 4) * P:(t % 4 + 1) * P], oT[:, t * P:(t + 1) * P], Wo[:, :], start=True, stop=True)
            mm.then_inc(y_ready.sem, 1)

        @block.scalar
        def _(act):
            act.wait_ge(small_in.sem, small_in.nth(48))
            act.activation(row[:, 20:24], row[:, 20:24], ACT.Exp, scale=-1.0).then_inc(temp_ready.sem, 1)
            act.wait_ge(shifted.sem, shifted.nth(1))
            act.activation(gates[:, :, :, :], gates[:, :, :, :], ACT.Exp).then_inc(exp_ready.sem, 1)
            for n in range(8):
                i, half = n // 2, n % 2
                act.wait_ge(turned.sem, turned.nth(n + 1))
                if i >= 2:
                    act.wait_ge(local_used.sem, local_used.nth(i - 1))
                act.activation(local[:, i % 2, 4 * half:4 * half + 4, :], ps_t[:, n % 2, :].rearrange("p (t d) -> p t d", d=D), ACT.Copy)\
                   .then_inc(local_ready.sem, 1)
            act.wait_ge(mean_ready.sem, mean_ready.nth(1))
            act.activation(stat[:, :, :], stat[:, :, :], ACT.Sqrt).then_inc(root_ready.sem, 1)
            for half in range(2):
                act.wait_ge(o_turned.sem, o_turned.nth(half + 1))
                act.activation(oT[:, half * BANK:(half + 1) * BANK], ps_t[:, half, :], ACT.Copy).then_inc(oT_ready.sem, 1)

        @block.vector
        def _(dve):
            def over(v, n):
                return v.rearrange("p t (h o) -> p (t h) o", o=1).broadcast_to([P, NT * H, n])

            dve.wait_ge(small_in.sem, small_in.nth(48))
            dve.wait_ge(gate_made.sem, gate_made.nth(1))
            b20 = row[:, 0:20].rearrange("p (o h) -> p o h", o=1).broadcast_to([P, NT, 20])
            flat = gates[:, :, :, :].rearrange("p t h g -> p (t h) g")
            dve.tensor_tensor(gates[:, :, :, :].rearrange("p t h g -> p t (h g)"), ps_g[:, 0:160].rearrange("p (t g) -> p t g", g=20),
                              b20, ALU.add)
            dve.wait_ge(temp_ready.sem, temp_ready.nth(1))
            dve.drain()
            for h in range(H):
                dve.tensor_scalar(gates[:, :, h, :], gates[:, :, h, :], row[:, 20 + h:21 + h], None, ALU.mult)
            dve.drain()
            dve.tensor_reduce(stat[:, :, :].rearrange("p t h -> p (t h)"), flat, AX.X, ALU.max)
            dve.drain()
            dve.tensor_tensor(flat, flat, over(stat[:, :, :], 5), ALU.subtract).then_inc(shifted.sem, 1)
            dve.tensor_scalar(row[:, 24:28], row[:, 24:28], 0.0, 0.2, ALU.max, ALU.min)
            dve.drain()
            dve.tensor_scalar(keep[:, :], row[:, 24:28], -5.0, 1.0, ALU.mult, ALU.add)
            dve.wait_ge(exp_ready.sem, exp_ready.nth(1))
            dve.tensor_reduce(stat[:, :, :].rearrange("p t h -> p (t h)"), flat, AX.X, ALU.add)
            dve.drain()
            dve.reciprocal(stat[:, :, :], stat[:, :, :])
            dve.drain()
            dve.tensor_tensor(flat, flat, over(stat[:, :, :], 5), ALU.mult)
            dve.drain()
            for h in range(H):
                dve.tensor_scalar(gates[:, :, h, :], gates[:, :, h, :], keep[:, h:h + 1], row[:, 24 + h:25 + h], ALU.mult, ALU.add)
            for i, (first, n) in enumerate(FIRS):
                for j in range(n):
                    tap = taps[:, first + j:first + j + 1]
                    src = vT[:, :, FIR_PAD - (n - 1) + j:FIR_PAD - (n - 1) + j + T]
                    if j == 0:
                        ins = dve.tensor_scalar(fir[:, i, :, :], src, tap, None, ALU.mult)
                    else:
                        ins = dve.scalar_tensor_tensor(out=fir[:, i, :, :], in0=src, scalar=tap, in1=fir[:, i, :, :],
                                                       op0=ALU.mult, op1=ALU.add)
                    if j < n - 1:
                        dve.drain()
                ins.then_inc(fir_ready.sem, 1)

            def gate(p):
                return gates[:, :, :, p:p + 1].rearrange("p t h o -> p (t h) o").broadcast_to([P, NT * H, 32])

            dve.tensor_tensor(rows(total[:, :, :]), rows(delta[:, :, :]), gate(3), ALU.mult)
            for i, p in enumerate((4, 0, 1, 2)):
                dve.wait_ge(local_ready.sem, local_ready.nth(2 * i + 2))
                dve.tensor_tensor(rows(local[:, i % 2, :, :]), rows(local[:, i % 2, :, :]), gate(p), ALU.mult)
                dve.drain()
                dve.tensor_tensor(total[:, :, :], total[:, :, :], local[:, i % 2, :, :], ALU.add).then_inc(local_used.sem, 1)
            dve.drain()
            dve.tensor_tensor(local[:, 0, :, :], total[:, :, :], total[:, :, :], ALU.mult)
            dve.drain()
            dve.tensor_reduce(stat[:, :, :].rearrange("p t h -> p (t h)"), rows(local[:, 0, :, :]), AX.X, ALU.add)
            dve.drain()
            dve.tensor_scalar(stat[:, :, :], stat[:, :, :], 1.0 / 32, 1e-5, ALU.mult, ALU.add).then_inc(mean_ready.sem, 1)
            dve.wait_ge(root_ready.sem, root_ready.nth(1))
            dve.reciprocal(stat[:, :, :], stat[:, :, :])
            dve.drain()
            dve.tensor_tensor(rows(total[:, :, :]), rows(total[:, :, :]), over(stat[:, :, :], 32), ALU.mult)
            dve.drain()
            w32 = row[:, 28:60].rearrange("p (o c) -> p o c", o=1).broadcast_to([P, NT * H, 32])
            dve.tensor_tensor(rows(total[:, :, :]), rows(total[:, :, :]), w32, ALU.mult).then_inc(normed.sem, 1)
            dve.wait_ge(y_ready.sem, y_ready.nth(1))
            dve.tensor_copy(m.Y[:, :, :], ps_y[:, :, :].rearrange("p h (t d) -> p (h t) d", d=D))


def bidaf(m):
    nc = m.nc
    with ExitStack() as outer:
        keep = Place(nc, outer, "bidaf")
        c2qT = keep.sbuf("c2qT", [P, B * T])
        neg_max = keep.sbuf("neg_max", [P, NT])
        attention(m, Heads("L0_xattn", S, 1, P, D, biased=True, context=True, n_heads=1), m.XT, c2qT, neg_max_out=neg_max)

        with ExitStack() as ctx:
            place = Place(nc, ctx, "join")
            w_c = place.sbuf("w_c", [P, 1])
            b3 = place.sbuf("b3", [P, 3])
            bias = place.sbuf("bias", [P, 1])
            W_l = place.sbuf("W_l", [P, 4, D])
            b_l = place.sbuf("b_l", [1, D])
            best = place.sbuf("best", [P, NT])
            row = place.sbuf("row", [1, B, T])
            stat = place.sbuf("stat", [1, B])
            weighted = place.sbuf("weighted", [P, B, T])
            q2c = place.sbuf("q2c", [P, B])
            prodT = place.sbuf("prodT", [P, B * T])
            c_q2cT = place.sbuf("c_q2cT", [P, B * T])
            ps_c = place.psum("ps_c", [P, BANK])
            ps_row = place.psum("ps_row", [P, 2, BANK])
            ps_b = place.psum("ps_b", [P, 2, BANK])
            ps_y = place.psum("ps_y", [P, 2, BANK])
            small_in = place.counter("small_in")
            self_ready = place.counter("self_ready")
            best_ready = place.counter("best_ready")
            row_ready = place.counter("row_ready")
            shifted = place.counter("shifted")
            exp_ready = place.counter("exp_ready")
            att_ready = place.counter("att_ready")
            spread = place.counter("spread")
            features_ready = place.counter("features_ready")
            y_ready = place.counter("y_ready")
            block = ctx.enter_context(nc.Block())

            @block.sync
            def _(sp):
                for tile, source in [(w_c[:, :], m.dram["L0_xattn_w_c"].rearrange("(p o) -> p o", o=1)),
                                     (b3[:, :], m.dram["L0_xattn_b"].broadcast_to([P, 3])),
                                     (W_l[:, :, :], m.dram["L0_xattn_W_l"]),
                                     (b_l[:, :], m.dram["L0_xattn_b_l"].rearrange("(o d) -> o d", o=1))]:
                    sp.dma_start(tile, source).then_inc(small_in.sem, 16)

            @block.tensor
            def _(pe):
                pe.wait_ge(small_in.sem, small_in.nth(64))
                for t in range(NT):
                    mm = pe.matmul(ps_c[:, t:t + 1], m.XT[:, t * P:(t + 1) * P], w_c[:, :], start=True, stop=True)
                mm.then_inc(self_ready.sem, 1)
                pe.wait_ge(best_ready.sem, best_ready.nth(1))
                for t in range(NT):
                    mm = pe.transpose(ps_row[0:1, t // 4, (t % 4) * P:(t % 4 + 1) * P], best[:, t:t + 1], m.ident[:, :])
                mm.then_inc(row_ready.sem, 1)
                pe.wait_ge(att_ready.sem, att_ready.nth(1))
                for half in range(2):
                    mm = pe.matmul(ps_b[:, half, :], m.ones[0:1, :], row[:, 2 * half:2 * half + 2, :].rearrange("o b t -> o (b t)"),
                                   start=True, stop=True)
                mm.then_inc(spread.sem, 1)
                pe.wait_ge(features_ready.sem, features_ready.nth(1))
                for t in range(NT):
                    tok = slice(t * P, (t + 1) * P)
                    out = ps_y[:, t // 4, (t % 4) * P:(t % 4 + 1) * P]
                    for k, feature in enumerate((m.XT, c2qT, prodT, c_q2cT)):
                        pe.matmul(out, feature[:, tok], W_l[:, k, :], start=(k == 0), stop=False)
                    mm = pe.matmul(out, m.ones[0:1, :], b_l[:, :], start=False, stop=True)
                mm.then_inc(y_ready.sem, 1)

            @block.scalar
            def _(act):
                act.wait_ge(shifted.sem, shifted.nth(1))
                act.activation(row[:, :, :], row[:, :, :], ACT.Exp).then_inc(exp_ready.sem, 1)

            @block.vector
            def _(dve):
                dve.wait_ge(small_in.sem, small_in.nth(64))
                dve.tensor_reduce(bias[:, :], b3[:, :], AX.X, ALU.add)
                dve.drain()
                dve.wait_ge(self_ready.sem, self_ready.nth(1))
                dve.scalar_tensor_tensor(out=best[:, :], in0=ps_c[:, 0:NT], scalar=bias[:, 0:1], in1=neg_max[:, :],
                                         op0=ALU.add, op1=ALU.subtract).then_inc(best_ready.sem, 1)
                dve.tensor_tensor(prodT[:, :], m.XT[:, :], c2qT[:, :], ALU.mult)
                dve.wait_ge(row_ready.sem, row_ready.nth(1))
                dve.tensor_copy(row[:, :, :], ps_row[0:1, :, :].rearrange("o h (b t) -> o (h b) t", b=2))
                dve.drain()
                dve.tensor_reduce(stat[:, :], row[:, :, :], AX.X, ALU.max)
                dve.drain()
                for b in range(B):
                    ins = dve.tensor_scalar(row[:, b, :], row[:, b, :], stat[:, b:b + 1], None, ALU.subtract)
                ins.then_inc(shifted.sem, 1)
                dve.wait_ge(exp_ready.sem, exp_ready.nth(1))
                dve.tensor_reduce(stat[:, :], row[:, :, :], AX.X, ALU.add)
                dve.drain()
                dve.reciprocal(stat[:, :], stat[:, :])
                dve.drain()
                for b in range(B):
                    ins = dve.tensor_scalar(row[:, b, :], row[:, b, :], stat[:, b:b + 1], None, ALU.mult)
                ins.then_inc(att_ready.sem, 1)
                dve.wait_ge(spread.sem, spread.nth(1))
                for half in range(2):
                    dve.tensor_tensor(weighted[:, 2 * half:2 * half + 2, :].rearrange("p b t -> p (b t)"), ps_b[:, half, :],
                                      m.XT[:, half * BANK:(half + 1) * BANK], ALU.mult)
                dve.drain()
                dve.tensor_reduce(q2c[:, :], weighted[:, :, :], AX.X, ALU.add)
                dve.drain()
                for b in range(B):
                    tok = slice(b * T, (b + 1) * T)
                    ins = dve.tensor_scalar(c_q2cT[:, tok], m.XT[:, tok], q2c[:, b:b + 1], None, ALU.mult)
                ins.then_inc(features_ready.sem, 1)
                dve.wait_ge(y_ready.sem, y_ready.nth(1))
                dve.tensor_copy(m.Y[:, :, :], ps_y[:, :, :].rearrange("p h (t d) -> p (h t) d", d=D))


def moe(m, name, E, normed):
    nc = m.nc
    F = 512
    FC = F // P
    HALVES = B * T // BANK
    U = FC * HALVES
    EB = 2
    N = U * EB
    RING = 4
    gates_dram = nc.dram_tensor(f"gates_{name}", (E, B * T), F32, kind="Internal").ap()
    w1_dram, w2_dram, b1_dram = (m.dram[f"{name}_{w}"] for w in (("W1", "W2", "b1") if normed else ("w1", "w2", "b1")))

    with ExitStack() as ctx:
        place = Place(nc, ctx, "moe")
        xn = place.sbuf("xn", [P, NT, D]) if normed else None
        xnT = place.sbuf("xnT", [P, B * T]) if normed else m.XT
        affine = place.sbuf("affine", [P, 2])
        stats = place.sbuf("stats", [P, NT, 6])
        mv = place.sbuf("mv", [P, NT, 2])
        rstd = place.sbuf("rstd", [P, NT])
        wg = place.sbuf("wg", [P, E])
        bg = place.sbuf("bg", [1, E])
        b2 = place.sbuf("b2", [E, D])
        number = place.sbuf("number", [P, E])
        scores = place.sbuf("scores", [P, NT, E])
        z = place.sbuf("z", [P, NT])
        top = place.sbuf("top", [P, NT, 8])
        at = place.sbuf("at", [P, NT, 8], U32)
        atf = place.sbuf("atf", [P, NT, 8])
        gate = place.sbuf("gate", [P, NT, 2])
        first = place.sbuf("first", [P, NT, E])
        second = place.sbuf("second", [P, NT, E])
        gT = place.sbuf("gT", [E, B * T])
        w1 = place.sbuf("w1", [P, EB, F])
        w2 = place.sbuf("w2", [P, EB, FC, D])
        b1 = place.sbuf("b1", [P, EB, FC])
        G = place.sbuf("G", [P, EB, B * T])
        h = place.sbuf("h", [P, RING, BANK])
        hg = place.sbuf("hg", [P, RING, BANK])
        yT = place.sbuf("yT", [P, B * T])
        ps_h = place.psum("ps_h", [P, RING, BANK])
        ps_y = place.psum("ps_y", [P, HALVES, BANK])
        ps_t = place.psum("ps_t", [P, 2, BANK])

        small_in = place.counter("small_in")
        var_ready = place.counter("var_ready")
        root_ready = place.counter("root_ready")
        xn_ready = place.counter("xn_ready")
        xn_turned = place.counter("xn_turned")
        xnT_ready = place.counter("xnT_ready")
        scores_ready = place.counter("scores_ready")
        exp_in = place.counter("exp_in")
        exp_out = place.counter("exp_out")
        gates_ready = place.counter("gates_ready")
        gates_turned = place.counter("gates_turned")
        gT_ready = place.counter("gT_ready")
        gates_stored = place.counter("gates_stored")
        expert_in = [place.counter(f"expert_in_{k}", per=64) for k in range(EB)]
        h_ready = place.counter("h_ready", per=N)
        gelu_ready = place.counter("gelu_ready", per=N)
        gated = place.counter("gated", per=N, ahead=RING)
        y_added = place.counter("y_added", per=N, ahead=EB * U)
        y_ready = place.counter("y_ready")
        yT_ready = place.counter("yT_ready")
        y_turned = place.counter("y_turned")
        block = ctx.enter_context(nc.Block())

        @block.sync
        def _(sp):
            for tile, source in ([(affine[:, 0:1], m.dram[name + "_gamma"].rearrange("(p o) -> p o", o=1)),
                                  (affine[:, 1:2], m.dram[name + "_beta"].rearrange("(p o) -> p o", o=1))] if normed else []) + [
                    (wg[:, :], m.dram[name + ("_Wg" if normed else "_gate_w")]),
                    (bg[:, :], m.dram[name + ("_bg" if normed else "_gate_b")].rearrange("(o e) -> o e", o=1)),
                    (b2[:, :], m.dram[name + "_b2"]),
                    (number[:, :], m.dram["c_number"][:, 0:E])]:
                sp.dma_start(tile, source).then_inc(small_in.sem, 16)
            sp.wait_ge(gT_ready.sem, gT_ready.nth(1))
            sp.dma_start(gates_dram, gT[:, :]).then_inc(gates_stored.sem, 16)
            sp.wait_ge(gates_stored.sem, gates_stored.nth(16))
            with sp.Fori(0, E // EB) as it:
                for k in range(EB):
                    e = it * EB + k
                    sp.wait_ge(y_added.sem, y_added.nth((k + 1 - EB) * U, it))
                    sp.dma_start(w1[:, k, :], w1_dram[bass.ds(e, 1), :, :].rearrange("e d f -> (e d) f")).then_inc(expert_in[k].sem, 16)
                    sp.dma_start(w2[:, k, :, :], w2_dram[bass.ds(e, 1), :, :].rearrange("e (c p) d -> p (e c) d", p=P)).then_inc(expert_in[k].sem, 16)
                    sp.dma_start(b1[:, k, :], b1_dram[bass.ds(e, 1), :, :].rearrange("e p c -> (e p) c")).then_inc(expert_in[k].sem, 16)
                    sp.dma_start(G[:, k, :], gates_dram[bass.ds(e, 1), :].broadcast_to([P, B * T])).then_inc(expert_in[k].sem, 16)

        @block.vector
        def _(dve):
            dve.sem_inc(gated.sem, gated.ahead)
            if normed:
                for t in range(NT):
                    dve.bn_stats(stats[:, t, :], m.X[:, t, :])
                dve.drain()
                for t in range(NT):
                    dve.bn_aggr(mv[:, t, :], stats[:, t, :])
                dve.drain()
                dve.tensor_scalar(rstd[:, :], mv[:, :, 1], 1e-5, None, ALU.add).then_inc(var_ready.sem, 1)
                dve.wait_ge(root_ready.sem, root_ready.nth(1))
                dve.reciprocal(rstd[:, :], rstd[:, :])
                dve.drain()
                for t in range(NT):
                    dve.tensor_scalar(xn[:, t, :], m.X[:, t, :], mv[:, t, 0:1], rstd[:, t:t + 1],
                                      ALU.subtract, ALU.mult).then_inc(xn_ready.sem, 1)
                dve.wait_ge(small_in.sem, small_in.nth(16 * 6))
                for half in range(HALVES):
                    dve.wait_ge(xn_turned.sem, xn_turned.nth(half + 1))
                    dve.tensor_scalar(xnT[:, half * BANK:(half + 1) * BANK], ps_t[:, half, :], affine[:, 0:1], affine[:, 1:2],
                                      ALU.mult, ALU.add).then_inc(xnT_ready.sem, 1)
            dve.wait_ge(scores_ready.sem, scores_ready.nth(1))
            dve.tensor_copy(scores[:, :, :], ps_h[:, 0, 0:NT * E].rearrange("p (t e) -> p t e", e=E))
            dve.drain()
            if normed:
                dve.tensor_reduce(z[:, :], scores[:, :, :], AX.X, ALU.max)
                dve.drain()
                for t in range(NT):
                    dve.tensor_scalar(scores[:, t, :], scores[:, t, :], z[:, t:t + 1], None, ALU.subtract)
                dve.drain()
                dve.sem_inc(exp_in.sem, 1)
                dve.wait_ge(exp_out.sem, exp_out.nth(1))
                dve.tensor_reduce(z[:, :], scores[:, :, :], AX.X, ALU.add)
                dve.drain()
                dve.reciprocal(z[:, :], z[:, :])
                dve.drain()
                for t in range(NT):
                    dve.tensor_scalar(scores[:, t, :], scores[:, t, :], z[:, t:t + 1], None, ALU.mult)
                dve.drain()
            for t in range(NT):
                dve.max(top[:, t, :], scores[:, t, :])
            dve.drain()
            for t in range(NT):
                dve.max_index(at[:, t, :], top[:, t, :], scores[:, t, :])
            if normed:
                dve.tensor_tensor(z[:, :], top[:, :, 0], top[:, :, 1], ALU.add)
                dve.drain()
                dve.tensor_scalar(z[:, :], z[:, :], 1e-8, None, ALU.add)
                dve.drain()
                dve.reciprocal(z[:, :], z[:, :])
                dve.drain()
                dve.tensor_tensor(gate[:, :, 0], top[:, :, 0], z[:, :], ALU.mult)
                dve.tensor_tensor(gate[:, :, 1], top[:, :, 1], z[:, :], ALU.mult)
            else:
                dve.tensor_tensor(z[:, :], top[:, :, 1], top[:, :, 0], ALU.subtract).then_inc(exp_in.sem, 1)
                dve.wait_ge(exp_out.sem, exp_out.nth(1))
                dve.tensor_scalar(gate[:, :, 0], z[:, :], 1.0, None, ALU.add)
                dve.drain()
                dve.reciprocal(gate[:, :, 0], gate[:, :, 0])
                dve.drain()
                dve.tensor_tensor(gate[:, :, 1], gate[:, :, 0], z[:, :], ALU.mult)
            dve.tensor_copy(atf[:, :, :], at[:, :, :])
            dve.wait_ge(small_in.sem, small_in.nth(16 * (6 if normed else 4)))
            dve.drain()
            for t in range(NT):
                dve.tensor_scalar(first[:, t, :], number[:, :], atf[:, t, 0:1], gate[:, t, 0:1], ALU.is_equal, ALU.mult)
                dve.tensor_scalar(second[:, t, :], number[:, :], atf[:, t, 1:2], gate[:, t, 1:2], ALU.is_equal, ALU.mult)
            dve.drain()
            dve.tensor_tensor(first[:, :, :], first[:, :, :], second[:, :, :], ALU.add).then_inc(gates_ready.sem, 1)
            dve.wait_ge(gates_turned.sem, gates_turned.nth(1))
            for half in range(HALVES):
                copied = dve.tensor_copy(gT[:, half * BANK:(half + 1) * BANK], ps_t[0:E, half, :])
            copied.then_inc(gT_ready.sem, 1)
            with dve.Fori(0, E // EB) as it:
                for n in range(N):
                    k, half = n // U, n % U // FC
                    if n % U == 0:
                        dve.wait_ge(expert_in[k].sem, expert_in[k].nth(64, it))
                    dve.wait_ge(gelu_ready.sem, gelu_ready.nth(n + 1, it))
                    dve.wait_ge(y_added.sem, y_added.nth(n + 1 - RING, it))
                    dve.tensor_tensor(hg[:, n % RING, :], h[:, n % RING, :], G[:, k, half * BANK:(half + 1) * BANK],
                                      ALU.mult).then_inc(gated.sem, 1)
            for half in range(HALVES):
                dve.wait_ge(y_ready.sem, y_ready.nth(half + 1))
                dve.tensor_copy(yT[:, half * BANK:(half + 1) * BANK], ps_y[:, half, :]).then_inc(yT_ready.sem, 1)
            for half in range(HALVES):
                dve.wait_ge(y_turned.sem, y_turned.nth(half + 1))
                dve.tensor_copy(m.Y[:, half * 4:half * 4 + 4, :], ps_t[:, half, :].rearrange("p (t d) -> p t d", d=D))

        @block.scalar
        def _(act):
            if normed:
                act.wait_ge(var_ready.sem, var_ready.nth(1))
                act.activation(rstd[:, :], rstd[:, :], ACT.Sqrt).then_inc(root_ready.sem, 1)
            act.wait_ge(exp_in.sem, exp_in.nth(1))
            v = scores[:, :, :] if normed else z[:, :]
            act.activation(v, v, ACT.Exp).then_inc(exp_out.sem, 1)
            act.preload_act_table(ACT.Gelu)
            with act.Fori(0, E // EB) as it:
                for n in range(N):
                    k, f = n // U, n % FC
                    if n % U == 0:
                        act.wait_ge(expert_in[k].sem, expert_in[k].nth(64, it))
                    act.wait_ge(h_ready.sem, h_ready.nth(n + 1, it))
                    act.wait_ge(gated.sem, gated.nth(n + 1 - RING, it))
                    act.activation(h[:, n % RING, :], ps_h[:, n % RING, :], ACT.Gelu, bias=b1[:, k, f:f + 1])\
                       .then_inc(gelu_ready.sem, 1)

        @block.tensor
        def _(pe):
            pe.sem_inc(y_added.sem, y_added.ahead)
            if normed:
                for t in range(NT):
                    pe.wait_ge(xn_ready.sem, xn_ready.nth(t + 1))
                    mm = pe.transpose(ps_t[:, t // 4, (t % 4) * P:(t % 4 + 1) * P], xn[:, t, :], m.ident[:, :])
                    if t % 4 == 3:
                        mm.then_inc(xn_turned.sem, 1)
                pe.wait_ge(xnT_ready.sem, xnT_ready.nth(HALVES))
            pe.wait_ge(small_in.sem, small_in.nth(16 * (6 if normed else 4)))
            for t in range(NT):
                out = ps_h[:, 0, t * E:(t + 1) * E]
                pe.matmul(out, xnT[:, t * P:(t + 1) * P], wg[:, :], start=True, stop=False)
                mm = pe.matmul(out, m.ones[0:1, :], bg[:, :], start=False, stop=True)
            mm.then_inc(scores_ready.sem, 1)
            pe.wait_ge(gates_ready.sem, gates_ready.nth(1))
            for t in range(NT):
                mm = pe.transpose(ps_t[0:E, t // 4, (t % 4) * P:(t % 4 + 1) * P], first[:, t, :], m.ident[:, :])
            mm.then_inc(gates_turned.sem, 1)
            pe.wait_ge(gT_ready.sem, gT_ready.nth(1))
            for half in range(HALVES):
                pe.matmul(ps_y[:, half, :], b2[:, :], gT[:, half * BANK:(half + 1) * BANK], start=True, stop=False,
                          skip_group_check=True)

            def up(it, n):
                k, half, f = n // U, n % U // FC, n % FC
                if n % U == 0:
                    pe.wait_ge(expert_in[k].sem, expert_in[k].nth(64, it))
                pe.wait_ge(gated.sem, gated.nth(n + 1 - RING, it))
                pe.matmul(ps_h[:, n % RING, :], w1[:, k, f * P:(f + 1) * P], xnT[:, half * BANK:(half + 1) * BANK],
                          start=True, stop=True).then_inc(h_ready.sem, 1)

            def down(it, n):
                k, half, f = n // U, n % U // FC, n % FC
                pe.wait_ge(gated.sem, gated.nth(n + 1, it))
                pe.matmul(ps_y[:, half, :], w2[:, k, f, :], hg[:, n % RING, :], start=False, stop=False,
                          skip_group_check=True).then_inc(y_added.sem, 1)

            with pe.Fori(0, E // EB) as it:
                for n in range(N):
                    up(it, n)
                    if n >= 2:
                        down(it, n - 2)
                down(it, N - 2)
                down(it, N - 1)
            for half in range(HALVES):
                pe.matmul(ps_y[:, half, :], m.ident[:, :], m.XT[:, half * BANK:(half + 1) * BANK], start=False, stop=True,
                          skip_group_check=True).then_inc(y_ready.sem, 1)
            for t in range(NT):
                pe.wait_ge(yT_ready.sem, yT_ready.nth(t // 4 + 1))
                mm = pe.transpose(ps_t[:, t // 4, (t % 4) * P:(t % 4 + 1) * P], yT[:, t * P:(t + 1) * P], m.ident[:, :])
                if t % 4 == 3:
                    mm.then_inc(y_turned.sem, 1)


def moe_0(m):
    moe(m, "L0_ffn", 8, normed=True)


def moe_1(m):
    moe(m, "L1_ffn", 24, normed=False)


def sparse_attention(m):
    with ExitStack() as ctx:
        place = Place(m.nc, ctx, "sparse")
        accT = place.sbuf("accT", [P, B * T])
        attention(m, Heads("L1_attn", T, 4, 32, 8, scale=8 ** -0.5, biased=True, masked=True), m.XT, accT)
        add_column(m, accT, m.dram["L1_attn_b_out"])
        to_rows(m, accT)


def cosine_cross(m):
    nc = m.nc
    with ExitStack() as ctx:
        place = Place(nc, ctx, "cosine")
        xnT = place.sbuf("xnT", [P, B * T])
        accT = place.sbuf("accT", [P, B * T])
        normed_columns(m, xnT, m.dram["L1_xattn_g_norm"])
        attention(m, Heads("L1_xattn", S + 1, 2, 64, 64, scale=8.0, context=True, cosine=True, null=True), xnT, accT)
        to_rows(m, accT, norm=m.dram["L1_xattn_g_out"])


def normed_columns(m, xnT, gain_dram):
    nc = m.nc
    with ExitStack() as ctx:
        place = Place(nc, ctx, "normed")
        gain = place.sbuf("gain", [P, 1])
        xn = place.sbuf("xn", [P, NT, D])
        stats = place.sbuf("stats", [P, NT, 6])
        mv = place.sbuf("mv", [P, NT, 2])
        rstd = place.sbuf("rstd", [P, NT])
        ps = place.psum("ps", [P, NT * P])
        gain_in = place.counter("gain_in")
        var_ready = place.counter("var_ready")
        root_ready = place.counter("root_ready")
        xn_ready = place.counter("xn_ready")
        turned = place.counter("turned")
        block = ctx.enter_context(nc.Block())

        @block.sync
        def _(sp):
            sp.dma_start(gain[:, :], gain_dram.rearrange("(p o) -> p o", o=1)).then_inc(gain_in.sem, 16)

        @block.vector
        def _(dve):
            for t in range(NT):
                dve.bn_stats(stats[:, t, :], m.X[:, t, :])
            dve.drain()
            for t in range(NT):
                dve.bn_aggr(mv[:, t, :], stats[:, t, :])
            dve.drain()
            dve.tensor_scalar(rstd[:, :], mv[:, :, 1], 1e-5, None, ALU.add).then_inc(var_ready.sem, 1)
            dve.wait_ge(root_ready.sem, root_ready.nth(1))
            dve.reciprocal(rstd[:, :], rstd[:, :])
            dve.drain()
            for t in range(NT):
                dve.tensor_scalar(xn[:, t, :], m.X[:, t, :], mv[:, t, 0:1], rstd[:, t:t + 1],
                                  ALU.subtract, ALU.mult).then_inc(xn_ready.sem, 1)
            dve.wait_ge(gain_in.sem, gain_in.nth(16))
            for half in range(2):
                dve.wait_ge(turned.sem, turned.nth(half + 1))
                cols = slice(half * BANK, (half + 1) * BANK)
                dve.tensor_scalar(xnT[:, cols], ps[:, cols], gain[:, 0:1], None, ALU.mult)

        @block.scalar
        def _(act):
            act.wait_ge(var_ready.sem, var_ready.nth(1))
            act.activation(rstd[:, :], rstd[:, :], ACT.Sqrt).then_inc(root_ready.sem, 1)

        @block.tensor
        def _(pe):
            for t in range(NT):
                pe.wait_ge(xn_ready.sem, xn_ready.nth(t + 1))
                mm = pe.transpose(ps[:, t * P:(t + 1) * P], xn[:, t, :], m.ident[:, :])
                if t % 4 == 3:
                    mm.then_inc(turned.sem, 1)


def peridynamic(m):
    nc = m.nc
    J = 64
    H = 16
    E = 16
    G = 2
    PAD = J - 1
    WT = PAD + T
    JB = 8
    NB = J // JB
    with ExitStack() as outer:
        keep = Place(nc, outer, "peri")
        logits = keep.sbuf("logits", [P, NT, J, H])
        value = keep.sbuf("value", [P, B, WT])
        with ExitStack() as mid:
            keep2 = Place(nc, mid, "peri_in")
            damage = keep2.sbuf("damage", [P, NT, J, H])
            moved = keep2.sbuf("moved", [P, G, B, 2, WT])
            pos = keep2.sbuf("pos", [P, J])
            b_dmg = keep2.sbuf("b_dmg", [P, 1])
            peridynamic_project(m, moved, value, pos, b_dmg)
            peridynamic_bonds(m, moved, pos, b_dmg, logits, damage)
            peridynamic_softmax(m, logits, damage)
        peridynamic_gather(m, logits, value)


def peridynamic_project(m, moved, value, pos, b_dmg):
    nc = m.nc
    G, J, PAD = 2, 64, 63
    with ExitStack() as ctx:
        place = Place(nc, ctx, "project")
        W_disp = place.sbuf("W_disp", [P, 256])
        W_val = place.sbuf("W_val", [P, D])
        blocks = place.sbuf("blocks", [P, 2, P])
        pos8 = place.sbuf("pos8", [16, P])
        rel_T = place.sbuf("rel_T", [16, J])
        dispT = place.sbuf("dispT", [P, G, B * T])
        ps = place.psum("ps", [P, 2, BANK])
        w_in = place.counter("w_in")
        product_ready = place.counter("product_ready")
        product_taken = place.counter("product_taken")
        block = ctx.enter_context(nc.Block())

        @block.sync
        def _(sp):
            for tile, name in [(W_disp, "W_disp"), (W_val, "W_val"), (blocks, "blocks"), (pos8, "pos8"), (rel_T, "rel_T"),
                               (b_dmg, "b_dmg8")]:
                at = tuple([slice(None)] * len(tile.shape))
                sp.dma_start(tile[at], m.dram["L2_attn_" + name]).then_inc(w_in.sem, 16)

        jobs = [("disp", g, half) for g in range(G) for half in range(2)] + [("val", 0, half) for half in range(2)] + \
            [("pos", 0, 0)] + [("moved", g * 2 + k, half) for g in range(G) for k in range(2) for half in range(2)]

        @block.tensor
        def _(pe):
            pe.wait_ge(w_in.sem, w_in.nth(16 * 6))
            for n, (what, i, half) in enumerate(jobs):
                cols = slice(half * BANK, (half + 1) * BANK)
                if what == "moved":
                    pe.wait_ge(product_taken.sem, product_taken.nth(max(n - 1, 4)))
                elif n >= 2:
                    pe.wait_ge(product_taken.sem, product_taken.nth(n - 1))
                if what == "disp":
                    mm = pe.matmul(ps[:, n % 2, :], W_disp[:, i * P:(i + 1) * P], m.XT[:, cols], start=True, stop=True)
                elif what == "val":
                    mm = pe.matmul(ps[:, n % 2, :], W_val[:, :], m.XT[:, cols], start=True, stop=True)
                elif what == "pos":
                    mm = pe.matmul(ps[:, n % 2, 0:J], pos8[:, :], rel_T[:, :], start=True, stop=True)
                else:
                    mm = pe.matmul(ps[:, n % 2, :], blocks[:, i % 2, :], dispT[:, i // 2, cols], start=True, stop=True)
                mm.then_inc(product_ready.sem, 1)

        @block.vector
        def _(dve):
            dve.memset(moved[:, :, :, :, 0:PAD], 0.0)
            dve.memset(value[:, :, 0:PAD], 0.0)
            for n, (what, i, half) in enumerate(jobs):
                dve.wait_ge(product_ready.sem, product_ready.nth(n + 1))
                cols = slice(half * BANK, (half + 1) * BANK)
                batches = slice(2 * half, 2 * half + 2)
                both = ps[:, n % 2, :].rearrange("p (b t) -> p b t", b=2)
                if what == "disp":
                    ins = dve.tensor_copy(dispT[:, i, cols], ps[:, n % 2, :])
                elif what == "val":
                    ins = dve.tensor_copy(value[:, batches, PAD:], both)
                elif what == "pos":
                    ins = dve.tensor_copy(pos[:, :], ps[:, n % 2, 0:J])
                else:
                    ins = dve.tensor_copy(moved[:, i // 2, batches, i % 2, PAD:], both)
                ins.then_inc(product_taken.sem, 1)


def peridynamic_bonds(m, moved, pos, b_dmg, logits, damage):
    nc = m.nc
    G, J, PAD, JB = 2, 64, 63, 16
    NB = J // JB
    Q = 2
    NQ = JB // Q
    plan = []
    for jb in range(NB):
        for q in range(NQ):
            plan.append(("set", jb, q))
            if jb and q < 3:
                plan.append((("take", "turn", "store")[q], jb - 1, None))
    plan += [(kind, NB - 1, None) for kind in ("take", "turn", "store")]
    with ExitStack() as ctx:
        place = Place(nc, ctx, "bonds")
        out16 = place.sbuf("out16", [P, 2, JB, P])
        strain = place.sbuf("strain", [P, 2, 2, Q, T])
        act_of = place.sbuf("act_of", [P, 2, 2, Q, T])
        rows = place.sbuf("rows", [P, 2, T])
        ps = place.psum("ps", [P, 2, 2, BANK])
        ps_t = place.psum("ps_t", [P, 2, TB, P])
        out16_in = place.counter("out16_in")
        strain_ready = place.counter("strain_ready", per=NQ * NB)
        gelu_ready = place.counter("gelu_ready", per=NQ * NB, ahead=NQ * NB)
        summed = place.counter("summed", per=NQ * NB, ahead=NQ * NB)
        rows_taken = place.counter("rows_taken", per=NB, ahead=NB)
        turned = place.counter("turned", per=NB, ahead=NB)
        stored = place.counter("stored", per=NB, ahead=NB)
        block = ctx.enter_context(nc.Block())

        @block.sync
        def _(sp):
            sp.dma_start(out16[:, :, :, :], m.dram["L2_attn_out16"]).then_inc(out16_in.sem, 16)

        @block.vector
        def _(dve):
            dve.sem_inc(stored.sem, stored.ahead)
            with dve.Fori(0, B) as b, dve.Fori(0, G) as g:
                it = b * G + g
                window = moved[:, bass.ds(g, 1), bass.ds(b, 1), :, :].rearrange("p g b k t -> p (g b k) t")
                for kind, jb, q in plan:
                    if kind == "set":
                        n = jb * NQ + q
                        dve.wait_ge(gelu_ready.sem, gelu_ready.nth(n - 1, it))
                        for o in range(Q):
                            j = jb * JB + q * Q + o
                            ins = dve.tensor_tensor(strain[:, q % 2, :, o, :], window[:, :, j:j + T], window[:, :, PAD:], ALU.subtract)
                        ins.then_inc(strain_ready.sem, 1)
                    elif kind == "store":
                        dve.wait_ge(turned.sem, turned.nth(jb + 1, it))
                        for k, where in enumerate((logits, damage)):
                            for t in range(TB):
                                at = where[:, bass.ds(b * TB + t, 1), jb * JB:(jb + 1) * JB, bass.ds(g * 8, 8)]
                                ins = dve.tensor_copy(at.rearrange("p o j h -> p (o j) h"),
                                                      ps_t[:, k, t, :].rearrange("p (j h) -> p j h", h=8))
                        ins.then_inc(stored.sem, 1)

        @block.scalar
        def _(act):
            act.sem_inc(gelu_ready.sem, gelu_ready.ahead)
            act.sem_inc(rows_taken.sem, rows_taken.ahead)
            act.preload_act_table(ACT.Gelu)
            with act.Fori(0, B) as b, act.Fori(0, G) as g:
                it = b * G + g
                for kind, jb, q in plan:
                    if kind == "set":
                        n = jb * NQ + q
                        act.wait_ge(strain_ready.sem, strain_ready.nth(n + 1, it))
                        act.wait_ge(summed.sem, summed.nth(n - 1, it))
                        for o in range(Q):
                            j = jb * JB + q * Q + o
                            act.activation(act_of[:, q % 2, 0, o, :], strain[:, q % 2, 0, o, :], ACT.Gelu, bias=pos[:, j:j + 1])
                        act.activation(act_of[:, q % 2, 1, :, :], strain[:, q % 2, 1, :, :], ACT.Gelu, bias=b_dmg[:, :])\
                           .then_inc(gelu_ready.sem, 1)
                    elif kind == "take":
                        act.wait_ge(summed.sem, summed.nth((jb + 1) * NQ, it))
                        act.wait_ge(turned.sem, turned.nth(jb, it))
                        act.activation(rows[:, :, :], ps[:, jb % 2, :, 0:T], ACT.Copy).then_inc(rows_taken.sem, 1)

        @block.tensor
        def _(pe):
            pe.sem_inc(summed.sem, summed.ahead)
            pe.sem_inc(turned.sem, turned.ahead)
            pe.wait_ge(out16_in.sem, out16_in.nth(16))
            with pe.Fori(0, B * G) as it:
                for kind, jb, q in plan:
                    if kind == "set":
                        if q == 0:
                            pe.wait_ge(rows_taken.sem, rows_taken.nth(jb - 1, it))
                        pe.wait_ge(gelu_ready.sem, gelu_ready.nth(jb * NQ + q + 1, it))
                        for k in range(2):
                            for o in range(Q):
                                j = q * Q + o
                                mm = pe.matmul(ps[:, jb % 2, k, 0:T], out16[:, k, j, :], act_of[:, q % 2, k, o, :], start=(j == 0),
                                               stop=(j == JB - 1))
                        mm.then_inc(summed.sem, 1)
                    elif kind == "turn":
                        pe.wait_ge(rows_taken.sem, rows_taken.nth(jb + 1, it))
                        pe.wait_ge(stored.sem, stored.nth(jb, it))
                        for k in range(2):
                            for t in range(TB):
                                mm = pe.transpose(ps_t[:, k, t, :], rows[:, k, t * P:(t + 1) * P], m.ident[:, :])
                        mm.then_inc(turned.sem, 1)


def peridynamic_softmax(m, logits, damage):
    nc = m.nc
    J, H = 64, 16
    with ExitStack() as ctx:
        place = Place(nc, ctx, "weights")
        mask = place.sbuf("mask", [P, J])
        b_out = place.sbuf("b_out", [P, 1])
        stat = place.sbuf("stat", [P, NT, H])
        small_in = place.counter("small_in")
        damage_ready = place.counter("damage_ready")
        shifted = place.counter("shifted")
        exp_l = place.counter("exp_l")
        block = ctx.enter_context(nc.Block())

        @block.sync
        def _(sp):
            sp.dma_start(mask[:, :], m.dram["L2_attn_mask"]).then_inc(small_in.sem, 16)
            sp.dma_start(b_out[:, :], m.dram["L2_attn_b_dmg_out"].rearrange("(o d) -> o d", o=1).broadcast_to([P, 1]))\
              .then_inc(small_in.sem, 16)

        @block.scalar
        def _(act):
            act.wait_ge(small_in.sem, small_in.nth(32))
            for t in range(NT):
                act.activation(damage[:, t, :, :], damage[:, t, :, :], ACT.Sigmoid, bias=b_out[:, :])\
                   .then_inc(damage_ready.sem, 1)
            for t in range(NT):
                act.wait_ge(shifted.sem, shifted.nth(t + 1))
                act.activation(logits[:, t, :, :], logits[:, t, :, :], ACT.Exp).then_inc(exp_l.sem, 1)

        @block.vector
        def _(dve):
            dve.wait_ge(small_in.sem, small_in.nth(32))
            for t in range(NT):
                dve.wait_ge(damage_ready.sem, damage_ready.nth(t + 1))
                dve.scalar_tensor_tensor(out=logits[:, t, :, :], in0=damage[:, t, :, :], scalar=-10.0, in1=logits[:, t, :, :],
                                         op0=ALU.mult, op1=ALU.add)
                if t % TB == 0:
                    dve.drain()
                    spread = mask[:, :].rearrange("p (j o) -> p j o", o=1).broadcast_to([P, J, H])
                    dve.tensor_tensor(logits[:, t, :, :], logits[:, t, :, :], spread, ALU.add)
                dve.drain()
                dve.tensor_reduce(stat[:, t, :], logits[:, t, :, :].rearrange("p j h -> p h j"), AX.X, ALU.max)
                dve.drain()
                over = stat[:, t:t + 1, :].broadcast_to([P, J, H])
                dve.tensor_tensor(logits[:, t, :, :], logits[:, t, :, :], over, ALU.subtract).then_inc(shifted.sem, 1)
            for t in range(NT):
                dve.wait_ge(exp_l.sem, exp_l.nth(t + 1))
                dve.tensor_reduce(stat[:, t, :], logits[:, t, :, :].rearrange("p j h -> p h j"), AX.X, ALU.add)
                dve.drain()
                dve.reciprocal(stat[:, t, :], stat[:, t, :])
                dve.drain()
                over = stat[:, t:t + 1, :].broadcast_to([P, J, H])
                dve.tensor_tensor(logits[:, t, :, :], logits[:, t, :, :], over, ALU.mult)


def peridynamic_gather(m, weights, value):
    nc = m.nc
    J, H, JB = 64, 16, 8
    NB = J // JB
    with ExitStack() as ctx:
        place = Place(nc, ctx, "gather")
        spread = place.sbuf("spread", [P, JB, P])
        W_cproj = place.sbuf("W_cproj", [P, D])
        now = place.sbuf("now", [P, TB, P])
        wT = place.sbuf("wT", [P, 2, T])
        prod = place.sbuf("prod", [P, 2, 2, T])
        oT = place.sbuf("oT", [P, B * T])
        ps_t = place.psum("ps_t", [P, T])
        ps_w = place.psum("ps_w", [P, 2, BANK])
        ps_o = place.psum("ps_o", [P, BANK])
        ps_y = place.psum("ps_y", [P, 2, BANK])
        NQ = JB // 2
        small_in = place.counter("small_in")
        staged = place.counter("staged")
        w_turned = place.counter("w_turned", ahead=1)
        wT_ready = place.counter("wT_ready")
        spread_ready = place.counter("spread_ready", per=NQ)
        prod_ready = place.counter("prod_ready", per=NQ, ahead=NQ)
        added = place.counter("added", per=NQ, ahead=NQ)
        sum_taken = place.counter("sum_taken", ahead=1)
        y_ready = place.counter("y_ready")
        block = ctx.enter_context(nc.Block())

        @block.sync
        def _(sp):
            sp.dma_start(spread[:, :, :], m.dram["L2_attn_spread"]).then_inc(small_in.sem, 16)
            sp.dma_start(W_cproj[:, :], m.dram["L2_attn_W_cproj"]).then_inc(small_in.sem, 16)

        @block.scalar
        def _(act):
            with act.Fori(0, B) as b:
                for jb in range(NB):
                    it = b * NB + jb
                    act.wait_ge(w_turned.sem, w_turned.nth(0, it))
                    at = weights[:, bass.ds(b * TB, TB), jb * JB:(jb + 1) * JB, :].rearrange("p t j h -> p t (j h)")
                    act.activation(now[:, :, :], at, ACT.Copy).then_inc(staged.sem, 1)
                    act.wait_ge(w_turned.sem, w_turned.nth(1, it))
                    act.activation(wT[:, jb % 2, :], ps_t[:, :], ACT.Copy).then_inc(wT_ready.sem, 1)

        @block.tensor
        def _(pe):
            pe.sem_inc(w_turned.sem, w_turned.ahead)
            pe.sem_inc(added.sem, added.ahead)
            pe.wait_ge(small_in.sem, small_in.nth(32))
            with pe.Fori(0, B) as b:
                pe.wait_ge(sum_taken.sem, sum_taken.nth(0, b))

                def turn(jb):
                    pe.wait_ge(staged.sem, staged.nth(jb + 1, b * NB))
                    for t in range(TB):
                        mm = pe.transpose(ps_t[:, t * P:(t + 1) * P], now[:, t, :], m.ident[:, :])
                    mm.then_inc(w_turned.sem, 1)

                def spread_out(jb, q):
                    it = b * NB + jb
                    if q == 0:
                        pe.wait_ge(wT_ready.sem, wT_ready.nth(1, it))
                    pe.wait_ge(prod_ready.sem, prod_ready.nth(q - 1, it))
                    for o in range(2):
                        mm = pe.matmul(ps_w[:, q % 2, o * T:(o + 1) * T], spread[:, 2 * q + o, :], wT[:, jb % 2, :], start=True,
                                       stop=True)
                    mm.then_inc(spread_ready.sem, 1)

                def add(jb, q):
                    pe.wait_ge(prod_ready.sem, prod_ready.nth(q + 1, b * NB + jb))
                    for o in range(2):
                        j = jb * JB + 2 * q + o
                        mm = pe.matmul(ps_o[:, 0:T], m.ident[:, :], prod[:, q % 2, o, :], start=(j == 0), stop=(j == J - 1),
                                       skip_group_check=True)
                    mm.then_inc(added.sem, 1)

                sets = [(jb, q) for jb in range(NB) for q in range(NQ)]
                turn(0)
                spread_out(0, 0)
                for n, (jb, q) in enumerate(sets):
                    if q == 0 and jb + 1 < NB:
                        turn(jb + 1)
                    if n + 1 < len(sets):
                        spread_out(*sets[n + 1])
                    add(jb, q)
            pe.wait_ge(sum_taken.sem, sum_taken.nth(B))
            for t in range(NT):
                mm = pe.matmul(ps_y[:, t // 4, (t % 4) * P:(t % 4 + 1) * P], oT[:, t * P:(t + 1) * P], W_cproj[:, :], start=True,
                               stop=True)
            mm.then_inc(y_ready.sem, 1)

        @block.vector
        def _(dve):
            dve.sem_inc(prod_ready.sem, prod_ready.ahead)
            dve.sem_inc(sum_taken.sem, sum_taken.ahead)
            with dve.Fori(0, B) as b:
                with dve.Fori(0, NB) as jb:
                    it = b * NB + jb
                    for q in range(NQ):
                        dve.wait_ge(spread_ready.sem, spread_ready.nth(q + 1, it))
                        dve.wait_ge(added.sem, added.nth(q - 1, it))
                        for o in range(2):
                            v = value[:, bass.ds(b, 1), bass.ds(jb * JB + 2 * q + o, T)].rearrange("p b t -> p (b t)")
                            ins = dve.tensor_tensor(prod[:, q % 2, o, :], ps_w[:, q % 2, o * T:(o + 1) * T], v, ALU.mult)
                        ins.then_inc(prod_ready.sem, 1)
                dve.wait_ge(added.sem, added.nth(NQ, b * NB + (NB - 1)))
                dve.tensor_copy(oT[:, bass.ds(b * T, T)], ps_o[:, 0:T]).then_inc(sum_taken.sem, 1)
            dve.wait_ge(y_ready.sem, y_ready.nth(1))
            dve.tensor_copy(m.Y[:, :, :], ps_y[:, :, :].rearrange("p h (t d) -> p (h t) d", d=D))


def top_k_cross(m):
    with ExitStack() as ctx:
        place = Place(m.nc, ctx, "topk")
        accT = place.sbuf("accT", [P, B * T])
        attention(m, Heads("L2_xattn", S, 1, P, D, scale=D ** -0.5, biased=True, context=True, n_heads=1, choose=32),
                  m.XT, accT)
        add_column(m, accT, m.dram["L2_xattn_bo"])
        to_rows(m, accT)


def local_transformer(m):
    nc = m.nc
    with ExitStack() as ctx:
        place = Place(nc, ctx, "local")
        Z = place.sbuf("Z", [P, B * T])
        shifted = place.sbuf("shifted", [P, B * T])
        copy_columns(m, m.XT, Z)
        with nc.Fori(0, 6) as layer:
            shift_tokens(m, Z, shifted)
            attention(m, Heads("L2_ffn", T, 2, 64, 64, scale=8.0, cosine=True, masked=True, rotary=True,
                               reach=[(0, P), (P - 32, T)]), shifted, Z,
                      layer=layer, add=True)
            gated_ffn(m, Z, shifted, layer)
        to_rows(m, Z)


def copy_columns(m, source, target):
    with ExitStack() as ctx:
        block = ctx.enter_context(m.nc.Block())

        @block.vector
        def _(dve):
            dve.tensor_copy(target[:, :], source[:, :])


def shift_tokens(m, Z, shifted):
    with ExitStack() as ctx:
        block = ctx.enter_context(m.nc.Block())
        lower, upper = slice(0, D // 2), slice(D // 2, D)

        @block.vector
        def _(dve):
            by_batch = shifted[upper, :].rearrange("p (b t) -> p b t", t=T)
            dve.tensor_copy(by_batch[:, :, 1:], Z[upper, :].rearrange("p (b t) -> p b t", t=T)[:, :, 0:T - 1])
            dve.memset(by_batch[:, :, 0:1], 0.0)

        @block.scalar
        def _(act):
            act.activation(shifted[lower, :], Z[lower, :], ACT.Copy)


def gated_ffn(m, Z, xs, layer):
    nc = m.nc
    FC = 3
    FP = FC * P
    N = 2 * FC
    BIAS = 2 * FP
    with ExitStack() as ctx:
        place = Place(nc, ctx, "gated")
        up = place.sbuf("up", [P, 2 * FP + 2 * FC + 3])
        down = place.sbuf("down", [P, FC, D])
        centred = place.sbuf("centred", [P, B * T])
        work = place.sbuf("work", [P, B * T])
        gate = place.sbuf("gate", [P, 2, BANK])
        h = place.sbuf("h", [P, 2, BANK])
        ps_m = place.psum("ps_m", [P, 2, BANK])
        ps_a = place.psum("ps_a", [P, 2, BANK])
        ps_g = place.psum("ps_g", [P, 2, BANK])
        ps_y = place.psum("ps_y", [P, 2, BANK])
        w_in = place.counter("w_in")
        xs_ready = place.counter("xs_ready")
        mean_ready = place.counter("mean_ready")
        squares_ready = place.counter("squares_ready")
        var_ready = place.counter("var_ready")
        var_taken = place.counter("var_taken")
        root_ready = place.counter("root_ready")
        xn_ready = place.counter("xn_ready")
        up_ready = place.counter("up_ready")
        gelu_ready = place.counter("gelu_ready")
        h_ready = place.counter("h_ready")
        down_done = place.counter("down_done")
        block = ctx.enter_context(nc.Block())
        halves = [slice(half * BANK, (half + 1) * BANK) for half in range(2)]

        @block.sync
        def _(sp):
            sp.dma_start(up[:, :], m.dram["L2_ffn_up"][bass.ds(layer, 1), :, :].rearrange("l p c -> (l p) c")).then_inc(w_in.sem, 16)
            sp.dma_start(down[:, :, :], m.dram["L2_ffn_down"][bass.ds(layer, 1), :, :, :].rearrange("l p c d -> (l p) c d"))\
              .then_inc(w_in.sem, 16)

        @block.vector
        def _(dve):
            by_batch = xs[D // 2:, :].rearrange("p (b t) -> p b t", t=T)
            dve.tensor_copy(by_batch[:, :, 1:], Z[D // 2:, :].rearrange("p (b t) -> p b t", t=T)[:, :, 0:T - 1])\
               .then_inc(xs_ready.sem, 1)
            for half in range(2):
                dve.wait_ge(mean_ready.sem, mean_ready.nth(half + 1))
                dve.scalar_tensor_tensor(out=centred[:, halves[half]], in0=ps_m[:, half, :], scalar=-1.0 / D, in1=xs[:, halves[half]],
                                         op0=ALU.mult, op1=ALU.add)
                dve.drain()
                dve.tensor_tensor(work[:, halves[half]], centred[:, halves[half]], centred[:, halves[half]], ALU.mult)\
                   .then_inc(squares_ready.sem, 1)
            for half in range(2):
                dve.wait_ge(var_ready.sem, var_ready.nth(half + 1))
                dve.tensor_scalar(work[:, halves[half]], ps_m[:, half, :], 1.0 / D, 1e-5, ALU.mult, ALU.add).then_inc(var_taken.sem, 1)
            dve.wait_ge(w_in.sem, w_in.nth(32))
            for half in range(2):
                dve.wait_ge(root_ready.sem, root_ready.nth(half + 1))
                dve.reciprocal(work[:, halves[half]], work[:, halves[half]])
                dve.drain()
                dve.tensor_tensor(centred[:, halves[half]], centred[:, halves[half]], work[:, halves[half]], ALU.mult)
                dve.drain()
                c = BIAS + 2 * FC
                dve.tensor_scalar(centred[:, halves[half]], centred[:, halves[half]], up[:, c:c + 1], up[:, c + 1:c + 2],
                                  ALU.mult, ALU.add).then_inc(xn_ready.sem, 1)
            for n in range(N):
                half, f = n // FC, n % FC
                dve.wait_ge(gelu_ready.sem, gelu_ready.nth(n + 1))
                if n >= 2:
                    dve.wait_ge(down_done.sem, down_done.nth(n - 1))
                dve.scalar_tensor_tensor(out=h[:, n % 2, :], in0=ps_a[:, n % 2, :], scalar=up[:, BIAS + f:BIAS + f + 1],
                                         in1=gate[:, n % 2, :], op0=ALU.add, op1=ALU.mult).then_inc(h_ready.sem, 1)
            for half in range(2):
                dve.wait_ge(down_done.sem, down_done.nth((half + 1) * FC))
                c = BIAS + 2 * FC + 2
                dve.scalar_tensor_tensor(out=Z[:, halves[half]], in0=ps_y[:, half, :], scalar=up[:, c:c + 1], in1=Z[:, halves[half]],
                                         op0=ALU.add, op1=ALU.add)

        @block.scalar
        def _(act):
            act.activation(xs[0:D // 2, :], Z[0:D // 2, :], ACT.Copy).then_inc(xs_ready.sem, 1)
            for half in range(2):
                act.wait_ge(var_taken.sem, var_taken.nth(half + 1))
                act.activation(work[:, halves[half]], work[:, halves[half]], ACT.Sqrt).then_inc(root_ready.sem, 1)
            act.wait_ge(w_in.sem, w_in.nth(32))
            for n in range(N):
                f = n % FC
                act.wait_ge(up_ready.sem, up_ready.nth(n + 1))
                if n >= 2:
                    act.wait_ge(h_ready.sem, h_ready.nth(n - 1))
                act.activation(gate[:, n % 2, :], ps_g[:, n % 2, :], ACT.Gelu, bias=up[:, BIAS + FC + f:BIAS + FC + f + 1])\
                   .then_inc(gelu_ready.sem, 1)

        @block.tensor
        def _(pe):
            pe.wait_ge(xs_ready.sem, xs_ready.nth(2))
            for half in range(2):
                pe.matmul(ps_m[:, half, :], m.ones[:, :], xs[:, halves[half]], start=True, stop=True).then_inc(mean_ready.sem, 1)
            for half in range(2):
                pe.wait_ge(squares_ready.sem, squares_ready.nth(half + 1))
                pe.matmul(ps_m[:, half, :], m.ones[:, :], work[:, halves[half]], start=True, stop=True).then_inc(var_ready.sem, 1)
            pe.wait_ge(w_in.sem, w_in.nth(32))

            def rise(n):
                half, f = n // FC, n % FC
                pe.wait_ge(xn_ready.sem, xn_ready.nth(half + 1))
                if n >= 2:
                    pe.wait_ge(h_ready.sem, h_ready.nth(n - 1))
                pe.matmul(ps_a[:, n % 2, :], up[:, f * P:(f + 1) * P], centred[:, halves[half]], start=True, stop=True)
                pe.matmul(ps_g[:, n % 2, :], up[:, FP + f * P:FP + (f + 1) * P], centred[:, halves[half]], start=True, stop=True)\
                  .then_inc(up_ready.sem, 1)

            rise(0)
            for n in range(N):
                if n + 1 < N:
                    rise(n + 1)
                half, f = n // FC, n % FC
                pe.wait_ge(h_ready.sem, h_ready.nth(n + 1))
                pe.matmul(ps_y[:, half, :], down[:, f, :], h[:, n % 2, :], start=(f == 0), stop=(f == FC - 1))\
                  .then_inc(down_done.sem, 1)


def linear_recurrence(m):
    nc = m.nc
    HALVES = B * T // BANK
    with ExitStack() as ctx:
        place = Place(nc, ctx, "recur")
        names = ["Wk", "Wv", "Ww", "Wr", "Wo"]
        w = place.sbuf("w", [P, len(names), D])
        same_head = place.sbuf("same_head", [P, P])
        kT = place.sbuf("kT", [P, B * T])
        vT = place.sbuf("vT", [P, B * T])
        dT = place.sbuf("dT", [P, B * T])
        rT = place.sbuf("rT", [P, B * T])
        oT = place.sbuf("oT", [P, B * T])
        o2T = place.sbuf("o2T", [P, B * T])
        ms = place.sbuf("ms", [P, NT])
        ps = place.psum("ps", [P, 2, BANK])
        ps_k = place.psum("ps_k", [P, 2, BANK])
        ps_y = place.psum("ps_y", [P, 2, BANK])
        ps_s = place.psum("ps_s", [P, BANK])
        w_in = place.counter("w_in")
        product_ready = place.counter("product_ready")
        product_taken = place.counter("product_taken")
        k_sum_ready = place.counter("k_sum_ready")
        o_ready = place.counter("o_ready")
        y_ready = place.counter("y_ready")
        mean_ready = place.counter("mean_ready")
        root_ready = place.counter("root_ready")
        block = ctx.enter_context(nc.Block())

        @block.sync
        def _(sp):
            for i, name in enumerate(names):
                sp.dma_start(w[:, i, :], m.dram["L3_attn_" + name]).then_inc(w_in.sem, 16)
            sp.dma_start(same_head[:, :], m.dram["c_same_head8"]).then_inc(w_in.sem, 16)

        @block.tensor
        def _(pe):
            pe.wait_ge(w_in.sem, w_in.nth(16 * (len(names) + 1)))
            for n in range(4 * HALVES):
                i, half = n // HALVES, n % HALVES
                cols = slice(half * BANK, (half + 1) * BANK)
                if n >= 2:
                    pe.wait_ge(product_taken.sem, product_taken.nth(n - 1))
                pe.matmul(ps[:, n % 2, :], w[:, i, :], m.XT[:, cols], start=True, stop=True)\
                  .then_inc(product_ready.sem, 1)
            for half in range(HALVES):
                cols = slice(half * BANK, (half + 1) * BANK)
                pe.wait_ge(product_taken.sem, product_taken.nth(HALVES))
                pe.matmul(ps_k[:, half, :], same_head[:, :], kT[:, cols], start=True, stop=True)\
                  .then_inc(k_sum_ready.sem, 1)
            pe.wait_ge(o_ready.sem, o_ready.nth(1))
            for t in range(NT):
                tok = slice(t * P, (t + 1) * P)
                pe.matmul(ps_y[:, t // 4, (t % 4) * P:(t % 4 + 1) * P], oT[:, tok], w[:, 4, :], start=True, stop=True)
                mm = pe.matmul(ps_s[:, t:t + 1], o2T[:, tok], m.ones[:, 0:1], start=True, stop=True)
            mm.then_inc(y_ready.sem, 1)

        @block.scalar
        def _(act):
            for n in range(4 * HALVES):
                i, half = n // HALVES, n % HALVES
                cols = slice(half * BANK, (half + 1) * BANK)
                act.wait_ge(product_ready.sem, product_ready.nth(n + 1))
                act.activation([kT, vT, dT, rT][i][:, cols], ps[:, n % 2, :], ACT.Sigmoid if i >= 2 else ACT.Copy)\
                   .then_inc(product_taken.sem, 1)
            act.wait_ge(mean_ready.sem, mean_ready.nth(1))
            act.activation(ms[:, :], ms[:, :], ACT.Sqrt).then_inc(root_ready.sem, 1)

        @block.vector
        def _(dve):
            dve.wait_ge(product_taken.sem, product_taken.nth(4 * HALVES))
            dve.tensor_scalar(dT[:, :], dT[:, :], 0.99, None, ALU.mult)
            for half in range(HALVES):
                cols = slice(half * BANK, (half + 1) * BANK)
                dve.wait_ge(k_sum_ready.sem, k_sum_ready.nth(half + 1))
                dve.tensor_tensor(vT[:, cols], ps_k[:, half, :], vT[:, cols], ALU.mult)
            dve.drain()
            for b in range(B):
                tok = slice(b * T, (b + 1) * T)
                dve.tensor_tensor_scan(oT[:, tok], dT[:, tok], vT[:, tok], 0.0, ALU.mult, ALU.add)
            dve.drain()
            dve.tensor_tensor(oT[:, :], oT[:, :], rT[:, :], ALU.mult)
            dve.drain()
            dve.tensor_tensor(o2T[:, :], oT[:, :], oT[:, :], ALU.mult).then_inc(o_ready.sem, 1)
            dve.wait_ge(y_ready.sem, y_ready.nth(1))
            eps = float(np.finfo(np.float32).eps)
            dve.tensor_scalar(ms[:, :], ps_s[:, 0:NT], 1.0 / D, eps, ALU.mult, ALU.add).then_inc(mean_ready.sem, 1)
            dve.wait_ge(root_ready.sem, root_ready.nth(1))
            dve.reciprocal(ms[:, :], ms[:, :])
            dve.drain()
            for t in range(NT):
                dve.tensor_scalar(m.Y[:, t, :], ps_y[:, t // 4, (t % 4) * P:(t % 4 + 1) * P], ms[:, t:t + 1], None,
                                  ALU.mult)


def double_mha(m):
    with ExitStack() as ctx:
        place = Place(m.nc, ctx, "double")
        hT = place.sbuf("hT", [P, B * T])
        accT = place.sbuf("accT", [P, B * T])
        attention(m, Heads("L3_xattn1", T, 4, 32, 8, scale=8 ** -0.5, biased=True, masked=True, reach=[(0, P), (0, T)]), m.XT, hT)
        add_column(m, hT, m.dram["L3_xattn_bo1"])
        attention(m, Heads("L3_xattn2", S, 4, 32, 8, scale=8 ** -0.5, biased=True, context=True), hT, accT)
        add_column(m, accT, m.dram["L3_xattn_bo2"])
        to_rows(m, accT)


def ternary_ffn(m):
    nc = m.nc
    F = 512
    FC = F // P
    with ExitStack() as ctx:
        place = Place(nc, ctx, "ternary")
        w = place.sbuf("w", [P, 2, FC * P])
        wq = place.sbuf("wq", [P, 2, FC * P])
        small = place.sbuf("small", [P, FC * P])
        sums = place.sbuf("sums", [P, 2])
        level = place.sbuf("level", [P, 2, 2])
        sq = place.sbuf("sq", [P, NT, D])
        rms = place.sbuf("rms", [P, NT])
        xnT = place.sbuf("xnT", [P, B * T])
        hT = place.sbuf("hT", [P, FC, B * T])
        hsq = place.sbuf("hsq", [P, FC, B * T])
        rms_h = place.sbuf("rms_h", [P, NT])
        ps_level = place.psum("ps_level", [P, BANK])
        ps_x = place.psum("ps_x", [P, 2, BANK])
        ps_h = place.psum("ps_h", [P, 2, BANK])
        ps_y = place.psum("ps_y", [P, 2, BANK])
        ps_s = place.psum("ps_s", [P, BANK])
        w_in = place.counter("w_in")
        sums_ready = place.counter("sums_ready")
        level_ready = place.counter("level_ready")
        w_ready = place.counter("w_ready")
        square_ready = place.counter("square_ready")
        root_ready = place.counter("root_ready")
        xn_ready = place.counter("xn_ready")
        xn_turned = place.counter("xn_turned")
        xnT_ready = place.counter("xnT_ready")
        h_ready = place.counter("h_ready")
        gelu_ready = place.counter("gelu_ready")
        hsq_ready = place.counter("hsq_ready")
        y_ready = place.counter("y_ready")
        s_ready = place.counter("s_ready")
        mean_ready = place.counter("mean_ready")
        root_h_ready = place.counter("root_h_ready")
        block = ctx.enter_context(nc.Block())

        @block.sync
        def _(sp):
            sp.dma_start(w[:, 0, :], m.dram["L3_ffn_w_up"]).then_inc(w_in.sem, 16)
            sp.dma_start(w[:, 1, :].rearrange("p (c d) -> p c d", c=FC), m.dram["L3_ffn_w_down"].rearrange("(c p) d -> p c d", p=P))\
              .then_inc(w_in.sem, 16)

        @block.vector
        def _(dve):
            dve.tensor_tensor(sq[:, :, :], m.X[:, :, :], m.X[:, :, :], ALU.mult)
            dve.drain()
            dve.tensor_reduce(rms[:, :], sq[:, :, :], AX.X, ALU.add).then_inc(square_ready.sem, 1)
            dve.wait_ge(w_in.sem, w_in.nth(32))
            for i in range(2):
                dve.tensor_reduce(sums[:, i:i + 1], w[:, i, :], AX.X, ALU.add, apply_absolute_value=True)\
                   .then_inc(sums_ready.sem, 1)
            dve.wait_ge(level_ready.sem, level_ready.nth(1))
            dve.tensor_scalar(level[:, 0, :], ps_level[:, 0:2], 0.5 / (F * D), None, ALU.mult)
            dve.tensor_scalar(level[:, 1, :], ps_level[:, 0:2], -0.5 / (F * D), None, ALU.mult)
            dve.drain()
            for i in range(2):
                dve.tensor_scalar(wq[:, i, :], w[:, i, :], level[:, 0, i:i + 1], None, ALU.is_gt)
                dve.tensor_scalar(small[:, :], w[:, i, :], level[:, 1, i:i + 1], None, ALU.is_lt)
                dve.drain()
                dve.tensor_tensor(wq[:, i, :], wq[:, i, :], small[:, :], ALU.subtract)
                dve.drain()
                dve.tensor_tensor(wq[:, i, :], wq[:, i, :], w[:, i, :], ALU.subtract)
                dve.drain()
                dve.tensor_tensor(wq[:, i, :], wq[:, i, :], w[:, i, :], ALU.add).then_inc(w_ready.sem, 1)
            dve.wait_ge(root_ready.sem, root_ready.nth(1))
            dve.tensor_scalar(rms[:, :], rms[:, :], 1e-8, None, ALU.add)
            dve.drain()
            dve.reciprocal(rms[:, :], rms[:, :])
            dve.drain()
            for t in range(NT):
                dve.tensor_scalar(sq[:, t, :], m.X[:, t, :], rms[:, t:t + 1], None, ALU.mult).then_inc(xn_ready.sem, 1)
            for half in range(2):
                dve.wait_ge(xn_turned.sem, xn_turned.nth(half + 1))
                dve.tensor_copy(xnT[:, half * BANK:(half + 1) * BANK], ps_x[:, half, :]).then_inc(xnT_ready.sem, 1)
            for n in range(2 * FC):
                half, f = n // FC, n % FC
                cols = slice(half * BANK, (half + 1) * BANK)
                dve.wait_ge(gelu_ready.sem, gelu_ready.nth(n + 1))
                dve.tensor_tensor(hsq[:, f, cols], hT[:, f, cols], hT[:, f, cols], ALU.mult).then_inc(hsq_ready.sem, 1)
            dve.wait_ge(s_ready.sem, s_ready.nth(1))
            dve.tensor_scalar(rms_h[:, :], ps_s[:, 0:NT], 1.0 / F, None, ALU.mult).then_inc(mean_ready.sem, 1)
            dve.wait_ge(root_h_ready.sem, root_h_ready.nth(1))
            dve.tensor_scalar(rms_h[:, :], rms_h[:, :], 1e-8, None, ALU.add)
            dve.drain()
            dve.reciprocal(rms_h[:, :], rms_h[:, :])
            dve.drain()
            for t in range(NT):
                dve.tensor_scalar(m.Y[:, t, :], ps_y[:, t // 4, (t % 4) * P:(t % 4 + 1) * P], rms_h[:, t:t + 1], None,
                                  ALU.mult)

        @block.scalar
        def _(act):
            act.wait_ge(square_ready.sem, square_ready.nth(1))
            act.activation(rms[:, :], rms[:, :], ACT.Sqrt, scale=1.0 / D).then_inc(root_ready.sem, 1)
            for n in range(2 * FC):
                half, f = n // FC, n % FC
                act.wait_ge(h_ready.sem, h_ready.nth(n + 1))
                act.activation(hT[:, f, half * BANK:(half + 1) * BANK], ps_h[:, n % 2, :], ACT.Gelu).then_inc(gelu_ready.sem, 1)
            act.wait_ge(mean_ready.sem, mean_ready.nth(1))
            act.activation(rms_h[:, :], rms_h[:, :], ACT.Sqrt).then_inc(root_h_ready.sem, 1)

        @block.tensor
        def _(pe):
            pe.wait_ge(sums_ready.sem, sums_ready.nth(2))
            pe.matmul(ps_level[:, 0:2], m.ones[:, :], sums[:, :], start=True, stop=True).then_inc(level_ready.sem, 1)
            for t in range(NT):
                pe.wait_ge(xn_ready.sem, xn_ready.nth(t + 1))
                mm = pe.transpose(ps_x[:, t // 4, (t % 4) * P:(t % 4 + 1) * P], sq[:, t, :], m.ident[:, :])
                if t % 4 == 3:
                    mm.then_inc(xn_turned.sem, 1)
            pe.wait_ge(w_ready.sem, w_ready.nth(2))
            for n in range(2 * FC):
                half, f = n // FC, n % FC
                pe.wait_ge(xnT_ready.sem, xnT_ready.nth(half + 1))
                if n >= 2:
                    pe.wait_ge(gelu_ready.sem, gelu_ready.nth(n - 1))
                pe.matmul(ps_h[:, n % 2, :], wq[:, 0, f * P:(f + 1) * P], xnT[:, half * BANK:(half + 1) * BANK],
                          start=True, stop=True).then_inc(h_ready.sem, 1)
            pe.wait_ge(hsq_ready.sem, hsq_ready.nth(2 * FC))
            for t in range(NT):
                tok = slice(t * P, (t + 1) * P)
                for f in range(FC):
                    pe.matmul(ps_y[:, t // 4, (t % 4) * P:(t % 4 + 1) * P], hT[:, f, tok], wq[:, 1, f * P:(f + 1) * P],
                              start=(f == 0), stop=(f == FC - 1))
                for f in range(FC):
                    mm = pe.matmul(ps_s[:, t:t + 1], hsq[:, f, tok], m.ones[:, 0:1], start=(f == 0), stop=(f == FC - 1))
            mm.then_inc(s_ready.sem, 1)


def transposed(a):
    return np.swapaxes(a, -1, -2)


def by_chunk(a):
    return transposed(a.reshape(*a.shape[:-1], -1, P))


LAYOUTS = {
    "L0_ffn_Wg": transposed, "L0_ffn_W1": transposed, "L0_ffn_W2": transposed, "L0_ffn_b1": by_chunk,
    "L1_ffn_b1": by_chunk,
    "L3_ffn_w_up": transposed, "L3_ffn_w_down": transposed,
    "L3_attn_Wr": transposed, "L3_attn_Wk": transposed, "L3_attn_Wv": transposed,
    "L3_attn_Ww": transposed, "L3_attn_Wo": transposed,
}


CLOSED = np.float32(-MASKED)


def pad_heads(a, axis, to):
    pad = [(0, 0)] * a.ndim
    pad[axis] = (0, to - a.shape[axis])
    return np.pad(a, pad)


def attention_layout(wq, wk, wv, wo, heads, bq=None, bk=None, bv=None, q_scale=None, k_scale=None):
    n, d, dh = wq.shape
    groups, stride = n // heads, P // heads
    zero = np.zeros((n, dh), np.float32)

    def side(a):
        a = pad_heads(a, 2, stride)
        return a.reshape(groups, heads, D, stride).transpose(0, 2, 1, 3).reshape(groups, D, P)

    def column(a):
        return pad_heads(a, 1, stride).reshape(groups, P, 1)

    values = wv.reshape(groups, heads, D, dh).transpose(0, 2, 1, 3).reshape(groups, D, heads * dh)
    columns = [column(zero if a is None else np.broadcast_to(a.reshape(-1, dh), (n, dh))) for a in (bq, bk, q_scale, k_scale)]
    both = np.concatenate([side(wq), side(wk), values] + columns, axis=2)
    wo = pad_heads(wo.reshape(groups, heads, dh, D), 2, stride).reshape(groups, P, D)
    out = {"w": np.concatenate([both, both[0:1]]), "wo": np.concatenate([wo, wo[0:1]])}
    if bv is not None:
        out["bv"] = np.concatenate([bv.reshape(groups, -1), bv.reshape(groups, -1)[0:1]])
    return out


def per_head(w):
    return w.reshape(D, 16, -1).transpose(1, 0, 2)


def attention_inputs(x):
    made = {}

    def put(name, **arrays):
        made.update({f"{name}_{k}": v for k, v in arrays.items()})

    w = x["L1_attn_w_qkv"]
    bias = x["L1_attn_b_qkv"].reshape(3, 16, 8)
    put("L1_attn", **attention_layout(per_head(w[:, 0:D]), per_head(w[:, D:2 * D]), per_head(w[:, 2 * D:]),
                                      x["L1_attn_w_out"], 4, bias[0], bias[1], bias[2]))
    i, j = np.arange(T)[:, None], np.arange(T)[None, :]
    open_ = (j % 32 == 0) | (np.abs(i - j) <= 64)
    put("L1_attn", mask=by_tile(np.where(open_, np.float32(0), CLOSED)))
    put("L3_xattn1", mask=by_tile(np.where(j <= i, np.float32(0), CLOSED)))
    for n in "12":
        v = [x[f"L3_xattn_{k}{n}"] for k in ("Wq", "Wk", "Wv", "Wo", "bq", "bk", "bv")]
        put("L3_xattn" + n, **attention_layout(v[0], v[1], v[2], v[3], 4, v[4], v[5], v[6]))
    kv = x["L1_xattn_Wkv"]
    put("L1_xattn", **attention_layout(per_head(x["L1_xattn_Wq"]), per_head(kv[:, 0:1024]), per_head(kv[:, 1024:]),
                                       x["L1_xattn_Wout"], 2, q_scale=x["L1_xattn_q_scale"], k_scale=x["L1_xattn_k_scale"]))
    null = x["L1_xattn_null_kv"]
    put("L1_xattn", null_k=np.tile(null[0], 2).reshape(P, 1), null_v=np.tile(null[1], 2).reshape(1, P))
    v = [x[f"L2_xattn_{k}"] for k in ("Wq", "Wk", "Wv", "Wo", "bq", "bk", "bv")]
    put("L2_xattn", **attention_layout(v[0].T[None], v[1].T[None], v[2].T[None], v[3].T[None], 1, v[4], v[5], v[6]))
    one = np.eye(D, dtype=np.float32)
    diagonal = np.zeros((D, D), np.float32)
    diagonal[np.arange(D), np.arange(D)] = x["L0_xattn_w_cq"]
    put("L0_xattn", **attention_layout(diagonal[None], one[None], one[None], one[None], 1, x["L0_xattn_w_q"],
                                       None, np.zeros((1, D), np.float32)))
    made["L0_xattn_b"] = np.concatenate([x[f"L0_xattn_b_{k}"].reshape(1, 1) for k in ("cq", "c", "q")], axis=1)
    made["L0_xattn_W_l"] = x["L0_xattn_W_l"].T.reshape(4, D, D).transpose(1, 0, 2)
    made["L2_ffn_mask"] = by_tile(np.where((j <= i) & (i - j <= 32), np.float32(0), CLOSED))
    layers = []
    for n in range(6):
        kqv = x["L2_ffn_Wqkv"][n]
        layers.append(attention_layout(per_head(kqv[:, 0:1024]), per_head(kqv[:, 1024:2048]), per_head(kqv[:, 2048:]),
                                       x["L2_ffn_Wo"][n], 2, q_scale=x["L2_ffn_q_scale"][n], k_scale=x["L2_ffn_k_scale"][n]))
    put("L2_ffn", **{k: np.concatenate([a[k] for a in layers]) for k in ("w", "wo")})
    F, FP = 341, 384

    def pad(a, axis):
        width = [(0, 0)] * a.ndim
        width[axis] = (0, FP - F)
        return np.pad(a, width)

    w1, b1 = x["L2_ffn_W1"], x["L2_ffn_b1"]
    sides = [pad(w1[..., :F], 2), pad(w1[..., F:], 2)]
    columns = [by_chunk(pad(b1[:, :F], 1)), by_chunk(pad(b1[:, F:], 1))] + [x[f"L2_ffn_{k}"][:, :, None] for k in ("ln_g", "ln_b", "b2")]
    made["L2_ffn_up"] = np.concatenate(sides + columns, axis=2)
    made["L2_ffn_down"] = pad(x["L2_ffn_W2"], 1).reshape(6, 3, P, D).transpose(0, 2, 1, 3)
    made["L0_attn_proj"] = np.stack([x["L0_attn_Wq"].T, x["L0_attn_Wk"].T, x["L0_attn_Wv"].T,
                                     np.repeat(x["L0_attn_Wb"], 32, axis=0).T], axis=1)
    made["L0_attn_taps"] = np.concatenate([x[f"L0_attn_conv_{k}"] for k in "qkv"] +
                                          [x[f"L0_attn_fir_{k}"].reshape(D, -1) for k in "sml"], axis=1)
    made["L0_attn_gate"] = x["L0_attn_gate_w"].reshape(20, D).T
    made["L0_attn_WoT"] = x["L0_attn_Wo"].T
    made["L0_attn_row"] = np.concatenate([x[f"L0_attn_{k}"].reshape(1, -1) for k in ("gate_b", "log_temp", "eps_param", "norm_w")],
                                         axis=1)
    def blocks(w, n):
        r, c = w.shape
        out = np.zeros((n, r, n, c), np.float32)
        out[np.arange(n), :, np.arange(n), :] = w
        return out.reshape(n * r, n * c)

    made["L2_attn_blocks"] = np.stack([blocks(x["L2_attn_W_strain"], 8), blocks(x["L2_attn_W_dmg"], 8)], axis=1)
    out16 = np.zeros((P, 2, 16, 16, 8), np.float32)
    for o in range(16):
        out16[:, 0, o, o], out16[:, 1, o, o] = blocks(x["L2_attn_W_bond"], 8), blocks(x["L2_attn_W_dmg_out"], 8)
    made["L2_attn_out16"] = out16.reshape(P, 2, 16, P)
    made["L2_attn_pos8"] = np.tile(x["L2_attn_W_pos"], (1, 8))
    made["L2_attn_rel_T"] = x["L2_attn_rel_pos_emb"].T
    made["L2_attn_b_dmg8"] = np.tile(x["L2_attn_b_dmg"], 8).reshape(P, 1)
    t, j = np.arange(P)[:, None], np.arange(64)[None, :]
    made["L2_attn_mask"] = np.where(t - 63 + j >= 0, np.float32(0), np.float32(MASKED))
    jj, p, q = np.arange(8)[None, :, None], np.arange(P)[:, None, None], np.arange(P)[None, None, :]
    made["L2_attn_spread"] = ((p // 16 == jj) & (p % 16 == q // 8)).astype(np.float32)
    return made


def by_tile(mask):
    return mask.reshape(TB, P, -1).transpose(1, 0, 2)


def constants():
    i = np.arange(P)
    half = np.arange(0, 64, 2, dtype=np.float32)
    inv_freq = (1.0 / 10000.0 ** (half / 64)).astype(np.float32)
    freqs = np.arange(T, dtype=np.float32)[:, None] * inv_freq[None, :]
    base = ((half + 0.4 * 64) / (1.4 * 64)).astype(np.float64)
    scale = base[None, :] ** ((np.arange(T) - T // 2) / 16)[:, None]
    freqs, scale = np.tile(freqs, (1, 4)).T, np.tile(scale, (1, 4)).T
    cos, sin = np.cos(freqs.astype(np.float64)), np.sin(freqs.astype(np.float64))
    rotation = np.zeros((P, P), np.float32)
    for h in range(2):
        k = np.arange(32)
        rotation[64 * h + 32 + k, 64 * h + k] = -1.0
        rotation[64 * h + k, 64 * h + 32 + k] = 1.0
    below = []
    r, c = i[:, None], i[None, :]
    for s in (1, 2, 4, 8, 16):
        low = (r // (2 * s) == c // (2 * s)) & (r // s % 2 == 1) & (c // s % 2 == 0)
        below += [-low.astype(np.float32), -low.T.astype(np.float32)]
    return {
        "c_below": np.stack(below, axis=1),
        "c_causal32": ((r // 32 == c // 32) & (r <= c)).astype(np.float32),
        "c_same_head32": (r // 32 == c // 32).astype(np.float32),
        "c_cos": np.concatenate([cos / scale, cos * scale], axis=1).astype(np.float32),
        "c_sin": np.concatenate([sin / scale, sin * scale], axis=1).astype(np.float32),
        "c_rotation": rotation,
        "c_ident": np.eye(P, dtype=np.float32),
        "c_same_head8": (i[:, None] // 8 == i[None, :] // 8).astype(np.float32),
        "c_same_head64": (i[:, None] // 64 == i[None, :] // 64).astype(np.float32),
        "c_number": np.broadcast_to(i, (P, P)).astype(np.float32),
    }


SUBLAYERS = [gated_delta, bidaf, moe_0, sparse_attention, cosine_cross, moe_1, peridynamic, top_k_cross,
             local_transformer, linear_recurrence, double_mha, ternary_ffn]


def program(nc, dram):
    with ExitStack() as ctx:
        m = Model(nc, ctx, dram)
        load_model(m)
        for i, sublayer in enumerate(SUBLAYERS):
            sublayer(m)
            post_norm(m, last=(i == len(SUBLAYERS) - 1))


def kernel(**inputs):
    import concourse.bacc as bacc
    from concourse.bass_utils import run_bass_kernel_spmd

    nc = bacc.Bacc("TRN2", target_bir_lowering=False, num_devices=1)
    laid_out = {name: np.asarray(a) for name, a in inputs.items()}
    for name, layout in LAYOUTS.items():
        laid_out[name] = layout(laid_out[name])
    laid_out.update(attention_inputs(laid_out))
    laid_out["ctx_T"] = transposed(laid_out["ctx_1024"])
    laid_out.update(constants())
    arrays, dram = {}, {}
    for name, a in laid_out.items():
        a = np.ascontiguousarray(a)
        arrays[f"in_{name}"] = a
        dram[name] = nc.dram_tensor(f"in_{name}", a.shape, mybir.dt.from_np(a.dtype), kind="ExternalInput").ap()
    dram["out"] = nc.dram_tensor("out", (B, T, D), F32, kind="ExternalOutput").ap()
    program(nc, dram)
    r = run_bass_kernel_spmd(nc, [arrays], core_ids=[0])
    return r.results[0]["out"]
```
